# Optimizing a Trainium2 kernel written in Bass

```python
import numpy as np
import jax
import jax.numpy as jnp

def _softmax(x, axis=-1):
    return jax.nn.softmax(x, axis=axis)

def _gelu(x):
    return jax.nn.gelu(x, approximate=True)

def _silu(x):
    return jax.nn.silu(x)

def _sigmoid(x):
    return jax.nn.sigmoid(x)

def _layernorm(x, axis=-1, eps=1e-05):
    m = jnp.mean(x, axis=axis, keepdims=True)
    v = jnp.var(x, axis=axis, keepdims=True)
    return (x - m) / jnp.sqrt(v + eps)

def _scatter_add(tgt, idx, src, axis=0):
    return tgt.at[idx].add(src)

def _segment_sum(src, seg, n):
    return jax.ops.segment_sum(src, seg, n)
kernel_name = 'mk_gnn_resnorm_d4_gnn_r32_fbb587'

def setup_inputs(seed: int=0):
    np.random.seed(seed)
    _w = jnp.asarray

    def _rec_inputs():
        import jax
        import jax.numpy as jnp
        _gk = jax.random.key(seed)
        x = -0.0003713 + 1 * jax.random.normal(jax.random.fold_in(_gk, 1), (3125, 256), jnp.float32)
        _s = jax.random.randint(jax.random.fold_in(_gk, 2), (25000,), 0, 3125, jnp.int32)
        _d = jax.random.randint(jax.random.fold_in(_gk, 3), (25000,), 0, 3125, jnp.int32)
        _loop = jnp.arange(3125, dtype=jnp.int32)
        src = jnp.concatenate([_s, _d, _loop])
        dst = jnp.concatenate([_d, _s, _loop])
        _o = jnp.argsort(dst, stable=True)
        src = src[_o]
        dst = dst[_o]
        edge_attr_64 = -9.77346e-05 + 0.999888 * jax.random.normal(jax.random.fold_in(_gk, 12), (53125, 64), jnp.float32)
        edge_weight = jax.random.uniform(jax.random.fold_in(_gk, 14), (53125,), jnp.float32, 0.0, 1)
        edge_weight1 = jax.random.uniform(jax.random.fold_in(_gk, 15), (53125, 1), jnp.float32, 0.0, 0.999994)
        return (x, src, dst, edge_attr_64, edge_weight, edge_weight1)
    x, src, dst, edge_attr_64, edge_weight, edge_weight1 = _rec_inputs()

    def _L0_gnn_setup():
        import jax, jax.numpy as jnp
        import numpy as np
        N, E, D, H, FE = (50000, 25000, 256, 8, 64)
        HD = D // H
        key = jax.random.key(seed)
        ks = jax.random.split(key, 14)
        sD = 1.0 / np.sqrt(D)
        sF = 1.0 / np.sqrt(FE)
        return {'h': jax.random.normal(ks[0], (N, D), jnp.float32), 'efeat': jax.random.normal(ks[1], (E, FE), jnp.float32), 'src': jax.random.randint(ks[2], (E,), 0, N), 'dst': jax.random.randint(ks[3], (E,), 0, N), 'Wq': jax.random.normal(ks[4], (D, D), jnp.float32) * sD, 'Wk': jax.random.normal(ks[5], (D, D), jnp.float32) * sD, 'Wv': jax.random.normal(ks[6], (D, D), jnp.float32) * sD, 'W1': jax.random.normal(ks[7], (FE, D), jnp.float32) * sF, 'b1': jnp.zeros((D,), jnp.float32), 'W2': jax.random.normal(ks[8], (D, H), jnp.float32) * sD, 'b2': jnp.zeros((H,), jnp.float32), 'Wo': jax.random.normal(ks[9], (D, D), jnp.float32) * sD, 'bo': jnp.zeros((D,), jnp.float32)}
    _L0_gnn_all = _L0_gnn_setup()
    _L0_gnn_in = {k: v for k, v in _L0_gnn_all.items() if k in ('Wq', 'Wk', 'Wv', 'W1', 'b1', 'W2', 'b2', 'Wo', 'bo')}
    del _L0_gnn_all

    def _L1_gnn_setup():
        import jax, jax.numpy as jnp
        import numpy as np
        N_NODES = 3125
        K_HOPS = 2
        ALPHA = 0.5

        def _gcn_norm(edge_index, edge_weight, num_nodes):
            loops = jnp.arange(num_nodes, dtype=edge_index.dtype)
            src = jnp.concatenate([edge_index[0], loops])
            dst = jnp.concatenate([edge_index[1], loops])
            w = jnp.concatenate([edge_weight, jnp.ones((num_nodes,), edge_weight.dtype)])
            deg = jax.ops.segment_sum(w, dst, num_segments=num_nodes)
            dinv = jnp.where(deg > 0, jax.lax.rsqrt(jnp.maximum(deg, 1e-12)), 0.0)
            norm = dinv[src] * w * dinv[dst]
            return (src, dst, norm)
        key = jax.random.key(seed)
        k1, k2, k3, k4, k5 = jax.random.split(key, 5)
        N, E, D_IN, D_OUT = (N_NODES, 100000, 256, 256)
        x = jax.random.normal(k1, (N, D_IN), dtype=jnp.float32)
        edge_index = jax.random.randint(k2, (2, E), 0, N, dtype=jnp.int64)
        edge_weight = jax.random.uniform(k3, (E,), dtype=jnp.float32)
        W = jax.random.normal(k4, (D_OUT, D_IN), dtype=jnp.float32) / np.sqrt(D_IN)
        b = jax.random.normal(k5, (D_OUT,), dtype=jnp.float32) * 0.01
        return {'x': x, 'edge_index': edge_index, 'edge_weight': edge_weight, 'W': W, 'b': b}
    _L1_gnn_all = _L1_gnn_setup()
    _L1_gnn_in = {k: v for k, v in _L1_gnn_all.items() if k in ('W', 'b')}
    del _L1_gnn_all

    def _L2_gnn_setup():
        import jax, jax.numpy as jnp
        import numpy as np
        N_NODES = 10000
        N_EDGES = 10000
        D_IN = 256
        D_OUT = 256
        key = jax.random.key(seed)
        k1, k2, k3, k4, k5, k6 = jax.random.split(key, 6)
        feat = jax.random.normal(k1, (N_NODES, D_IN), dtype=jnp.float32)
        eweight = jax.random.uniform(k2, (N_EDGES, 1), dtype=jnp.float32)
        W = jax.random.normal(k3, (D_OUT, 2 * D_IN), dtype=jnp.float32) / np.sqrt(2 * D_IN)
        b = jax.random.normal(k4, (D_OUT,), dtype=jnp.float32) * 0.01
        src = jax.random.randint(k5, (N_EDGES,), 0, N_NODES, dtype=jnp.int64)
        dst = jax.random.randint(k6, (N_EDGES,), 0, N_NODES, dtype=jnp.int64)
        return {'feat': feat, 'eweight': eweight, 'W': W, 'b': b, 'src': src, 'dst': dst}
    _L2_gnn_all = _L2_gnn_setup()
    _L2_gnn_in = {k: v for k, v in _L2_gnn_all.items() if k in ('W', 'b')}
    del _L2_gnn_all

    def _L3_gnn_setup():
        import jax, jax.numpy as jnp
        import numpy as np
        N = 50000
        E = 25000
        DIN = 256
        DOUT = 256
        K_HOPS = 3
        LAMBDA = 0.0
        key = jax.random.key(seed)
        k1, k2, k3, k4 = jax.random.split(key, 4)
        feature = jax.random.normal(k1, (N, DIN), dtype=jnp.float32)
        limit = float(np.sqrt(6.0 / (DIN + DOUT)))
        W = jax.random.uniform(k2, (DIN, DOUT), dtype=jnp.float32, minval=-limit, maxval=limit)
        b = jnp.zeros((DOUT,), dtype=jnp.float32)
        src = jax.random.randint(k3, (E,), 0, N, dtype=jnp.int32)
        dst = jax.random.randint(k4, (E,), 0, N, dtype=jnp.int32)
        return {'feature': feature, 'W': W, 'b': b, 'src': src, 'dst': dst}
    _L3_gnn_all = _L3_gnn_setup()
    _L3_gnn_in = {k: v for k, v in _L3_gnn_all.items() if k in ('W', 'b')}
    del _L3_gnn_all
    return {'x': x, 'src': src, 'dst': dst, 'edge_attr_64': edge_attr_64, 'edge_weight': edge_weight, 'edge_weight1': edge_weight1, 'L0_gnn_Wq': _L0_gnn_in['Wq'], 'L0_gnn_Wk': _L0_gnn_in['Wk'], 'L0_gnn_Wv': _L0_gnn_in['Wv'], 'L0_gnn_W1': _L0_gnn_in['W1'], 'L0_gnn_b1': _L0_gnn_in['b1'], 'L0_gnn_W2': _L0_gnn_in['W2'], 'L0_gnn_b2': _L0_gnn_in['b2'], 'L0_gnn_Wo': _L0_gnn_in['Wo'], 'L0_gnn_bo': _L0_gnn_in['bo'], 'L1_gnn_W': _L1_gnn_in['W'], 'L1_gnn_b': _L1_gnn_in['b'], 'L2_gnn_W': _L2_gnn_in['W'], 'L2_gnn_b': _L2_gnn_in['b'], 'L3_gnn_W': _L3_gnn_in['W'], 'L3_gnn_b': _L3_gnn_in['b']}

def reference(x, src, dst, edge_attr_64, edge_weight, edge_weight1, L0_gnn_Wq, L0_gnn_Wk, L0_gnn_Wv, L0_gnn_W1, L0_gnn_b1, L0_gnn_W2, L0_gnn_b2, L0_gnn_Wo, L0_gnn_bo, L1_gnn_W, L1_gnn_b, L2_gnn_W, L2_gnn_b, L3_gnn_W, L3_gnn_b):
    import jax
    import jax.numpy as jnp

    def _L0_gnn_ref(h, efeat, src, dst, Wq, Wk, Wv, W1, b1, W2, b2, Wo, bo):
        import jax, jax.numpy as jnp
        import numpy as np
        N, E, D, H, FE = (50000, 25000, 256, 8, 64)
        HD = D // H
        n = h.shape[0]
        Q = (h @ Wq).reshape(n, H, HD)
        K = (h @ Wk).reshape(n, H, HD)
        V = (h @ Wv).reshape(n, H, HD)
        score = jnp.einsum('ehd,ehd->eh', Q[dst], K[src]) / np.sqrt(HD)
        score = score + jax.nn.relu(efeat @ W1 + b1) @ W2 + b2
        m = jax.ops.segment_max(score, dst, num_segments=n)
        ex = jnp.exp(score - m[dst])
        denom = jax.ops.segment_sum(ex, dst, num_segments=n)
        alpha = ex / denom[dst]
        out = jax.ops.segment_sum(alpha[:, :, None] * V[src], dst, num_segments=n)
        out = out.reshape(n, D)
        return out @ Wo + bo

    def _L1_gnn_ref(x, edge_index, edge_weight, W, b):
        import jax, jax.numpy as jnp
        import numpy as np
        N_NODES = 3125
        K_HOPS = 2
        ALPHA = 0.5

        def _gcn_norm(edge_index, edge_weight, num_nodes):
            loops = jnp.arange(num_nodes, dtype=edge_index.dtype)
            src = jnp.concatenate([edge_index[0], loops])
            dst = jnp.concatenate([edge_index[1], loops])
            w = jnp.concatenate([edge_weight, jnp.ones((num_nodes,), edge_weight.dtype)])
            deg = jax.ops.segment_sum(w, dst, num_segments=num_nodes)
            dinv = jnp.where(deg > 0, jax.lax.rsqrt(jnp.maximum(deg, 1e-12)), 0.0)
            norm = dinv[src] * w * dinv[dst]
            return (src, dst, norm)
        N = x.shape[0]
        src, dst, norm = _gcn_norm(edge_index, edge_weight, N)
        h = x
        for _ in range(K_HOPS):
            msg = jax.ops.segment_sum(norm[:, None] * h[src], dst, num_segments=N)
            h = (1.0 - ALPHA) * msg + ALPHA * x
        h = jax.nn.relu(h)
        return h @ W.T + b

    def _L2_gnn_ref(feat, eweight, W, b, src, dst):
        import jax, jax.numpy as jnp
        import numpy as np
        N_NODES = 10000
        N_EDGES = 10000
        D_IN = 256
        D_OUT = 256
        n = feat.shape[0]
        msg = feat[src] * eweight
        agg = jax.ops.segment_sum(msg, dst, num_segments=n)
        deg = jax.ops.segment_sum(jnp.ones((src.shape[0],), dtype=feat.dtype), dst, num_segments=n)
        h_neigh = agg / jnp.maximum(deg, 1.0)[:, None]
        h = jnp.concatenate([h_neigh, feat], axis=-1)
        return h @ W.T + b

    def _L3_gnn_ref(feature, W, b, src, dst):
        import jax, jax.numpy as jnp
        import numpy as np
        N = 50000
        E = 25000
        DIN = 256
        DOUT = 256
        K_HOPS = 3
        LAMBDA = 0.0
        n = feature.shape[0]
        deg = jax.ops.segment_sum(jnp.ones_like(src, dtype=jnp.float32), src, num_segments=n)
        norm = jnp.clip(deg, 1.0, None) ** (-0.5)
        norm = norm[:, None]
        result = feature @ W + b
        h = feature
        for i in range(1, K_HOPS + 1):
            h = h * norm
            h = jax.ops.segment_sum(h[src], dst, num_segments=n)
            h = h * norm
            y = h @ W + b
            result = result + y * (1.0 - LAMBDA * i)
        return jax.nn.relu(result)
    edge_index = jnp.stack([src, dst])
    x = _layernorm(x + _L0_gnn_ref(x, edge_attr_64, src, dst, L0_gnn_Wq, L0_gnn_Wk, L0_gnn_Wv, L0_gnn_W1, L0_gnn_b1, L0_gnn_W2, L0_gnn_b2, L0_gnn_Wo, L0_gnn_bo), axis=-1)
    x = _layernorm(x + _L1_gnn_ref(x, edge_index, edge_weight, L1_gnn_W, L1_gnn_b), axis=-1)
    x = _layernorm(x + _L2_gnn_ref(x, edge_weight1, L2_gnn_W, L2_gnn_b, src, dst), axis=-1)
    x = _layernorm(x + _L3_gnn_ref(x, L3_gnn_W, L3_gnn_b, src, dst), axis=-1)
    return x

_drawn_inputs = setup_inputs


def setup_inputs(seed=0):
    import zlib

    import numpy as np

    out = dict(_drawn_inputs(seed))
    spreads = {'L0_gnn_b1': (0.0, 0.575),
     'L0_gnn_b2': (0.0, 0.8),
     'L0_gnn_bo': (0.0, 0.1),
     'L3_gnn_b': (0.0, 0.1)}
    factors = {'L1_gnn_b': 2.772, 'L2_gnn_b': 3.902}
    for name, (base, spread) in spreads.items():
        noise = np.random.default_rng([zlib.crc32(name.encode()), seed]).standard_normal(out[name].shape)
        drawn = base * np.exp(spread * noise) if base else spread * noise
        out[name] = jnp.asarray(drawn.astype(out[name].dtype))
    for name, factor in factors.items():
        out[name] = (out[name] * factor).astype(out[name].dtype)
    return out
```

```python
import concourse.bass as bass
from concourse import mybir
from contextlib import ExitStack

F32 = mybir.dt.float32
I32 = mybir.dt.int32
BF16 = mybir.dt.bfloat16
ALU = mybir.AluOpType
ACT = mybir.ActivationFunctionType
AX = mybir.AxisListType

P = 128
N = 3125
D = 256
FC = D // P
E = 53125
HEADS = 8
HD = D // HEADS
FE = 64
TG = 8
EG = TG * P
NG = -(-E // EG)
NG += NG % 2
EP = NG * EG
NB = -(-N // P)
NB += NB % 2
NP = NB * P
NT = NG * TG
PJ = EP // P
BIG = 1.0e30
SEED = 2
XW = HEADS + 2
EPS = 1e-5

PASS_SCORE, PASS_VALUE, PASS_GCN1, PASS_GCN2, PASS_SAGE, PASS_SG1, PASS_SG2, PASS_SG3 = range(8)
HOPS = [PASS_VALUE, PASS_GCN1, PASS_GCN2, PASS_SAGE, PASS_SG1, PASS_SG2, PASS_SG3]


def gnn_program(nc, a, out):
    ctx = ExitStack()
    with ctx:
        def sb(name, shape, dt=F32):
            return ctx.enter_context(nc.sbuf_tensor(name, shape, dt))

        def sem(name):
            return ctx.enter_context(nc.semaphore(name))

        def dram(name, shape):
            return nc.dram_tensor(name, shape, F32).ap()

        q_table = dram("q_table", [NP, D])
        gather_table = {PASS_SCORE: dram("k_table", [NP, D]), PASS_VALUE: dram("v_table", [NP, D])}
        for q in HOPS[1:]:
            gather_table[q] = dram(f"h_table{q}", [NP, D])
        score_dram = dram("score_dram", [EP, HEADS])
        x3_save = dram("x3_save", [NP, D])
        exp_dram = dram("exp_dram", [EP, HEADS])

        x_rows = sb("x_rows", [P, NB, D])
        r_rows = sb("r_rows", [P, NB, D])
        h_rows = sb("h_rows", [P, NB, D])
        acc = sb("acc", [P, FC, NP])
        gath = sb("gath", [P, 2, TG, D])
        onehot = sb("onehot", [P, 2, TG, P])
        q_win = sb("q_win", [P, 2, D])
        prod = sb("prod", [P, 2, 2, D])
        stage = sb("stage", [P, 2, FC, P])
        w_qkv = sb("w_qkv", [P, 3, FC, D])
        w_lin = sb("w_lin", [P, 5, FC, D])
        bias = sb("bias", [P, 4, D])
        w1 = sb("w1", [FE, D])
        b1c = sb("b1c", [P, FC])
        w2 = sb("w2", [P, FC, HEADS])
        b2b = sb("b2b", [P, HEADS])
        src_i = sb("src_i", [P, NT], I32)
        dst_i = sb("dst_i", [P, NT], I32)
        src_lo = sb("src_lo", [P, NT])
        src_hi = sb("src_hi", [P, NT])
        ew = sb("ew", [P, NT])
        ew1 = sb("ew1", [P, NT])
        ones = sb("ones", [P, 1])
        rel = sb("rel", [P, NG, TG])
        base_i = sb("base_i", [P, NG], I32)
        xcol = sb("xcol", [P, 2, TG, XW])
        rden_t = sb("rden", [P, NB, HEADS])
        rden = rden_t[:, :, :]
        idx_slot = sb("idx_slot", [P, 2, TG], I32)
        iota_i = sb("iota_i", [P, P], I32)
        iota_f = sb("iota_f", [P, P])
        part_i = sb("part_i", [P, 1], I32)
        part_f = sb("part_f", [P, 1])
        ident = sb("ident", [P, P])
        zero_b = sb("zero_b", [P, P], BF16)
        den = sb("den", [XW, NP])
        den_stage = sb("den_stage", [XW, 2, P])
        node_sc = sb("node_sc", [P, NB, XW])
        small = sb("small", [P, 12, NB])
        mean, var, std, rstd, dinv, hdinv, deg, rdeg, norm, norm2, tmp_a, tmp_b = (small[:, k, :] for k in range(12))
        ends = sb("ends", [HEADS, 2, P])
        ends_i = sb("ends_i", [HEADS, 2, P], I32)
        chain_m = sb("chain_m", [HEADS, 4, P])
        tails = sb("tails", [HEADS, 4, P])
        carry = sb("carry", [P, 4, HEADS])

        accf = acc[:, :, :].rearrange("p c n -> p (c n)")
        oht = accf[:, 0:2 * EG].rearrange("p (k e) -> p k e", k=2)
        ef = accf[0:FE, 2 * EG:4 * EG].rearrange("p (k e) -> p k e", k=2)
        hid = accf[:, 4 * EG:6 * EG].rearrange("p (u e) -> p u e", u=4)
        ohf = onehot[:, :, :, :].rearrange("p k t n -> p (k t n)").bitcast(BF16)
        oh_lo = ohf[:, 0:2 * EG].rearrange("p (k t n) -> p k t n", k=2, t=TG)
        oh_hi = ohf[:, 2 * EG:2 * EG + 2 * TG * 32].rearrange("p (k t n) -> p k t n", k=2, t=TG)
        hf = h_rows[:, :, :].rearrange("p b d -> p (b d)")
        rf = r_rows[:, :, :].rearrange("p b d -> p (b d)")
        score = hf[:, 0:NT * HEADS]
        expo = hf[:, 0:NT * XW].rearrange("p (t w) -> p t w", w=XW)
        s_run = rf[:, 0:PJ * HEADS].rearrange("p (j h) -> p j h", h=HEADS)
        exp_tiles = rf[:, PJ * HEADS:2 * PJ * HEADS]
        m_run = rf[:, PJ * HEADS:2 * PJ * HEADS].rearrange("p (j h) -> p j h", h=HEADS)
        b_run = accf[:, 0:PJ * HEADS].rearrange("p (j h) -> p j h", h=HEADS)
        dst_run_i = accf[:, PJ * HEADS:PJ * HEADS + PJ].bitcast(I32)
        dst_run = accf[:, PJ * HEADS + PJ:PJ * HEADS + 2 * PJ]
        mask_f = accf[:, PJ * HEADS + 2 * PJ:PJ * HEADS + 3 * PJ]
        mask_b = accf[:, PJ * HEADS + 3 * PJ:PJ * HEADS + 4 * PJ]

        banks = ctx.enter_context(nc.psum_tensor("banks", [P, 8, 512], F32))

        loaded = sem("loaded")
        gath_done = [sem(f"gath_done{k}") for k in range(2)]
        idx_ready = sem("idx_ready")
        pool_step = sem("pool_step")
        consts_done = sem("consts_done")
        dve_link = sem("dve_link")
        rows_ready = sem("rows_ready")
        act_link = sem("act_link")
        tables = sem("tables")
        moved = sem("moved")
        oh_ready = sem("oh_ready")
        msg_ready = sem("msg_ready")
        grp_done = sem("grp_done")
        evac_done = sem("evac_done")
        stg_ready = sem("stg_ready")
        sq_done = sem("sq_done")
        sq_evac = sem("sq_evac")
        hist_oh = sem("hist_oh")
        hist_done = sem("hist_done")
        qwin_done = [sem(f"qwin_done{k}") for k in range(2)]
        ef_done = [sem(f"ef_done{k}") for k in range(2)]
        tr_done = sem("tr_done")
        tr_evac = sem("tr_evac")
        hid_done = sem("hid_done")
        hid_evac = sem("hid_evac")
        s_done = sem("s_done")
        s_read = sem("s_read")
        qk_done = sem("qk_done")
        qk_read = sem("qk_read")
        red_done = sem("red_done")
        pe_small = sem("pe_small")
        b2_loaded = sem("b2_loaded")
        x3_back = sem("x3_back")
        stored = sem("stored")
        pe_step = sem("pe_step")

        N_LOADS = 23

        SQ = {name: r for r, name in enumerate(
            ["q", "k", "v", "l0_rows", "l0_den", "l0_t", "l0_wo", "g1_rows", "g2_rows", "g2_t", "g2_w",
             "sage_w", "x2_t", "x2_w", "s1_rows", "s2_rows", "s3_rows", "s3_t", "s3_w"])}
        READY = {name: v + 1 for v, name in enumerate(
            ["setup", "q_out", "k_out", "v_out", "deg_src", "scores", "tails_f", "chain_f", "tails_b", "chain_b", "shifted",
             "l0_norm", "l0_t", "l0_var", "deg_w", "l0_table", "g1_table", "g2_h", "g2_t", "g2_var", "x2",
             "sage_mean", "x2_t", "sage_var", "x3", "sage_table", "s1_table", "s2_table", "s3_sum", "s3_t", "s3_var",
             "out"])}
        ACTL = {name: v + 1 for v, name in enumerate(
            ["deg_src", "exps", "l0_var", "deg_w", "g2_var", "sage_var", "s3_var"])}

        block = ctx.enter_context(nc.Block())

        def node_rows(t):
            return t.rearrange("(b p) f -> p b f", p=P)

        def hop_no(q):
            return HOPS.index(q)

        def hop_end(q):
            return SEED + NG * (hop_no(q) + 1)

        def bcast_heads(t):
            return t.unsqueeze(3).to_broadcast([P, t.shape[1], HEADS, HD])

        @block.sync
        def _(sp):
            def w_view(t):
                return t.rearrange("(c p) f -> p c f", p=P)

            loads = [
                (src_i[:, :], a["src_t"]), (dst_i[:, :], a["dst_t"]), (ew[:, :], a["ew_t"]), (ew1[:, :], a["ew1_t"]),
                (base_i[:, :], a["base"].partition_broadcast(P)),
                (x_rows[:, :, :], node_rows(a["x"])),
                (acc[:, :, :], a["x_t"].rearrange("(c p) n -> p c n", p=P)),
                (w_qkv[:, 0, :, :], w_view(a["Wq"])), (w_qkv[:, 1, :, :], w_view(a["Wk"])),
                (w_qkv[:, 2, :, :], w_view(a["Wv"])),
                (w_lin[:, 0, :, :], w_view(a["Wo"])), (w_lin[:, 1, :, :], w_view(a["L1_Wt"])),
                (w_lin[:, 2, :, :], w_view(a["L2_Wt"][0:D, :])), (w_lin[:, 3, :, :], w_view(a["L2_Wt"][D:2 * D, :])),
                (w_lin[:, 4, :, :], w_view(a["L3_W"])),
                (bias[:, 0, :], a["bo"].partition_broadcast(P)), (bias[:, 1, :], a["L1_b"].partition_broadcast(P)),
                (bias[:, 2, :], a["L2_b"].partition_broadcast(P)), (bias[:, 3, :], a["L3_b"].partition_broadcast(P)),
                (w1[:, :], a["W1"]), (b1c[:, :], a["b1_t"]), (w2[:, :, :], w_view(a["W2"])),
                (ends_i[:, :, :], a["ends"].partition_broadcast(HEADS)),
            ]
            assert len(loads) == N_LOADS
            for dst, src in loads:
                sp.dma_start(dst, src).then_inc(loaded, 16)
            sp.dma_start(b2b[:, :], a["b2"].partition_broadcast(P)).then_inc(b2_loaded, 16)

            sp.wait_ge(rows_ready, READY["q_out"])
            sp.dma_start(node_rows(q_table), r_rows[:, :, :]).then_inc(tables, 16)
            sp.wait_ge(rows_ready, READY["k_out"])
            sp.dma_start(node_rows(gather_table[PASS_SCORE]), h_rows[:, :, :]).then_inc(tables, 16)
            sp.wait_ge(rows_ready, READY["v_out"])
            sp.dma_start(node_rows(gather_table[PASS_VALUE]), r_rows[:, :, :]).then_inc(tables, 16)
            sp.wait_ge(tables, 16 * 3)

            with sp.Fori(0, NG // 2) as i:
                for k in range(2):
                    g = i * 2 + k
                    first = sp.value_load(base_i[0:1, bass.ds(g, 1)], min_val=0, max_val=NP - P)
                    sp.wait_ge(qk_done, g * 4 + 4)
                    sp.dma_start(q_win[:, k, :], q_table[bass.ds(first, P), :]).then_inc(qwin_done[k], 16)
                    sp.wait_ge(hid_done, g * 4 + 4)
                    sp.dma_start(ef[:, k, :], a["ef_t"][:, bass.ds(g * EG, EG)]).then_inc(ef_done[k], 16)

            sp.wait_ge(rows_ready, READY["scores"])
            sp.dma_start(score_dram.rearrange("(g p i) h -> p g (i h)", g=NG, p=P),
                         score.rearrange("p (g x) -> p g x", g=NG)).then_inc(moved, 16)
            sp.wait_ge(moved, 16)
            sp.dma_start(dst_run_i, a["dst_run"]).then_inc(moved, 16)
            sp.dma_start(s_run, score_dram.rearrange("(p j) h -> p j h", p=P)).then_inc(moved, 16)
            sp.wait_ge(act_link, ACTL["exps"])
            sp.dma_start(exp_dram.rearrange("(p j) h -> p j h", p=P), s_run).then_inc(moved, 16)
            sp.wait_ge(moved, 64)
            sp.dma_start(exp_tiles.rearrange("p (g x) -> p g x", g=NG),
                         exp_dram.rearrange("(g p i) h -> p g (i h)", g=NG, p=P)).then_inc(moved, 16)

            for name, dst, rows in [
                    ("l0_table", gather_table[PASS_GCN1], h_rows), ("g1_table", gather_table[PASS_GCN2], h_rows),
                    ("x2", gather_table[PASS_SAGE], x_rows), ("x3", x3_save, x_rows),
                    ("sage_table", gather_table[PASS_SG1], h_rows), ("s1_table", gather_table[PASS_SG2], h_rows),
                    ("s2_table", gather_table[PASS_SG3], h_rows)]:
                sp.wait_ge(rows_ready, READY[name])
                sp.dma_start(node_rows(dst), rows[:, :, :]).then_inc(tables, 16)
            sp.wait_ge(tables, 16 * 10)
            sp.dma_start(h_rows[:, :, :], node_rows(x3_save)).then_inc(x3_back, 16)
            sp.wait_ge(rows_ready, READY["out"])
            full = N // P
            sp.dma_start(out[0:full * P, :].rearrange("(b p) f -> p b f", p=P), r_rows[:, 0:full, :]).then_inc(stored, 16)
            sp.dma_start(out[full * P:N, :], r_rows[0:N - full * P, full, :]).then_inc(stored, 16)
            sp.wait_ge(stored, 32)

        TABLES_FOR = {PASS_SCORE: 2, PASS_VALUE: 3, PASS_GCN1: 4, PASS_GCN2: 5, PASS_SAGE: 6, PASS_SG1: 8,
                      PASS_SG2: 9, PASS_SG3: 10}

        @block.gpsimd
        def _(pool):
            pool.iota(iota_i[:, :], pattern=[[1, P]], base=0, channel_multiplier=0).then_inc(consts_done, 1)
            pool.iota(part_i[:, :], pattern=[[1, 1]], base=0, channel_multiplier=1).then_inc(consts_done, 1)
            pool.wait_ge(loaded, 16 * N_LOADS)
            for q in range(8):
                pool.wait_ge(tables, 16 * TABLES_FOR[q])
                if q == PASS_VALUE:
                    pool.wait_ge(qk_read, NG * 4 + 8)
                with pool.Fori(0, NG // 2) as i:
                    for k in range(2):
                        g = i * 2 + k
                        if q == PASS_SCORE:
                            pool.wait_ge(qk_read, g * 4 + 4)
                        else:
                            pool.wait_ge(grp_done, g + NG * hop_no(q) + 1)
                        pool.sem_inc(pool_step, 1)
                        pool.tensor_copy(idx_slot[:, k, :], src_i[:, bass.ds(g * TG, TG)]).then_inc(idx_ready, 1)
                        pool.wait_ge(idx_ready, g + NG * q + 1)
                        pool.sem_inc(pool_step, 1)
                        for t in range(TG):
                            pool.indirect_dma_start(gath[:, k, t, :], None, gather_table[q],
                                                    bass.IndirectOffsetOnAxis(idx_slot[:, k, t:t + 1], 0)
                                                    ).then_inc(gath_done[k], 16)

        @block.scalar
        def _(act):
            act.sem_inc(stg_ready, SEED)
            act.sem_inc(hid_evac, 8)
            act.sem_inc(tr_evac, 4)

            def stage_pass(name, src):
                with act.Fori(0, NB // 2) as i:
                    for k in range(2):
                        b = i * 2 + k
                        act.wait_ge(sq_done, b + SQ[name] * NB + 1)
                        if src is den:
                            nc.scalar.activation(den_stage[:, k, :], den[:, bass.ds(b * P, P)], ACT.Copy).then_inc(stg_ready, 1)
                        elif src is acc:
                            nc.scalar.activation(stage[:, k, :, :], acc[:, :, bass.ds(b * P, P)], ACT.Copy).then_inc(stg_ready, 1)
                        else:
                            nc.scalar.activation(stage[:, k, :, :].rearrange("p c n -> p (c n)").unsqueeze(1),
                                                 src[:, bass.ds(b, 1), :], ACT.Copy).then_inc(stg_ready, 1)

            act.wait_ge(rows_ready, READY["setup"])
            for name in ("q", "k", "v"):
                stage_pass(name, acc)
            act.wait_ge(rows_ready, READY["deg_src"])
            nc.scalar.activation(tmp_a, norm, ACT.Sqrt).then_inc(act_link, 1)

            with act.Fori(0, NG // 2) as i:
                for k in range(2):
                    g = i * 2 + k
                    for half in range(2):
                        act.wait_ge(tr_done, g * 2 + half + 1 + 4)
                        act.wait_ge(qk_done, g * 4 + 4)
                        nc.scalar.activation(oht[:, k, half * 512:half * 512 + 512], banks[:, half, :], ACT.Copy
                                             ).then_inc(tr_evac, 1)
                    for u in range(4):
                        half, c = u // 2, u % 2
                        act.wait_ge(hid_done, g * 4 + u + 1 + 8)
                        act.wait_ge(s_done, g * 2 + half + 1)
                        nc.scalar.activation(hid[:, u, :], banks[:, 2 + u % 2, :], ACT.Relu, bias=b1c[:, c:c + 1]
                                             ).then_inc(hid_evac, 1)

            act.wait_ge(rows_ready, READY["shifted"])
            nc.scalar.activation(s_run, s_run, ACT.Exp).then_inc(act_link, 1)

            def root(name, dst, src):
                act.wait_ge(rows_ready, READY[name])
                nc.scalar.activation(dst, src, ACT.Sqrt).then_inc(act_link, 1)

            act.wait_ge(evac_done, hop_end(PASS_VALUE))
            stage_pass("l0_rows", acc)
            stage_pass("l0_den", den)
            act.wait_ge(rows_ready, READY["l0_norm"])
            stage_pass("l0_t", r_rows)
            act.wait_ge(rows_ready, READY["l0_t"])
            stage_pass("l0_wo", acc)
            root("l0_var", std, var)
            root("deg_w", tmp_b, deg)
            act.wait_ge(evac_done, hop_end(PASS_GCN1))
            stage_pass("g1_rows", acc)
            act.wait_ge(evac_done, hop_end(PASS_GCN2))
            stage_pass("g2_rows", acc)
            act.wait_ge(rows_ready, READY["g2_h"])
            stage_pass("g2_t", r_rows)
            act.wait_ge(rows_ready, READY["g2_t"])
            stage_pass("g2_w", acc)
            root("g2_var", std, var)
            act.wait_ge(evac_done, hop_end(PASS_SAGE))
            stage_pass("sage_w", acc)
            act.wait_ge(rows_ready, READY["sage_mean"])
            stage_pass("x2_t", x_rows)
            act.wait_ge(rows_ready, READY["x2_t"])
            stage_pass("x2_w", acc)
            root("sage_var", std, var)
            for q, name in ((PASS_SG1, "s1_rows"), (PASS_SG2, "s2_rows"), (PASS_SG3, "s3_rows")):
                act.wait_ge(evac_done, hop_end(q))
                stage_pass(name, acc)
            act.wait_ge(rows_ready, READY["s3_sum"])
            stage_pass("s3_t", x_rows)
            act.wait_ge(rows_ready, READY["s3_t"])
            stage_pass("s3_w", acc)
            root("s3_var", std, var)

        @block.tensor
        def _(pe):
            pe.sem_inc(sq_done, SEED)
            pe.sem_inc(grp_done, SEED)
            pe.sem_inc(hist_done, SEED)
            pe.sem_inc(qk_done, 8)
            pe.sem_inc(hid_done, 8)
            pe.sem_inc(tr_done, 4)
            pe.sem_inc(s_done, 2)
            pe.wait_ge(rows_ready, READY["setup"])

            def square_pass(name, weight):
                with pe.Fori(0, NB // 2) as i:
                    for k in range(2):
                        b = i * 2 + k
                        pe.wait_ge(stg_ready, b + SQ[name] * NB + 1 + SEED)
                        pe.wait_ge(sq_evac, b + SQ[name] * NB + 1)
                        if weight == "den":
                            pe.sem_inc(pe_step, 1)
                            last = nc.tensor.transpose(banks[:, 6 + k, 0:XW], den_stage[:, k, :], ident[0:XW, 0:XW])
                        else:
                            for c in range(FC):
                                if weight is None:
                                    last = nc.tensor.transpose(banks[:, 6 + k, c * P:(c + 1) * P], stage[:, k, c, :], ident[:, :])
                                else:
                                    last = nc.tensor.matmul(banks[:, 6 + k, 0:D], stage[:, k, c, :], weight[:, c, :],
                                                            start=(c == 0), stop=(c == FC - 1))
                        last.then_inc(sq_done, 1)

            for n, name in enumerate(("q", "k", "v")):
                square_pass(name, w_qkv[:, n, :, :])

            pe.wait_ge(sq_evac, SEED + 3 * NB)
            nc.tensor.matmul(banks[:, 7, 0:32], zero_b[:, :], zero_b[:, 0:32], start=True, stop=False)
            with pe.Fori(0, NG // 2) as i:
                for k in range(2):
                    pe.wait_ge(hist_oh, i * 2 + k + 1)
                    for t in range(TG):
                        last = nc.tensor.matmul(banks[:, 7, 0:32], oh_lo[:, k, t, :], oh_hi[:, k, t, :], start=False, stop=False,
                                                skip_group_check=True)
                    last.then_inc(hist_done, 1)
            nc.tensor.matmul(banks[:, 7, 0:32], zero_b[:, :], zero_b[:, 0:32], start=False, stop=True
                             ).then_inc(hist_done, 1)

            with pe.Fori(0, NG // 2) as i:
                for k in range(2):
                    g = i * 2 + k
                    pe.wait_ge(oh_ready, g + 1)
                    for half in range(2):
                        pe.wait_ge(tr_evac, g * 2 + half + 3)
                        for t in range(4):
                            last = nc.tensor.transpose(banks[:, half, t * P:(t + 1) * P], onehot[:, k, half * 4 + t, :], ident[:, :])
                        last.then_inc(tr_done, 1)
                    pe.wait_ge(ef_done[k], i * 16 + 16)
                    for half in range(2):
                        for c in range(2):
                            u = half * 2 + c
                            pe.wait_ge(hid_evac, g * 4 + u + 7)
                            nc.tensor.matmul(banks[:, 2 + u % 2, :], w1[:, c * P:(c + 1) * P],
                                             ef[:, k, half * 512:half * 512 + 512], start=True, stop=True).then_inc(hid_done, 1)
                    pe.wait_ge(s_read, g + 1)
                    for half in range(2):
                        pe.wait_ge(hid_evac, g * 4 + half * 2 + 10)
                        for t in range(4):
                            for c in range(2):
                                col = (half * 4 + t) * HEADS
                                last = nc.tensor.matmul(banks[:, 6, col:col + HEADS], hid[:, half * 2 + c, t * P:(t + 1) * P],
                                                        w2[:, c, :], start=(c == 0), stop=(c == 1))
                        last.then_inc(s_done, 1)
                    pe.wait_ge(qwin_done[k], i * 16 + 16)
                    for pair in range(4):
                        pe.wait_ge(tr_evac, g * 2 + pair // 2 + 5)
                        pe.wait_ge(qk_read, g * 4 + pair + 7)
                        for t in range(2):
                            tile = pair * 2 + t
                            last = nc.tensor.matmul(banks[:, 4 + pair % 2, t * D:(t + 1) * D], oht[:, k, tile * P:(tile + 1) * P],
                                                    q_win[:, k, :], start=True, stop=True)
                        last.then_inc(qk_done, 1)

            for n in range(2):
                pe.wait_ge(rows_ready, READY["tails_f" if n == 0 else "tails_b"])
                nc.tensor.transpose(banks[0:HEADS, 7, 0:P], carry[:, 2 * n, :], ident[:, :]).then_inc(pe_small, 1)
                pe.wait_ge(rows_ready, READY["chain_f" if n == 0 else "chain_b"])
                nc.tensor.transpose(banks[:, 7, P:P + HEADS], tails[:, 2 * n + 1, :], ident[0:HEADS, 0:HEADS]).then_inc(pe_small, 1)

            def hop_pass(q):
                h = hop_no(q)
                with pe.Fori(0, NG // 2) as i:
                    for k in range(2):
                        g = i * 2 + k
                        pe.wait_ge(oh_ready, g + NG * q + 1)
                        if q == PASS_VALUE:
                            pe.wait_ge(msg_ready, g + 1)
                        else:
                            pe.wait_ge(gath_done[k], i * (16 * TG) + 16 * TG * (NG // 2 * q + 1))
                        pe.wait_ge(evac_done, g + NG * h + 1)
                        for t in range(TG):
                            for c in range(FC):
                                last = nc.tensor.matmul(banks[:, 3 * k + c, 0:P], gath[:, k, t, c * P:(c + 1) * P],
                                                        onehot[:, k, t, :], start=(t == 0), stop=(t == TG - 1))
                            if q == PASS_VALUE:
                                last = nc.tensor.matmul(banks[0:XW, 3 * k + 2, 0:P], xcol[:, k, t, :],
                                                        onehot[:, k, t, :], start=(t == 0), stop=(t == TG - 1))
                        last.then_inc(grp_done, 1)

            hop_pass(PASS_VALUE)
            square_pass("l0_rows", None)
            square_pass("l0_den", "den")
            square_pass("l0_t", None)
            square_pass("l0_wo", w_lin[:, 0, :, :])
            hop_pass(PASS_GCN1)
            square_pass("g1_rows", None)
            hop_pass(PASS_GCN2)
            square_pass("g2_rows", None)
            square_pass("g2_t", None)
            square_pass("g2_w", w_lin[:, 1, :, :])
            hop_pass(PASS_SAGE)
            square_pass("sage_w", w_lin[:, 2, :, :])
            square_pass("x2_t", None)
            square_pass("x2_w", w_lin[:, 3, :, :])
            for q, name in ((PASS_SG1, "s1_rows"), (PASS_SG2, "s2_rows"), (PASS_SG3, "s3_rows")):
                hop_pass(q)
                square_pass(name, None)
            square_pass("s3_t", None)
            square_pass("s3_w", w_lin[:, 4, :, :])

        @block.vector
        def _(dve):
            chain = [0]

            def link(ins):
                chain[0] += 1
                ins.then_inc(dve_link, 1)
                dve.wait_ge(dve_link, chain[0])

            def ready(ins, name):
                ins.then_inc(rows_ready, 1)
                dve.wait_ge(rows_ready, READY[name])

            def per_node(t):
                return t.unsqueeze(2).to_broadcast([P, NB, D])

            dve.sem_inc(sq_evac, SEED)
            dve.sem_inc(evac_done, SEED)
            dve.sem_inc(qk_read, 8)
            dve.sem_inc(s_read, 1)
            dve.wait_ge(consts_done, 2)
            dve.wait_ge(loaded, 16 * N_LOADS)
            nc.vector.memset(zero_b[:, :], 0.0)
            nc.vector.memset(ones[:, :], 1.0)
            nc.vector.tensor_copy(part_f[:, :], part_i[:, :])
            link(nc.vector.tensor_copy(iota_f[:, :], iota_i[:, :]))
            nc.vector.tensor_scalar(ident[:, :], iota_f[:, :], part_f[:, :], None, ALU.is_equal)
            nc.vector.tensor_tensor(rel[:, :, :], dst_i[:, :].rearrange("p (g t) -> p g t", g=NG),
                                    base_i[:, :].unsqueeze(2).to_broadcast([P, NG, TG]), ALU.subtract)
            lo_i = gath[:, 0, 0:2, :].rearrange("p a b -> p (a b)").bitcast(I32)[:, 0:NT]
            hi_i = gath[:, 0, 2:4, :].rearrange("p a b -> p (a b)").bitcast(I32)[:, 0:NT]
            nc.vector.tensor_scalar(lo_i, src_i[:, :], P - 1, None, ALU.bitwise_and)
            link(nc.vector.tensor_scalar(hi_i, src_i[:, :], 7, None, ALU.arith_shift_right))
            nc.vector.tensor_copy(src_lo[:, :], lo_i)
            ready(nc.vector.tensor_copy(src_hi[:, :], hi_i), "setup")

            def evac_pass(name, dst):
                with dve.Fori(0, NB // 2) as i:
                    for k in range(2):
                        b = i * 2 + k
                        dve.wait_ge(sq_done, b + SQ[name] * NB + 1 + SEED)
                        if dst is node_sc:
                            nc.vector.tensor_copy(node_sc[:, bass.ds(b, 1), :], banks[:, 6 + k, 0:XW].unsqueeze(1)).then_inc(sq_evac, 1)
                        elif dst is acc:
                            nc.vector.tensor_copy(acc[:, :, bass.ds(b * P, P)],
                                                  banks[:, 6 + k, 0:D].rearrange("p (c n) -> p c n", c=FC)).then_inc(sq_evac, 1)
                        else:
                            nc.vector.tensor_copy(dst[:, bass.ds(b, 1), :], banks[:, 6 + k, 0:D].unsqueeze(1)).then_inc(sq_evac, 1)
                dve.wait_ge(sq_evac, SEED + (SQ[name] + 1) * NB)

            evac_pass("q", r_rows)
            dve.sem_inc(rows_ready, 1)
            evac_pass("k", h_rows)
            dve.sem_inc(rows_ready, 1)
            dve.wait_ge(tables, 16)
            dve.wait_ge(tables, 32)
            evac_pass("v", r_rows)
            dve.sem_inc(rows_ready, 1)

            with dve.Fori(0, NG // 2) as i:
                for k in range(2):
                    g = i * 2 + k
                    dve.wait_ge(hist_done, g + 1)
                    nc.vector.tensor_tensor(oh_hi[:, k, :, :], iota_f[:, 0:32].unsqueeze(1).to_broadcast([P, TG, 32]),
                                            src_hi[:, bass.ds(g * TG, TG)].unsqueeze(2).to_broadcast([P, TG, 32]), ALU.is_equal)
                    nc.vector.tensor_tensor(oh_lo[:, k, :, :], iota_f[:, :].unsqueeze(1).to_broadcast([P, TG, P]),
                                            src_lo[:, bass.ds(g * TG, TG)].unsqueeze(2).to_broadcast([P, TG, P]), ALU.is_equal
                                            ).then_inc(hist_oh, 1)
            dve.wait_ge(hist_done, SEED + NG + 1)
            ready(nc.vector.tensor_scalar(norm, banks[:, 7, 0:NB], 1.0, None, ALU.max), "deg_src")
            dve.wait_ge(act_link, ACTL["deg_src"])
            link(nc.vector.reciprocal(norm, tmp_a))
            link(nc.vector.tensor_tensor(norm2, norm, norm, ALU.mult))

            weights = {PASS_SCORE: None, PASS_VALUE: None, PASS_GCN1: ew, PASS_GCN2: ew, PASS_SAGE: ew1,
                       PASS_SG1: None, PASS_SG2: None, PASS_SG3: None}

            def make_onehot(q, g, k):
                w = weights[q]
                for t in range(TG):
                    r = rel[:, bass.ds(g, 1), t:t + 1].rearrange("p a b -> p (a b)")
                    if w is None:
                        last = nc.vector.tensor_scalar(onehot[:, k, t, :], iota_f[:, :], r, None, ALU.is_equal)
                    else:
                        last = nc.vector.tensor_scalar(onehot[:, k, t, :], iota_f[:, :], r,
                                                       w[:, bass.ds(g * TG + t, 1)], ALU.is_equal, ALU.mult)
                last.then_inc(oh_ready, 1)

            def groups(prepare, finish):
                prepare(0, 0)
                with dve.Fori(0, NG // 2 - 1) as i:
                    for k in range(2):
                        prepare(i * 2 + k + 1, 1 - k)
                        finish(i * 2 + k, k, i)
                prepare(NG - 1, 1)
                finish(NG - 2, 0, NG // 2 - 1)
                finish(NG - 1, 1, NG // 2 - 1)

            def score_prepare(g, k):
                dve.wait_ge(tr_done, g * 2 + 2)
                make_onehot(PASS_SCORE, g, k)

            def score_finish(g, k, i):
                dve.wait_ge(gath_done[k], i * (16 * TG) + 16 * TG)
                for pair in range(4):
                    dve.wait_ge(qk_done, g * 4 + pair + 1 + 8)
                    dve.wait_ge(red_done, g * 4 + pair + 7)
                    nc.vector.tensor_tensor(prod[:, pair % 2, :, :], banks[:, 4 + pair % 2, :].rearrange("p (t d) -> p t d", t=2),
                                            gath[:, k, 2 * pair:2 * pair + 2, :], ALU.mult).then_inc(qk_read, 1)
                    dve.wait_ge(qk_read, g * 4 + pair + 1 + 8)
                    nc.vector.tensor_reduce(score[:, bass.ds(g * (TG * HEADS) + pair * 2 * HEADS, 2 * HEADS)],
                                            prod[:, pair % 2, :, :].rearrange("p t (h d) -> p (t h) d", h=HEADS),
                                            AX.X, ALU.add).then_inc(red_done, 1)
                dve.wait_ge(red_done, g * 4 + 4 + 8)
                dve.wait_ge(s_done, g * 2 + 2 + 2)
                part = score[:, bass.ds(g * (TG * HEADS), TG * HEADS)]
                nc.vector.scalar_tensor_tensor(part, part, float(HD) ** -0.5, banks[:, 6, 0:TG * HEADS], ALU.mult, ALU.add
                                               ).then_inc(s_read, 1)

            dve.sem_inc(red_done, 8)
            dve.wait_ge(tables, 48)
            groups(score_prepare, score_finish)
            dve.wait_ge(s_read, NG + 1)
            dve.wait_ge(b2_loaded, 16)
            s3 = score.rearrange("p (t h) -> p t h", h=HEADS)
            ready(nc.vector.tensor_tensor(s3, s3, b2b[:, :].unsqueeze(1).to_broadcast([P, NT, HEADS]), ALU.add), "scores")

            dve.wait_ge(moved, 48)
            first, last_ = ends[:, 0, :], ends[:, 1, :]
            link(nc.vector.tensor_copy(ends[:, :, :], ends_i[:, :, :]))
            link(nc.vector.tensor_copy(dst_run, dst_run_i))

            def to_mask(m):
                link(nc.vector.tensor_scalar(m, m, BIG, -BIG, ALU.mult, ALU.add))

            link(nc.vector.tensor_tensor(mask_f[:, 1:PJ], dst_run[:, 1:PJ], dst_run[:, 0:PJ - 1], ALU.is_equal))
            link(nc.vector.memset(mask_f[:, 0:1], 1.0))
            to_mask(mask_f)
            link(nc.vector.tensor_copy(mask_b[:, 0:PJ - 1], mask_f[:, 1:PJ]))
            link(nc.vector.memset(mask_b[:, PJ - 1:PJ], 0.0))
            link(nc.vector.memset(chain_m[:, :, :], 0.0))
            link(nc.vector.tensor_tensor(chain_m[:, 0, :], first, last_, ALU.is_equal))
            link(nc.vector.tensor_tensor(chain_m[:, 1, 1:P], first[:, 1:P], last_[:, 0:P - 1], ALU.is_equal))
            link(nc.vector.tensor_tensor(chain_m[:, 2, 1:P], chain_m[:, 0, 1:P], chain_m[:, 1, 1:P], ALU.mult))
            link(nc.vector.tensor_tensor(chain_m[:, 3, 0:P - 1], chain_m[:, 0, 0:P - 1], chain_m[:, 1, 1:P], ALU.mult))
            to_mask(chain_m[:, 1:4, :])

            def scan_heads(dst, src, mask, back, initial):
                for h in range(HEADS):
                    d, s, m = dst[:, :, h], src[:, :, h], mask
                    if back:
                        d, s, m = d[:, ::-1], s[:, ::-1], m[:, ::-1]
                    last = nc.vector.tensor_tensor_scan(d, m, s, -BIG if initial is None else initial[:, h:h + 1], ALU.add, ALU.max)
                    link(last)

            for n, (dst, src, mask) in enumerate(((m_run, s_run, mask_f), (b_run, m_run, mask_b))):
                scan_heads(dst, src, mask, n == 1, None)
                edge = PJ - 1 if n == 0 else 0
                ready(nc.vector.tensor_copy(carry[:, 2 * n, :], dst[:, edge, :]), "tails_f" if n == 0 else "tails_b")
                dve.wait_ge(pe_small, 2 * n + 1)
                link(nc.vector.tensor_copy(tails[:, 2 * n, :], banks[0:HEADS, 7, 0:P]))
                run, tl, cm = chain_m[:, 2 + n, :], tails[:, 2 * n, :], tails[:, 2 * n + 1, :]
                if n == 0:
                    link(nc.vector.tensor_tensor_scan(cm, run, tl, -BIG, ALU.add, ALU.max))
                    link(nc.vector.memset(tl[:, 0:1], -BIG))
                    link(nc.vector.tensor_tensor(tl[:, 1:P], cm[:, 0:P - 1], chain_m[:, 1, 1:P], ALU.add))
                else:
                    link(nc.vector.tensor_tensor_scan(cm[:, ::-1], run[:, ::-1], tl[:, ::-1], -BIG, ALU.add, ALU.max))
                    link(nc.vector.memset(tl[:, P - 1:P], -BIG))
                    link(nc.vector.tensor_tensor(tl[:, 0:P - 1], cm[:, 1:P], chain_m[:, 1, 1:P], ALU.add))
                ready(nc.vector.tensor_copy(cm, tl), "chain_f" if n == 0 else "chain_b")
                dve.wait_ge(pe_small, 2 * n + 2)
                link(nc.vector.tensor_copy(carry[:, 2 * n + 1, :], banks[:, 7, P:P + HEADS]))
                scan_heads(dst, src, mask, n == 1, carry[:, 2 * n + 1, :])
            ready(nc.vector.tensor_tensor(s_run, s_run, b_run, ALU.subtract), "shifted")
            dve.wait_ge(moved, 80)
            link(nc.vector.tensor_copy(expo[:, :, 0:HEADS], exp_tiles.rearrange("p (t h) -> p t h", h=HEADS)))
            link(nc.vector.memset(expo[:, :, HEADS:HEADS + 1], 1.0))
            link(nc.vector.tensor_copy(expo[:, :, HEADS + 1:XW], ew[:, :].unsqueeze(2)))

            def hop(q):
                h = hop_no(q)
                link(nc.vector.memset(acc[:, :, :], 0.0))
                if q == PASS_VALUE:
                    link(nc.vector.memset(den[:, :], 0.0))

                def prepare(g, k):
                    dve.wait_ge(grp_done, g + NG * h + 1)
                    make_onehot(q, g, k)
                    if q == PASS_VALUE:
                        i = g // 2 if isinstance(g, int) else (g - k) // 2
                        dve.wait_ge(gath_done[k], value_count(g, k))
                        rows = gath[:, k, :, :].rearrange("p t (h d) -> p t h d", h=HEADS)
                        e = expo[:, bass.ds(g * TG, TG), 0:HEADS].unsqueeze(3).to_broadcast([P, TG, HEADS, HD])
                        nc.vector.tensor_tensor(rows, rows, e, ALU.mult)
                        nc.vector.tensor_copy(xcol[:, k, :, :], expo[:, bass.ds(g * TG, TG), :]).then_inc(msg_ready, 1)

                def value_count(g, k):
                    if isinstance(g, int):
                        return 16 * TG * (NG // 2 + g // 2 + 1)
                    return (g - k) * (8 * TG) + 16 * TG * (NG // 2 + 1)

                def finish(g, k, i):
                    first = dve.value_load(base_i[0:1, bass.ds(g, 1)], min_val=0, max_val=NP - P)
                    dve.wait_ge(grp_done, g + NG * h + 1 + SEED)
                    dve.wait_ge(evac_done, g + NG * h + SEED)
                    win = acc[:, :, bass.ds(first, P)]
                    if q == PASS_VALUE:
                        dw = den[:, bass.ds(first, P)]
                        nc.vector.tensor_tensor(dw, dw, banks[0:XW, 3 * k + 2, 0:P], ALU.add)
                    nc.vector.tensor_tensor(win, win, banks[:, 3 * k:3 * k + 2, 0:P], ALU.add).then_inc(evac_done, 1)

                groups(prepare, finish)
                dve.wait_ge(evac_done, hop_end(q))

            def scale_nodes(dst, src, t):
                link(nc.vector.tensor_tensor(dst, src, per_node(t), ALU.mult))

            R, H, X = r_rows[:, :, :], h_rows[:, :, :], x_rows[:, :, :]

            def add_bias(n, scale=None):
                link(nc.vector.tensor_tensor(R, R, bias[:, n, :].unsqueeze(1).to_broadcast([P, NB, D]), ALU.add))

            def layernorm(name, dst):
                link(nc.vector.tensor_reduce(mean, R, AX.X, ALU.add))
                link(nc.vector.tensor_scalar(mean, mean, 1.0 / D, None, ALU.mult))
                link(nc.vector.tensor_tensor(R, R, per_node(mean), ALU.subtract))
                link(nc.vector.tensor_tensor(H, R, R, ALU.mult))
                link(nc.vector.tensor_reduce(var, H, AX.X, ALU.add))
                ready(nc.vector.tensor_scalar(var, var, 1.0 / D, EPS, ALU.mult, ALU.add), name)
                dve.wait_ge(act_link, ACTL[name])
                link(nc.vector.reciprocal(rstd, std))
                return nc.vector.tensor_tensor(dst, R, per_node(rstd), ALU.mult)

            hop(PASS_VALUE)
            evac_pass("l0_rows", r_rows)
            evac_pass("l0_den", node_sc)
            link(nc.vector.tensor_scalar(rden, node_sc[:, :, 0:HEADS], 1e-30, None, ALU.max))
            link(nc.vector.reciprocal(rden, rden))
            r4 = R.rearrange("p b (h d) -> p b h d", h=HEADS)
            ready(nc.vector.tensor_tensor(r4, r4, rden.unsqueeze(3).to_broadcast([P, NB, HEADS, HD]), ALU.mult), "l0_norm")
            evac_pass("l0_t", acc)
            dve.sem_inc(rows_ready, 1)
            evac_pass("l0_wo", r_rows)
            add_bias(0)
            link(nc.vector.tensor_tensor(R, R, X, ALU.add))
            link(layernorm("l0_var", X))
            wsum, count = node_sc[:, :, HEADS + 1], node_sc[:, :, HEADS]
            link(nc.vector.tensor_scalar(deg, wsum, 1.0, None, ALU.add))
            link(nc.vector.tensor_scalar(hdinv, deg, 0.0, None, ALU.is_gt))
            ready(nc.vector.tensor_scalar(deg, deg, 1e-12, None, ALU.max), "deg_w")
            dve.wait_ge(act_link, ACTL["deg_w"])
            link(nc.vector.reciprocal(dinv, tmp_b))
            link(nc.vector.tensor_tensor(dinv, dinv, hdinv, ALU.mult))
            link(nc.vector.tensor_scalar(hdinv, dinv, 0.5, None, ALU.mult))
            link(nc.vector.tensor_scalar(rdeg, count, 1.0, None, ALU.max))
            link(nc.vector.reciprocal(rdeg, rdeg))
            ready(nc.vector.tensor_tensor(H, X, per_node(dinv), ALU.mult), "l0_table")

            def restart():
                link(nc.vector.tensor_tensor(R, R, H, ALU.add))
                scale_nodes(R, R, hdinv)
                link(nc.vector.scalar_tensor_tensor(R, X, 0.5, R, ALU.mult, ALU.add))

            hop(PASS_GCN1)
            evac_pass("g1_rows", r_rows)
            restart()
            dve.wait_ge(tables, 16 * 4)
            ready(nc.vector.tensor_tensor(H, R, per_node(dinv), ALU.mult), "g1_table")
            hop(PASS_GCN2)
            evac_pass("g2_rows", r_rows)
            restart()
            ready(nc.vector.tensor_scalar(R, R, 0.0, None, ALU.max), "g2_h")
            evac_pass("g2_t", acc)
            dve.sem_inc(rows_ready, 1)
            evac_pass("g2_w", r_rows)
            add_bias(1)
            link(nc.vector.tensor_tensor(R, R, X, ALU.add))
            dve.wait_ge(tables, 16 * 5)
            ready(layernorm("g2_var", X), "x2")
            hop(PASS_SAGE)
            evac_pass("sage_w", r_rows)
            ready(nc.vector.tensor_tensor(R, R, per_node(rdeg), ALU.mult), "sage_mean")
            evac_pass("x2_t", acc)
            dve.sem_inc(rows_ready, 1)
            evac_pass("x2_w", h_rows)
            link(nc.vector.tensor_tensor(R, R, H, ALU.add))
            add_bias(2)
            link(nc.vector.tensor_tensor(R, R, X, ALU.add))
            dve.wait_ge(tables, 16 * 6)
            ready(layernorm("sage_var", X), "x3")
            ready(nc.vector.tensor_tensor(H, X, per_node(norm), ALU.mult), "sage_table")
            dve.wait_ge(tables, 16 * 8)
            for q, name, table in ((PASS_SG1, "s1_rows", "s1_table"), (PASS_SG2, "s2_rows", "s2_table"), (PASS_SG3, "s3_rows", None)):
                hop(q)
                evac_pass(name, r_rows)
                if table:
                    ready(nc.vector.tensor_tensor(H, R, per_node(norm2), ALU.mult), table)
                scale_nodes(R, R, norm)
                last = nc.vector.tensor_tensor(X, X, R, ALU.add)
                if table:
                    link(last)
                else:
                    ready(last, "s3_sum")
            evac_pass("s3_t", acc)
            dve.sem_inc(rows_ready, 1)
            evac_pass("s3_w", r_rows)
            for _ in range(4):
                add_bias(3)
            link(nc.vector.tensor_scalar(R, R, 0.0, None, ALU.max))
            dve.wait_ge(x3_back, 16)
            link(nc.vector.tensor_tensor(R, R, H, ALU.add))
            ready(layernorm("s3_var", R), "out")


def kernel(**inputs):
    import numpy as np
    import concourse.bacc as bacc
    from concourse.bass_utils import run_bass_kernel_spmd

    nc = bacc.Bacc("TRN2", target_bir_lowering=False, num_devices=1)
    x = np.asarray(inputs["x"])

    def padded(v, fill, rows):
        v = np.asarray(v)
        o = np.full((rows,) + v.shape[1:], fill, v.dtype)
        o[:v.shape[0]] = v
        return o

    def tiles(v):
        return v.reshape(NG, P, TG).transpose(1, 0, 2).reshape(P, NT)

    xp = padded(x, 0, NP)
    src = padded(inputs["src"], N, EP)
    dst = padded(inputs["dst"], N, EP)
    run = dst.reshape(P, PJ)
    ef = padded(inputs["edge_attr_64"], 0, EP)
    arrays = {
        "x": xp, "x_t": xp.T,
        "src_t": tiles(src), "dst_t": tiles(dst), "dst_run": run,
        "base": dst[::EG], "ends": np.stack([run[:, 0], run[:, -1]]),
        "ew_t": tiles(padded(inputs["edge_weight"], 0, EP)),
        "ew1_t": tiles(padded(np.asarray(inputs["edge_weight1"])[:, 0], 0, EP)),
        "ef_t": ef.reshape(NG, P, TG, FE).transpose(3, 0, 2, 1).reshape(FE, EP),
        "Wq": inputs["L0_gnn_Wq"], "Wk": inputs["L0_gnn_Wk"], "Wv": inputs["L0_gnn_Wv"], "Wo": inputs["L0_gnn_Wo"],
        "W1": inputs["L0_gnn_W1"], "b1_t": np.asarray(inputs["L0_gnn_b1"]).reshape(FC, P).T,
        "W2": inputs["L0_gnn_W2"], "b2": inputs["L0_gnn_b2"], "bo": inputs["L0_gnn_bo"],
        "L1_Wt": np.asarray(inputs["L1_gnn_W"]).T, "L1_b": inputs["L1_gnn_b"],
        "L2_Wt": np.asarray(inputs["L2_gnn_W"]).T, "L2_b": inputs["L2_gnn_b"],
        "L3_W": inputs["L3_gnn_W"], "L3_b": inputs["L3_gnn_b"],
    }
    arrays = {k: np.ascontiguousarray(v) for k, v in arrays.items()}
    a = {k: nc.dram_tensor("in_" + k, v.shape, mybir.dt.from_np(v.dtype), kind="ExternalInput").ap()
         for k, v in arrays.items()}
    out = nc.dram_tensor("out", [N, D], F32, kind="ExternalOutput").ap()
    gnn_program(nc, a, out)
    r = run_bass_kernel_spmd(nc, [{"in_" + k: v for k, v in arrays.items()}], core_ids=[0])
    return r.results[0]["out"]
```

```python
import concourse.bass as bass
from concourse import mybir
from contextlib import ExitStack

F32 = mybir.dt.float32
I32 = mybir.dt.int32
BF16 = mybir.dt.bfloat16
F16 = mybir.dt.float16
ALU = mybir.AluOpType
ACT = mybir.ActivationFunctionType
AX = mybir.AxisListType

P = 128
N = 3125
D = 256
FC = D // P
E = 53125
HEADS = 8
HD = D // HEADS
FE = 64
TG = 8
EG = TG * P
NG = -(-E // EG)
NG += NG % 2
EP = NG * EG
NT = NG * TG
PJ = EP // P
NB = -(-N // P)
NP = NB * P
NA = NP + P
LAG = 3
LOOPED = NG // 2 - LAG
BIG = 1.0e30
XW = HEADS + 2
EPS = 1e-5
SW = 32
ST = 7
STRIPS = 2 * NG
PER_BLOCK = P // SW
SC = NB * SW
SPLIT_BANK = 512 // SW

PASS_SCORE, PASS_VALUE, PASS_GCN1, PASS_GCN2, PASS_SAGE, PASS_SG1, PASS_SG2, PASS_SG3 = range(8)
HOPS = [PASS_VALUE, PASS_GCN1, PASS_GCN2, PASS_SAGE, PASS_SG1, PASS_SG2, PASS_SG3]
TABLED = [PASS_VALUE, PASS_GCN1, PASS_GCN2, PASS_SG3]
GATHERED = [PASS_GCN1, PASS_GCN2, PASS_SAGE]
SUMMED = [PASS_VALUE] + GATHERED
BUILDS = [PASS_GCN2, PASS_SAGE]
COUNTED = [PASS_SG1, PASS_SG2, PASS_SG3]
DENSE = {PASS_VALUE: 0, PASS_GCN2: 1, PASS_SAGE: 3, PASS_SG3: 4}
TURNED = [PASS_VALUE, PASS_GCN2, PASS_SG3]


def gnn_program(nc, a, out):
    ctx = ExitStack()
    with ctx:
        def sb(name, shape, dt=F32):
            return ctx.enter_context(nc.sbuf_tensor(name, shape, dt))

        def sem(name):
            return ctx.enter_context(nc.semaphore(name))

        def dram(name, shape):
            return nc.dram_tensor(name, shape, F32).ap()

        q_table = dram("q_table", [NP, D])
        kv_table = dram("kv_table", [NP, 2 * D])
        table = {q: dram(f"h_table{q}", [NP, D]) for q in (PASS_GCN1, PASS_GCN2, PASS_SAGE)}
        counts = nc.dram_tensor("counts", [STRIPS // PER_BLOCK, P, NB, P], BF16).ap()
        v_spill = dram("v_spill", [NG, P, TG, D])
        score_dram = dram("score_dram", [EP, HEADS])
        exp_dram = dram("exp_dram", [EP, HEADS])

        x_rows = sb("x_rows", [P, NB, D])
        r_rows = sb("r_rows", [P, NB, D])
        h_rows = sb("h_rows", [P, NB, D])
        acc = sb("acc", [P, FC, NA])
        gath = sb("gath", [P, 2, TG, 2 * D])
        onehot = sb("onehot", [P, 2, TG, P])
        q_win = sb("q_win", [P, 2, D])
        prod = sb("prod", [P, 2, 2, D])
        w_qkv_t = sb("w_qkv", [P, FC * 3 * D])
        w_lin = sb("w_lin", [P, 5, FC, D])
        bias = sb("bias", [P, 4, D])
        w1 = sb("w1", [FE, D])
        b1c = sb("b1c", [P, FC])
        w2 = sb("w2", [P, FC, HEADS])
        b2b = sb("b2b", [P, HEADS])
        src_i = sb("src_i", [P, NT + 2 * TG], I32)
        dst_i = sb("dst_i", [P, NT], I32)
        src_lo = sb("src_lo", [P, NT])
        src_hi = sb("src_hi", [P, NT])
        ew = sb("ew", [P, NT])
        ew1 = sb("ew1", [P, NT])
        rel = sb("rel", [P, NG, TG])
        base_i = sb("base_i", [P, NG], I32)
        idx_slot = sb("idx_slot", [P, 2, 2 * TG], I32)
        tile0_i = sb("tile0_i", [1, P], I32)
        iota_i = sb("iota_i", [P, P], I32)
        iota_f = sb("iota_f", [P, P])
        part_i = sb("part_i", [P, 1], I32)
        part_f = sb("part_f", [P, 1])
        ident = sb("ident", [P, P])
        zero_b = sb("zero_b", [P, P], BF16)
        eps = sb("eps", [P, 1])
        misc = sb("misc", [P, NA])
        xcol = sb("xcol", [P, 2, TG, XW])
        oh_hi = sb("oh_hi", [P, 2, TG, 32], BF16)
        stage = sb("stage", [P, FC, P])
        den_stage = sb("den_stage", [XW, P])
        x_stage = sb("x_stage", [P, D])
        rows = sb("rows", [P, D])
        turned = sb("turned", [P, FC, P])

        pre_b = sb("pre_b", [P, D])
        tab_row = sb("tab_row", [P, D])
        ysum = sb("ysum", [P, D])
        stats = sb("stats", [P, 6])
        mv = sb("mv", [P, 2])
        std = sb("std", [P, 1])
        rstd = sb("rstd", [P, 1])
        dstd = sb("dstd", [P, 1])
        blk_sc = sb("blk_sc", [P, 20])
        node = sb("node", [P, 8, NB])
        DINV, HDINV, HD2, HD2P, RDEG, NORM, NORM2, OUTDEG = range(8)
        ends = sb("ends", [HEADS, 2, P])
        ends_i = sb("ends_i", [HEADS, 2, P], I32)
        carry = sb("carry", [P, 4, HEADS])

        accf = acc[:, :, :].rearrange("p c n -> p (c n)")
        oht = accf[:, 0:2 * EG].rearrange("p (k e) -> p k e", k=2)
        ef = accf[0:FE, 2 * EG:4 * EG].rearrange("p (k e) -> p k e", k=2)
        hid = accf[:, 4 * EG:6 * EG].rearrange("p (u e) -> p u e", u=4)
        ohf = onehot[:, :, :, :].rearrange("p k t n -> p (k t n)")
        den = misc[0:XW, :]
        miscb = misc[:, :].bitcast(BF16)
        c_build = miscb[:, 0:NB * P].rearrange("p (c n) -> p c n", n=P)
        c_slot = miscb[:, 0:2 * NB * P].rearrange("p (k c n) -> p k c n", k=2, n=P)
        w_qkv = w_qkv_t[:, :].rearrange("p (c f) -> p c f", c=FC)
        key1 = w_qkv_t[:, 0:NT]
        dstrip = w_qkv_t[:, NT:2 * NT]
        key_iota = w_qkv_t[:, 2 * NT:2 * NT + SC // 2].bitcast(F16)
        key_tile = w_qkv_t[:, 1300:1300 + 2 * TG].rearrange("p (k t) -> p k t", k=2)
        chain_m = ohf[0:HEADS, 0:4 * P].rearrange("h (m p) -> h m p", m=4)
        tails = ohf[0:HEADS, 4 * P:8 * P].rearrange("h (m p) -> h m p", m=4)
        qkv_out = ohf[:, 0:6 * D].rearrange("p (k f) -> p k f", k=2)
        xst = prod[:, :, :, :].rearrange("p a b d -> p (a b d)").rearrange("p (k c n) -> p k c n", k=4, c=FC)[:, 0:2, :, :]
        oh_lo = prod[:, :, :, :].rearrange("p a b d -> p (a b d)").bitcast(BF16).rearrange("p (k t n) -> p k t n", k=2, t=TG)
        hf = h_rows[:, :, :].rearrange("p b d -> p (b d)")
        score = hf[:, 0:NT * HEADS]
        s_run = r_rows[:, :, :].rearrange("p b d -> p (b d)")[:, 0:PJ * HEADS].rearrange("p (j h) -> p j h", h=HEADS)
        m_run = hf[:, 0:PJ * HEADS].rearrange("p (j h) -> p j h", h=HEADS)
        b_run = accf[:, 0:PJ * HEADS].rearrange("p (j h) -> p j h", h=HEADS)
        dst_run_i = accf[:, PJ * HEADS:PJ * HEADS + PJ].bitcast(I32)
        dst_run = accf[:, PJ * HEADS + PJ:PJ * HEADS + 2 * PJ]
        mask_f = accf[:, PJ * HEADS + 2 * PJ:PJ * HEADS + 3 * PJ]
        mask_b = accf[:, PJ * HEADS + 3 * PJ:PJ * HEADS + 4 * PJ]
        gathf = gath[:, :, :, :].rearrange("p k t f -> p (k t f)")
        v_slot = gathf[:, 0:2 * TG * D].rearrange("p (k t f) -> p k t f", k=2, t=TG)
        expo = gathf[:, 2 * TG * D:2 * TG * D + NT * HEADS].rearrange("p (t h) -> p t h", h=HEADS)

        upper = gathf[:, 2 * TG * D:4 * TG * D]
        oh_key = upper[:, 0:ST * SC // 2].bitcast(BF16).rearrange("p (t n) -> p t n", t=ST)
        oh_src = upper[:, ST * SC // 2:ST * SC // 2 + ST * P // 2].bitcast(BF16).rearrange("p (t n) -> p t n", t=ST)
        edge_i = upper[:, 0:2 * NT].bitcast(I32).rearrange("p (k t) -> p k t", k=2)
        edge_t = upper[:, 2 * NT:4 * NT].bitcast(I32).rearrange("p (k t) -> p k t", k=2)
        last_i = gathf[:, 2 * NT:3 * NT].bitcast(I32)
        last_lt = gathf[:, 3 * NT:4 * NT]
        gathb = gathf.bitcast(BF16)
        hfb = hf.bitcast(BF16)
        accb = accf.bitcast(BF16)

        def parts_of(hi_mid, lo):
            v = [hi_mid[:, 0:NB * D], hi_mid[:, NB * D:2 * NB * D], lo]
            return [t.rearrange("p (b f) -> p b f", b=NB) for t in v]

        parts = [parts_of(accb, gathb[:, 0:NB * D]), parts_of(hfb, gathb[:, NB * D:2 * NB * D])]

        banks = ctx.enter_context(nc.psum_tensor("banks", [P, 8, 512], F32))
        B_ROWS, B_TURN = 6, 7

        loaded = sem("loaded")
        b2_loaded = sem("b2_loaded")
        gath_done = [[sem(f"gath_done{k}{half}") for half in range(2)] for k in range(2)]
        v_back = [sem(f"v_back{k}") for k in range(2)]
        idx_ready = sem("idx_ready")
        pool_step = sem("pool_step")
        consts_done = sem("consts_done")
        link_sem = sem("link_sem")
        setup_done = sem("setup_done")
        phase = sem("phase")
        exps_done = sem("exps_done")
        xt_in = [sem(f"xt_in{k}") for k in range(2)]
        qkv_done = sem("qkv_done")
        qkv_dve = sem("qkv_dve")
        qkv_act = sem("qkv_act")
        qkv_stored = [sem(f"qkv_stored{k}") for k in range(2)]
        qkv_free = sem("qkv_free")
        moved = sem("moved")
        spilled = [sem(f"spilled{k}") for k in range(2)]
        spill_free = sem("spill_free")
        oh_ready = sem("oh_ready")
        msg_ready = sem("msg_ready")
        grp_done = sem("grp_done")
        evac_done = sem("evac_done")
        hist_oh = sem("hist_oh")
        hist_done = sem("hist_done")
        qwin_done = [sem(f"qwin_done{k}") for k in range(2)]
        ef_done = [sem(f"ef_done{k}") for k in range(2)]
        tr_done = sem("tr_done")
        tr_evac = sem("tr_evac")
        hid_done = sem("hid_done")
        hid_evac = sem("hid_evac")
        s_done = sem("s_done")
        s_read = sem("s_read")
        qk_done = sem("qk_done")
        qk_read = sem("qk_read")
        red_done = sem("red_done")
        pe_small = sem("pe_small")
        dve_step = sem("dve_step")
        pe_step = sem("pe_step")
        staged = sem("staged")
        pe_a = sem("pe_a")
        rows_done = sem("rows_done")
        rows_done_sage = sem("rows_done_sage")
        pe_b = sem("pe_b")
        turn_done = sem("turn_done")
        pe_c = sem("pe_c")
        var_done = sem("var_done")
        std_done = sem("std_done")
        deg_done = sem("deg_done")
        dstd_done = sem("dstd_done")
        x_done = sem("x_done")
        blk_done = sem("blk_done")
        tab_ready = sem("tab_ready")
        tab_stored = sem("tab_stored")
        val_stored = sem("val_stored")
        tab_free = sem("tab_free")
        edges_in = sem("edges_in")
        oh_strip = sem("oh_strip")
        key_done = sem("key_done")
        strip_done = sem("strip_done")
        strip_out = sem("strip_out")
        c_stored = sem("c_stored")
        c_free = sem("c_free")
        c_in = [sem(f"c_in{k}") for k in range(2)]
        u_ready = sem("u_ready")
        hi_done = sem("hi_done")
        mid_done = sem("mid_done")
        rest1 = sem("rest1")
        lo_done = sem("lo_done")
        hop_done = sem("hop_done")
        hop_dve = sem("hop_dve")
        hop_act = sem("hop_act")
        norm_ready = sem("norm_ready")
        norm_root = sem("norm_root")
        stored = sem("stored")

        N_LOADS = 24
        STAGES = ["scores", "tails_f", "chain_f", "tails_b", "chain_b", "shifted"]
        PHASE = {name: v + 1 for v, name in enumerate(STAGES)}

        block = ctx.enter_context(nc.Block())

        def hop_no(q):
            return HOPS.index(q)

        def blocks_before(q, only=HOPS):
            return NB * sum(1 for p in only if p < q)

        def gathered(eng, k, half, i, n):
            eng.wait_ge(gath_done[k][half], i * (8 * TG) + 8 * TG * (NG // 2 * n + 1))

        def each_group(eng, body):
            with eng.Fori(0, NG // 2) as i:
                for k in range(2):
                    body(i * 2 + k, k, i)

        def each_block_pair(eng, body):
            with eng.Fori(0, NB // 2) as i:
                for k in range(2):
                    body(i * 2 + k, k, i)
            for b in range(NB // 2 * 2, NB):
                body(b, b % 2, b // 2)

        def store_block(eng, q, b, n):
            done = blocks_before(q, TABLED)
            eng.wait_ge(tab_ready, b + (done + 2))
            if q == PASS_VALUE:
                landed, before = val_stored, 0
                eng.sem_inc(pool_step, 1)
            else:
                landed, before = tab_stored, done - NB
            dst = out if q == PASS_SG3 else table[q + 1]
            eng.dma_start(dst[bass.ds(b * P, n), :], tab_row[0:n, :]).then_inc(landed, 16)
            eng.wait_ge(landed, b * 16 + (16 * before + 16))
            eng.sem_inc(tab_free, 1)

        def odd_block_pairs(eng, t0, body):
            with eng.Fori(0, NB // 2) as i:
                for k in range(2):
                    body(i * 2 + k, (t0 + k) % 2, i)
            for b in range(NB // 2 * 2, NB):
                body(b, (t0 + b) % 2, b // 2)

        @block.sync
        def _(sp):
            sp.sem_inc(qkv_free, 2)
            sp.sem_inc(spill_free, 2)
            sp.sem_inc(tab_free, 1)
            sp.sem_inc(c_free, 1)

            def w_view(t):
                return t.rearrange("(c p) f -> p c f", p=P)

            loads = [
                (w_qkv[:, :, 0:D], w_view(a["Wq"])), (w_qkv[:, :, D:2 * D], w_view(a["Wk"])),
                (w_qkv[:, :, 2 * D:3 * D], w_view(a["Wv"])),
                (src_i[:, 0:NT], a["src_t"]), (edge_t[:, 0, :], a["src_e"]), (edge_t[:, 1, :], a["dst_e"]),
                (last_i, a["last"].partition_broadcast(P)), (dst_i[:, :], a["dst_t"]), (base_i[:, :], a["base"].partition_broadcast(P)),
                (w1[:, :], a["W1"]), (b1c[:, :], a["b1_t"]), (w2[:, :, :], w_view(a["W2"])),
                (ends_i[:, :, :], a["ends"].partition_broadcast(HEADS)),
                (ew[:, :], a["ew_t"]), (ew1[:, :], a["ew1_t"]),
                (w_lin[:, 0, :, :], w_view(a["Wo"])), (w_lin[:, 1, :, :], w_view(a["L1_Wt"])),
                (w_lin[:, 2, :, :], w_view(a["L2_Wt"][0:D, :])), (w_lin[:, 3, :, :], w_view(a["L2_Wt"][D:2 * D, :])),
                (w_lin[:, 4, :, :], w_view(a["L3_W"])),
                (bias[:, 0, :], a["bo"].partition_broadcast(P)), (bias[:, 1, :], a["L1_b"].partition_broadcast(P)),
                (bias[:, 2, :], a["L2_b"].partition_broadcast(P)), (bias[:, 3, :], a["L3_b"].partition_broadcast(P)),
            ]
            assert len(loads) == N_LOADS
            for dst, src in loads:
                sp.dma_start(dst, src).then_inc(loaded, 16)
            sp.dma_start(b2b[:, :], a["b2"].partition_broadcast(P)).then_inc(b2_loaded, 16)

            def store_qkv(b, k, i):
                sp.wait_ge(qkv_dve, b + 3)
                sp.dma_start(q_table[bass.ds(b * P, P), :], qkv_out[:, k, 0:D]).then_inc(qkv_stored[k], 16)
                sp.wait_ge(qkv_act, b + 3)
                sp.dma_start(kv_table[bass.ds(b * P, P), :], qkv_out[:, k, D:3 * D]).then_inc(qkv_stored[k], 16)
                sp.wait_ge(qkv_stored[k], i * 32 + 32)
                sp.sem_inc(qkv_free, 1)

            def load_xt(b, k):
                sp.wait_ge(qkv_done, b + 1)
                sp.dma_start(xst[:, k, :, :], a["x_t"].rearrange("(c p) n -> p c n", p=P)[:, :, bass.ds(b * P, P)]
                             ).then_inc(xt_in[k], 16)

            load_xt(0, 0)
            load_xt(1, 1)
            with sp.Fori(0, NB // 2 - 1) as i:
                for k in range(2):
                    store_qkv(i * 2 + k, k, i)
                    load_xt(i * 2 + k + 2, k)
            for b in range(NB // 2 * 2 - 2, NB):
                store_qkv(b, b % 2, b // 2)
                if b + 2 < NB:
                    load_xt(b + 2, b % 2)
            sp.dma_start(x_rows[:, :, :], a["x"].rearrange("(b p) f -> p b f", p=P)).then_inc(b2_loaded, 16)

            def score_io(g, k, i):
                first = sp.value_load(base_i[0:1, bass.ds(g, 1)], min_val=0, max_val=NP - P)
                sp.wait_ge(qk_done, g * 4 + 4)
                sp.dma_start(q_win[:, k, :], q_table[bass.ds(first, P), :]).then_inc(qwin_done[k], 16)
                sp.wait_ge(hid_done, g * 4 + 4)
                sp.dma_start(ef[:, k, :], a["ef_t"][:, bass.ds(g * EG, EG)]).then_inc(ef_done[k], 16)
                gathered(sp, k, 0, i, 0)
                gathered(sp, k, 1, i, 0)
                sp.dma_start(v_spill[bass.ds(g, 1), :, :, :].rearrange("a p t f -> p (a t) f"), gath[:, k, :, D:2 * D]
                             ).then_inc(spilled[k], 16)
                sp.wait_ge(spilled[k], i * 16 + 16)
                sp.sem_inc(spill_free, 1)

            each_group(sp, score_io)

            sp.wait_ge(phase, PHASE["scores"])
            sp.dma_start(score_dram.rearrange("(g p i) h -> p g (i h)", g=NG, p=P),
                         score.rearrange("p (g x) -> p g x", g=NG)).then_inc(moved, 16)
            sp.dma_start(dst_run_i, a["dst_run"]).then_inc(moved, 16)
            sp.wait_ge(moved, 32)
            sp.dma_start(s_run, score_dram.rearrange("(p j) h -> p j h", p=P)).then_inc(moved, 16)
            sp.wait_ge(exps_done, 1)
            sp.dma_start(exp_dram.rearrange("(p j) h -> p j h", p=P), s_run).then_inc(moved, 16)
            sp.wait_ge(moved, 64)
            sp.dma_start(expo.rearrange("p (g t) h -> p g (t h)", g=NG),
                         exp_dram.rearrange("(g p i) h -> p g (i h)", g=NG, p=P)).then_inc(moved, 16)

            def load_v(g, k, i):
                sp.wait_ge(grp_done, g + 1)
                sp.dma_start(v_slot[:, k, :, :], v_spill[bass.ds(g, 1), :, :, :].rearrange("a p t f -> p (a t) f")
                             ).then_inc(v_back[k], 16)

            sp.wait_ge(phase, PHASE["shifted"])
            sp.wait_ge(spill_free, NG + 2)
            each_group(sp, load_v)
            sp.wait_ge(grp_done, NG + 2)
            sp.dma_start(edge_i[:, 0, :], a["src_e"]).then_inc(edges_in, 16)
            sp.dma_start(edge_i[:, 1, :], a["dst_e"]).then_inc(edges_in, 16)

            def store_table(q, b):
                store_block(sp, q, b, P)

            with sp.Fori(0, NB) as b:
                store_table(PASS_GCN1, b)

            def store_counts(q, m):
                n = BUILDS.index(q) * (NG // 4)
                sp.wait_ge(strip_out, m * PER_BLOCK + (PER_BLOCK * (n + 1) + 1))
                sp.dma_start(counts[bass.ds(m + n, 1), :, :, :].rearrange("a p c n -> p (a c) n"), c_build).then_inc(c_stored, 16)
                sp.wait_ge(c_stored, m * 16 + (16 * n + 16))
                sp.sem_inc(c_free, 1)

            for q in BUILDS:
                tabled = q in TABLED
                store_counts(q, 0)
                store_counts(q, 1)
                if tabled:
                    store_table(q, 0)
                with sp.Fori(2, NG // 4) as m:
                    if tabled:
                        store_table(q, m * 2 - 3)
                    store_counts(q, m)
                    if tabled:
                        store_table(q, m * 2 - 2)
                if tabled:
                    for b in range(NG // 2 - 3, NB):
                        store_table(q, b)

            def load_nth(t, k, b):
                if not isinstance(t, int) or t >= 2:
                    sp.wait_ge(hop_done, t - 1)
                sp.dma_start(c_slot[:, k, :, :], counts[bass.ds(b, 1), :, :, :].rearrange("a p c n -> p (a c) n")
                             ).then_inc(c_in[k], 16)

            for n in range(len(COUNTED)):
                t0 = NB * n
                if n < 2:
                    first_pair = 0
                    if n == 0:
                        load_nth(0, 0, 0)
                        load_nth(1, 1, 1)
                        first_pair = 1
                    with sp.Fori(first_pair, NB // 2) as i:
                        for k in range(2):
                            load_nth(i * 2 + (k + t0), (t0 + k) % 2, i * 2 + k)
                    load_nth(t0 + NB - 1, (t0 + NB - 1) % 2, NB - 1)
                else:
                    load_nth(t0, t0 % 2, 0)
                    load_nth(t0 + 1, (t0 + 1) % 2, 1)
                    with sp.Fori(0, NB // 2 - 1) as i:
                        for k in range(2):
                            load_nth(i * 2 + (k + t0 + 2), (t0 + k) % 2, i * 2 + (k + 2))
                            store_block(sp, PASS_SG3, i * 2 + k, P)
                    store_block(sp, PASS_SG3, NB - 3, P)
                    load_nth(t0 + NB - 1, (t0 + NB - 1) % 2, NB - 1)
                    store_block(sp, PASS_SG3, NB - 2, P)
                    store_block(sp, PASS_SG3, NB - 1, N - (NB - 1) * P)

        @block.gpsimd
        def _(pool):
            pool.iota(iota_i[:, :], pattern=[[1, P]], base=0, channel_multiplier=0).then_inc(consts_done, 1)
            pool.iota(part_i[:, :], pattern=[[1, 1]], base=0, channel_multiplier=1).then_inc(consts_done, 1)
            pool.wait_ge(loaded, 16 * N_LOADS)

            pool.memset(src_i[:, NT:NT + 2 * TG], 0).then_inc(consts_done, 1)
            pool.wait_ge(consts_done, 3)

            for n, q in enumerate([PASS_SCORE] + GATHERED):
                if q == PASS_SCORE:
                    pool.wait_ge(qkv_free, NB + 2)
                else:
                    pool.wait_ge(tab_free, blocks_before(q, TABLED) + 1)
                width = 2 * D if q == PASS_SCORE else D
                copies = 1 + NG // 2

                def gather(g, j, m):
                    k = m % 2
                    if q == PASS_SCORE:
                        pool.wait_ge(spill_free, g + 1)
                    else:
                        pool.wait_ge(grp_done, g + (NG * SUMMED.index(q) + 1))
                    if k == 1:
                        pool.sem_inc(pool_step, 1)
                        pool.tensor_copy(idx_slot[:, (m + 1) // 2 % 2, :], src_i[:, bass.ds((g + 1) * TG, 2 * TG)]
                                         ).then_inc(idx_ready, 1)
                    else:
                        pool.wait_ge(idx_ready, j * 2 + (m // 2 + 1 + copies * n))
                        pool.sem_inc(pool_step, 1)
                    for t in range(TG):
                        if q == PASS_SCORE and t % 2 == 0:
                            pool.wait_ge(qk_read, g * 4 + (t // 2 + 1))
                            pool.sem_inc(pool_step, 1)
                        dst = gath[:, k, t, :] if q == PASS_SCORE else v_slot[:, k, t, :]
                        pool.indirect_dma_start(dst, None, kv_table if q == PASS_SCORE else table[q],
                                                bass.IndirectOffsetOnAxis(idx_slot[:, m // 2, k * TG + t:k * TG + t + 1], 0)
                                                ).then_inc(gath_done[k][t // (TG // 2)], 16)

                if n:
                    pool.wait_ge(idx_ready, copies * n)
                    pool.wait_ge(grp_done, NG * SUMMED.index(q) + 2)
                    pool.wait_ge(gath_done[0][0], 8 * TG * (NG // 2) * n)
                pool.tensor_copy(idx_slot[:, 0, :], src_i[:, 0:2 * TG]).then_inc(idx_ready, 1)
                with pool.Fori(0, NG // 4) as j:
                    for m in range(4):
                        gather(j * 4 + m, j, m)
                if q == PASS_SCORE:
                    with pool.Fori(0, NB) as b:
                        store_block(pool, PASS_VALUE, b, P)

        @block.scalar
        def _(act):
            act.sem_inc(hid_evac, 8)
            act.sem_inc(tr_evac, 4)
            act.sem_inc(tab_ready, 1)
            act.sem_inc(strip_out, 1)
            act.sem_inc(hop_act, 2)
            act.sem_inc(qkv_act, 2)

            def copy_v(b, k, i):
                act.wait_ge(qkv_done, b + 3)
                act.wait_ge(qkv_free, b + 1)
                nc.scalar.activation(qkv_out[:, k, 2 * D:3 * D], banks[:, 3 * k + 2, 0:D], ACT.Copy).then_inc(qkv_act, 1)

            each_block_pair(act, copy_v)

            def score_copies(g, k, i):
                for half in range(2):
                    act.wait_ge(tr_done, g * 2 + (half + 5))
                    act.wait_ge(qk_done, g * 4 + 4)
                    nc.scalar.activation(oht[:, k, half * 512:half * 512 + 512], banks[:, half, :], ACT.Copy
                                         ).then_inc(tr_evac, 1)
                for u in range(4):
                    half, c = u // 2, u % 2
                    act.wait_ge(hid_done, g * 4 + (u + 9))
                    act.wait_ge(s_done, g * 2 + (half + 1))
                    nc.scalar.activation(hid[:, u, :], banks[:, 2 + u % 2, :], ACT.Relu, bias=b1c[:, c:c + 1]
                                         ).then_inc(hid_evac, 1)

            each_group(act, score_copies)
            act.wait_ge(phase, PHASE["shifted"])
            nc.scalar.activation(s_run, s_run, ACT.Exp).then_inc(exps_done, 1)

            def root(dst, src, done, biased=False):
                if biased:
                    nc.scalar.activation(dst, src, ACT.Sqrt, bias=eps[:, :]).then_inc(done, 1)
                else:
                    nc.scalar.activation(dst, src, ACT.Sqrt).then_inc(done, 1)

            def scale(j, b):
                return node[:, j, bass.ds(b, 1)]

            def x_block(b):
                return x_rows[:, bass.ds(b, 1), :].rearrange("p a d -> p (a d)")

            def stage_block(q, b):
                done = blocks_before(q)
                groups = min(2 * (b + LAG), NG) if isinstance(b, int) else b * 2 + 2 * LAG
                act.wait_ge(evac_done, groups + (NG * hop_no(q) + 2))
                act.wait_ge(pe_a, b + (done + 1))
                if q == PASS_VALUE:
                    nc.scalar.activation(den_stage[:, :], den[:, bass.ds(b * P, P)], ACT.Copy)
                if q == PASS_SAGE:
                    nc.scalar.activation(x_stage[:, :].unsqueeze(1), x_rows[:, bass.ds(b, 1), :], ACT.Copy)
                nc.scalar.activation(stage[:, :, :], acc[:, :, bass.ds(b * P, P)], ACT.Copy).then_inc(staged, 1)
                if q == PASS_VALUE:
                    act.wait_ge(deg_done, b + 1)
                    root(dstd[:, :], blk_sc[:, 16:17], dstd_done)

            def turn_block(q, b):
                if q in DENSE:
                    bank_sem = pe_a if q == PASS_SAGE else pe_b
                    before = blocks_before(q) + 1 if q == PASS_SAGE else blocks_before(q, TURNED)
                    act.wait_ge(bank_sem, b + (before + 1))
                    nc.scalar.activation(turned[:, :, :], banks[:, B_TURN, 0:D].rearrange("p (c n) -> p c n", c=FC), ACT.Copy
                                         ).then_inc(turn_done, 1)

            def finish_block(q, b):
                if q in DENSE:
                    act.wait_ge(var_done, b + (blocks_before(q, DENSE) + 1))
                    root(std[:, :], mv[:, 1:2], std_done, biased=True)
                if q == PASS_SAGE:
                    act.wait_ge(x_done, b + (blocks_before(q, SUMMED) + 1))
                    nc.scalar.activation(h_rows[:, bass.ds(b, 1), :].rearrange("p a d -> p (a d)"), x_block(b), ACT.Copy,
                                         scale=scale(NORM, b)).then_inc(u_ready, 1)
                    return
                act.wait_ge(tab_free, b + (blocks_before(q, TABLED) + 1))
                act.wait_ge(x_done, b + (blocks_before(q, SUMMED) + 1))
                if q == PASS_VALUE:
                    nc.scalar.activation(tab_row[:, :], x_block(b), ACT.Copy, scale=scale(DINV, b)).then_inc(tab_ready, 1)
                elif q == PASS_GCN1:
                    nc.scalar.activation(tab_row[:, :], rows[:, :], ACT.Copy, scale=scale(DINV, b)).then_inc(tab_ready, 1)
                else:
                    nc.scalar.activation(tab_row[:, :], x_block(b), ACT.Copy).then_inc(tab_ready, 1)

            def strip_copy(q, i, k):
                n = BUILDS.index(q) * NG
                act.wait_ge(strip_done, i * 2 + (n + k + 2))
                act.wait_ge(c_free, i // 2 + (BUILDS.index(q) * (NG // 4) + 1))
                at = i % 2 * (2 * SW) + k * SW
                nc.scalar.activation(c_build[:, 0:SPLIT_BANK, bass.ds(at, SW)],
                                     banks[:, 2, :].rearrange("p (c n) -> p c n", n=SW), ACT.Copy)
                nc.scalar.activation(c_build[:, SPLIT_BANK:NB, bass.ds(at, SW)],
                                     banks[:, 5, 0:SC - 512].rearrange("p (c n) -> p c n", n=SW), ACT.Copy).then_inc(strip_out, 1)

            for q in SUMMED:
                if q in BUILDS:
                    with act.Fori(0, LAG) as i:
                        for k in range(2):
                            strip_copy(q, i, k)
                with act.Fori(LAG, NG // 2) as i:
                    stage_block(q, i - LAG)
                    if q in BUILDS:
                        strip_copy(q, i, 0)
                    turn_block(q, i - LAG)
                    if q in BUILDS:
                        strip_copy(q, i, 1)
                    finish_block(q, i - LAG)
                for b in range(LOOPED, NB):
                    stage_block(q, b)
                    turn_block(q, b)
                    finish_block(q, b)
                if q == PASS_GCN1:
                    act.wait_ge(norm_ready, 1)
                    root(node[:, NORM2, :], node[:, OUTDEG, :], norm_root)

            def split(stage_no, b, src, to, factor=None):
                hi, mid, _ = parts[to]
                n = stage_no * NB
                kw = {} if factor is None else {"scale": factor}
                if factor is not None:
                    act.wait_ge(lo_done, b + n)
                    nc.scalar.activation(tab_row[:, :], src, ACT.Copy, **kw)
                nc.scalar.activation(hi[:, bass.ds(b, 1), :].rearrange("p a d -> p (a d)"), src, ACT.Copy, **kw).then_inc(hi_done, 1)

            def middle(stage_no, b, to, rest):
                act.wait_ge(rest1, b + (stage_no * NB + 1))
                nc.scalar.activation(parts[to][1][:, bass.ds(b, 1), :].rearrange("p a d -> p (a d)"), rest, ACT.Copy
                                     ).then_inc(mid_done, 1)

            act.wait_ge(evac_done, NG * len(SUMMED) + 2)
            act.wait_ge(u_ready, NB)
            act.wait_ge(staged, NB * len(SUMMED))
            act.wait_ge(pe_a, NB * len(SUMMED) + 1)

            def h_block(b):
                return h_rows[:, bass.ds(b, 1), :].rearrange("p a d -> p (a d)")

            split(0, 0, h_block(0), 0)
            with act.Fori(0, NB - 1) as b:
                split(0, b + 1, h_block(b + 1), 0)
                middle(0, b, 0, h_block(b))
            middle(0, NB - 1, 0, h_block(NB - 1))
            for n, q in enumerate(COUNTED):
                if q != PASS_SG3:
                    def hop_split(b, slot, i):
                        act.wait_ge(hop_done, b + (NB * n + 1))
                        split(n + 1, b, banks[:, slot, 0:D], (n + 1) % 2, scale(NORM2, b))
                        act.wait_ge(hi_done, b + (NB * (n + 1) + 1))
                        act.sem_inc(hop_act, 1)
                        middle(n + 1, b, (n + 1) % 2, ysum[:, :])

                    odd_block_pairs(act, NB * n, hop_split)
                else:
                    with act.Fori(0, NB) as b:
                        turn_block(q, b)
                        finish_block(q, b)

        @block.tensor
        def _(pe):
            for s, n in ((qkv_done, 2), (grp_done, 2), (hist_done, 2), (qk_done, 8), (hid_done, 8), (tr_done, 4), (s_done, 2),
                         (pe_a, 1), (strip_done, 1)):
                pe.sem_inc(s, n)
            pe.wait_ge(setup_done, 1)
            nc.tensor.transpose(banks[0:1, 7, 0:P], part_f[:, :], ident[:, :]).then_inc(pe_small, 1)

            def qkv(b, k, i):
                pe.wait_ge(xt_in[k], i * 16 + 16)
                pe.wait_ge(qkv_dve, b + 1)
                pe.wait_ge(qkv_act, b + 1)
                for n in range(3):
                    for c in range(FC):
                        last = nc.tensor.matmul(banks[:, 3 * k + n, 0:D], xst[:, k, c, :], w_qkv[:, c, n * D:(n + 1) * D],
                                                start=(c == 0), stop=(c == FC - 1))
                last.then_inc(qkv_done, 1)

            each_block_pair(pe, qkv)
            pe.wait_ge(qkv_dve, NB + 2)
            pe.wait_ge(qkv_act, NB + 2)

            def scores(g, k, i):
                pe.wait_ge(oh_ready, g + 1)
                for half in range(2):
                    pe.wait_ge(tr_evac, g * 2 + (half + 3))
                    for t in range(4):
                        last = nc.tensor.transpose(banks[:, half, t * P:(t + 1) * P], onehot[:, k, half * 4 + t, :], ident[:, :])
                    last.then_inc(tr_done, 1)
                pe.wait_ge(ef_done[k], i * 16 + 16)
                for half in range(2):
                    for c in range(2):
                        u = half * 2 + c
                        pe.wait_ge(hid_evac, g * 4 + (u + 7))
                        nc.tensor.matmul(banks[:, 2 + u % 2, :], w1[:, c * P:(c + 1) * P],
                                         ef[:, k, half * 512:half * 512 + 512], start=True, stop=True).then_inc(hid_done, 1)
                pe.wait_ge(s_read, g + 1)
                for half in range(2):
                    pe.wait_ge(hid_evac, g * 4 + (half * 2 + 10))
                    for t in range(4):
                        for c in range(2):
                            col = (half * 4 + t) * HEADS
                            last = nc.tensor.matmul(banks[:, 6, col:col + HEADS], hid[:, half * 2 + c, t * P:(t + 1) * P],
                                                    w2[:, c, :], start=(c == 0), stop=(c == 1))
                    last.then_inc(s_done, 1)
                pe.wait_ge(qwin_done[k], i * 16 + 16)
                for pair in range(4):
                    pe.wait_ge(tr_evac, g * 2 + (pair // 2 + 5))
                    pe.wait_ge(qk_read, g * 4 + (pair + 7))
                    for t in range(2):
                        tile = pair * 2 + t
                        last = nc.tensor.matmul(banks[:, 4 + pair % 2, t * D:(t + 1) * D], oht[:, k, tile * P:(tile + 1) * P],
                                                q_win[:, k, :], start=True, stop=True)
                    last.then_inc(qk_done, 1)

            each_group(pe, scores)

            for n in range(2):
                pe.wait_ge(phase, PHASE["tails_f" if n == 0 else "tails_b"])
                nc.tensor.transpose(banks[0:HEADS, 7, 0:P], carry[:, 2 * n, :], ident[:, :]).then_inc(pe_small, 1)
                pe.wait_ge(phase, PHASE["chain_f" if n == 0 else "chain_b"])
                nc.tensor.transpose(banks[:, 7, P:P + HEADS], tails[:, 2 * n + 1, :], ident[0:HEADS, 0:HEADS]).then_inc(pe_small, 1)

            def group_sums(q, g, k, i):
                h = hop_no(q)
                pe.wait_ge(oh_ready, g + (NG * q + 1))
                if q == PASS_VALUE:
                    pe.wait_ge(msg_ready, g + 1)
                else:
                    gathered(pe, k, 0, i, GATHERED.index(q) + 1)
                    gathered(pe, k, 1, i, GATHERED.index(q) + 1)
                pe.wait_ge(evac_done, g + (NG * h + 1))
                for t in range(TG):
                    for c in range(FC):
                        if q == PASS_VALUE:
                            message = v_slot[:, k, t, c * P:(c + 1) * P]
                        else:
                            message = v_slot[:, k, t, c * P:(c + 1) * P]
                        last = nc.tensor.matmul(banks[:, 3 * k + c, 0:P], message, onehot[:, k, t, :],
                                                start=(t == 0), stop=(t == TG - 1))
                    if q == PASS_VALUE:
                        last = nc.tensor.matmul(banks[0:XW, 3 * k + 2, 0:P], xcol[:, k, t, :], onehot[:, k, t, :],
                                                start=(t == 0), stop=(t == TG - 1))
                last.then_inc(grp_done, 1)
                if q == PASS_GCN1:
                    pe.wait_ge(hist_oh, g + 1)
                    for t in range(TG):
                        last = nc.tensor.matmul(banks[:, 2, 0:32], oh_lo[:, k, t, :], oh_hi[:, k, t, :], start=False, stop=False,
                                                skip_group_check=True)
                    last.then_inc(hist_done, 1)

            def turn_rows(q, b):
                done = blocks_before(q)
                pe.wait_ge(staged, b + (done + 1))
                pe.wait_ge(blk_done, b + (done + 1))
                if q == PASS_VALUE:
                    pe.sem_inc(pe_step, 1)
                    nc.tensor.transpose(banks[:, B_ROWS, D:D + XW], den_stage[:, :], ident[0:XW, 0:XW])
                for c in range(FC):
                    if q == PASS_SAGE:
                        nc.tensor.transpose(banks[:, B_TURN, c * P:(c + 1) * P], x_stage[:, c * P:(c + 1) * P], ident[:, :])
                for c in range(FC):
                    if q == PASS_SAGE:
                        last = nc.tensor.matmul(banks[:, B_ROWS, 0:D], stage[:, c, :], w_lin[:, 2, c, :],
                                                start=(c == 0), stop=(c == FC - 1))
                    else:
                        last = nc.tensor.transpose(banks[:, B_ROWS, c * P:(c + 1) * P], stage[:, c, :], ident[:, :])
                last.then_inc(pe_a, 1)

            def turn_back(q, b):
                if q in TURNED:
                    pe.wait_ge(rows_done, b + (blocks_before(q, TURNED) + 1))
                    for c in range(FC):
                        last = nc.tensor.transpose(banks[:, B_TURN, c * P:(c + 1) * P], rows[:, c * P:(c + 1) * P], ident[:, :])
                    last.then_inc(pe_b, 1)

            def product(q, b):
                if q in DENSE:
                    pe.wait_ge(turn_done, b + (blocks_before(q, DENSE) + 1))
                    if q == PASS_SAGE:
                        pe.wait_ge(rows_done_sage, b + 1)
                    for c in range(FC):
                        last = nc.tensor.matmul(banks[:, B_ROWS, 0:D], turned[:, c, :], w_lin[:, DENSE[q], c, :],
                                                start=(c == 0), stop=(c == FC - 1))
                    last.then_inc(pe_c, 1)

            def strip(q, i, k):
                n = BUILDS.index(q) * NG
                pe.wait_ge(oh_strip, i * 2 + (n + k + 1))
                pe.wait_ge(strip_out, i * 2 + (n + k + 1))
                for t in range(ST):
                    nc.tensor.matmul(banks[:, 2, :], oh_src[:, t, :], oh_key[:, t, 0:512], start=(t == 0), stop=(t == ST - 1))
                    last = nc.tensor.matmul(banks[:, 5, 0:SC - 512], oh_src[:, t, :], oh_key[:, t, 512:SC],
                                            start=(t == 0), stop=(t == ST - 1))
                last.then_inc(strip_done, 1)

            for q in SUMMED:
                if q == PASS_GCN1:
                    nc.tensor.matmul(banks[:, 2, 0:32], zero_b[:, :], zero_b[:, 0:32], start=True, stop=False)
                with pe.Fori(0, LAG) as i:
                    for k in range(2):
                        group_sums(q, i * 2 + k, k, i)
                        if q in BUILDS:
                            strip(q, i, k)
                with pe.Fori(LAG, NG // 2) as i:
                    turn_rows(q, i - LAG)
                    group_sums(q, i * 2, 0, i)
                    if q in BUILDS:
                        strip(q, i, 0)
                    turn_back(q, i - LAG)
                    group_sums(q, i * 2 + 1, 1, i)
                    product(q, i - LAG)
                    if q in BUILDS:
                        strip(q, i, 1)
                if q == PASS_GCN1:
                    nc.tensor.matmul(banks[:, 2, 0:32], zero_b[:, :], zero_b[:, 0:32], start=False, stop=True
                                     ).then_inc(hist_done, 1)
                for b in range(LOOPED, NB):
                    turn_rows(q, b)
                    turn_back(q, b)
                    product(q, b)

            for n, q in enumerate(COUNTED):
                def counted(b, slot, i, first):
                    t = NB * n
                    pe.wait_ge(c_in[slot], (i * 16 + (t // 2 * 16 + 16)) if slot == t % 2 or t % 2 == 0 else (i * 16 + (t // 2 * 16 + 32)))
                    pe.wait_ge(hop_dve, b + (t + 1))
                    if q != PASS_SG3:
                        pe.wait_ge(hop_act, b + (t + 1))
                    else:
                        pe.wait_ge(hop_act, 2 * NB + 2)

                    for c in range(NB):
                        if first:
                            pe.wait_ge(lo_done, NB * n + c + 1)
                        for j in range(3):
                            last = nc.tensor.matmul(banks[:, slot, 0:D], c_slot[:, slot, c, :], parts[n % 2][j][:, c, :],
                                                    start=(c == 0 and j == 0), stop=(c == NB - 1 and j == 2))
                    last.then_inc(hop_done, 1)

                counted(0, (NB * n) % 2, 0, True)
                if q == PASS_SG3:
                    counted(1, (NB * n + 1) % 2, 0, False)
                    turn_back(q, 0)
                    product(q, 0)
                else:
                    counted(1, (NB * n + 1) % 2, 0, False)
                with pe.Fori(1, NB // 2) as i:
                    for k in range(2):
                        counted(i * 2 + k, (NB * n + k) % 2, i, False)
                        if q == PASS_SG3:
                            turn_back(q, i * 2 + (k - 1))
                            product(q, i * 2 + (k - 1))
                counted(NB - 1, (NB * n) % 2, NB // 2, False)
                if q == PASS_SG3:
                    for b in (NB - 2, NB - 1):
                        turn_back(q, b)
                        product(q, b)

        @block.vector
        def _(dve):
            class Chain:
                def __init__(self):
                    self.total, self.at, self.n = 0, 0, 0

                def link(self, ins):
                    self.n += 1
                    ins.then_inc(link_sem, 1)
                    dve.wait_ge(link_sem, self.at + self.n)

                def enter(self, at):
                    self.at, self.n = at, 0

                def leave(self):
                    n, self.n = self.n, 0
                    return n

            def chain_total(c):
                c.enter(c.at + c.n)
                return c.at

            LINKS = {PASS_VALUE: 12, PASS_GCN1: 0, PASS_GCN2: 5, PASS_SAGE: 4, PASS_SG1: 0, PASS_SG2: 0, PASS_SG3: 4}
            chain = Chain()
            link = chain.link

            def advance(name):
                dve.wait_ge(phase, PHASE[name])

            for s, n in ((qkv_dve, 2), (evac_done, 2), (qk_read, 8), (s_read, 1), (red_done, 8), (blk_done, 1), (hop_dve, 2)):
                dve.sem_inc(s, n)
            dve.wait_ge(consts_done, 2)
            dve.wait_ge(loaded, 16 * N_LOADS)
            nc.vector.memset(zero_b[:, :], 0.0)
            nc.vector.memset(eps[:, :], EPS)
            nc.vector.memset(xcol[:, :, :, HEADS:HEADS + 1], 1.0)
            nc.vector.tensor_copy(part_f[:, :], part_i[:, :])
            link(nc.vector.tensor_copy(iota_f[:, :], iota_i[:, :]))
            nc.vector.tensor_scalar(ident[:, :], iota_f[:, :], part_f[:, :], None, ALU.is_equal)
            nc.vector.tensor_tensor(rel[:, :, :], dst_i[:, :].rearrange("p (g t) -> p g t", g=NG),
                                    base_i[:, :].unsqueeze(2).to_broadcast([P, NG, TG]), ALU.subtract)
            lo_i = gathf[:, 0:NT].bitcast(I32)
            hi_i = gathf[:, NT:2 * NT].bitcast(I32)
            nc.vector.tensor_scalar(lo_i, edge_t[:, 0, :], P - 1, None, ALU.bitwise_and)
            link(nc.vector.tensor_scalar(hi_i, edge_t[:, 0, :], 7, None, ALU.arith_shift_right))
            nc.vector.tensor_copy(src_lo[:, :], lo_i)
            link(nc.vector.tensor_copy(src_hi[:, :], hi_i))
            link(nc.vector.tensor_scalar(part_f[:, :], part_f[:, :], float(SW), None, ALU.mult))
            link(nc.vector.tensor_scalar(last_lt, last_i, part_f[:, :], None, ALU.is_lt))
            link(nc.vector.tensor_reduce(part_f[:, :], last_lt, AX.X, ALU.add))
            link(nc.vector.tensor_scalar(part_f[:, :], part_f[:, :], float(NT - ST), None, ALU.min))
            link(nc.vector.tensor_tensor(bias[:, 3, :], bias[:, 3, :], bias[:, 3, :], ALU.add))
            nc.vector.tensor_tensor(bias[:, 3, :], bias[:, 3, :], bias[:, 3, :], ALU.add).then_inc(setup_done, 1)

            def copy_qk(b, k, i):
                dve.wait_ge(qkv_done, b + 3)
                dve.wait_ge(qkv_free, b + 1)
                nc.vector.tensor_copy(qkv_out[:, k, 0:2 * D].rearrange("p (n f) -> p n f", n=2), banks[:, 3 * k:3 * k + 2, 0:D]
                                      ).then_inc(qkv_dve, 1)

            each_block_pair(dve, copy_qk)
            dve.wait_ge(pe_small, 1)
            link(nc.vector.tensor_copy(tile0_i[:, :], banks[0:1, 7, 0:P]))

            weights = {PASS_GCN1: ew, PASS_GCN2: ew, PASS_SAGE: ew1}

            def make_onehot(q, g, k):
                w = weights.get(q)
                for t in range(TG):
                    r = rel[:, bass.ds(g, 1), t:t + 1].rearrange("p a b -> p (a b)")
                    if w is None:
                        last = nc.vector.tensor_scalar(onehot[:, k, t, :], iota_f[:, :], r, None, ALU.is_equal)
                    else:
                        last = nc.vector.tensor_scalar(onehot[:, k, t, :], iota_f[:, :], r,
                                                       w[:, bass.ds(g * TG + t, 1)], ALU.is_equal, ALU.mult)
                last.then_inc(oh_ready, 1)

            def score_prepare(g, k):
                dve.wait_ge(tr_done, g * 2 + 2)
                make_onehot(PASS_SCORE, g, k)

            def score_finish(g, k, i):
                for pair in range(4):
                    if pair % 2 == 0:
                        gathered(dve, k, pair // 2, i, 0)
                    dve.wait_ge(qk_done, g * 4 + (pair + 9))
                    dve.wait_ge(red_done, g * 4 + (pair + 7))
                    nc.vector.tensor_tensor(prod[:, pair % 2, :, :], banks[:, 4 + pair % 2, :].rearrange("p (t d) -> p t d", t=2),
                                            gath[:, k, 2 * pair:2 * pair + 2, 0:D], ALU.mult).then_inc(qk_read, 1)
                    dve.wait_ge(qk_read, g * 4 + (pair + 9))
                    nc.vector.tensor_reduce(score[:, bass.ds(g * (TG * HEADS) + pair * 2 * HEADS, 2 * HEADS)],
                                            prod[:, pair % 2, :, :].rearrange("p t (h d) -> p (t h) d", h=HEADS),
                                            AX.X, ALU.add).then_inc(red_done, 1)
                dve.wait_ge(red_done, g * 4 + 12)
                dve.wait_ge(s_done, g * 2 + 4)
                part = score[:, bass.ds(g * (TG * HEADS), TG * HEADS)]
                nc.vector.scalar_tensor_tensor(part, part, float(HD) ** -0.5, banks[:, 6, 0:TG * HEADS], ALU.mult, ALU.add
                                               ).then_inc(s_read, 1)

            dve.wait_ge(qkv_free, NB + 2)
            score_prepare(0, 0)
            with dve.Fori(0, NG // 2 - 1) as i:
                for k in range(2):
                    score_prepare(i * 2 + k + 1, 1 - k)
                    score_finish(i * 2 + k, k, i)
            score_prepare(NG - 1, 1)
            score_finish(NG - 2, 0, NG // 2 - 1)
            score_finish(NG - 1, 1, NG // 2 - 1)
            dve.wait_ge(s_read, NG + 1)
            dve.wait_ge(b2_loaded, 32)
            s3 = score.rearrange("p (t h) -> p t h", h=HEADS)
            nc.vector.tensor_tensor(s3, s3, b2b[:, :].unsqueeze(1).to_broadcast([P, NT, HEADS]), ALU.add).then_inc(phase, 1)

            dve.wait_ge(moved, 48)
            first, last_ = ends[:, 0, :], ends[:, 1, :]
            link(nc.vector.tensor_copy(ends[:, :, :], ends_i[:, :, :]))
            link(nc.vector.tensor_copy(dst_run, dst_run_i))

            def to_mask(m):
                link(nc.vector.tensor_scalar(m, m, BIG, -BIG, ALU.mult, ALU.add))

            nc.vector.memset(mask_f[:, 0:1], 1.0)
            link(nc.vector.tensor_tensor(mask_f[:, 1:PJ], dst_run[:, 1:PJ], dst_run[:, 0:PJ - 1], ALU.is_equal))
            to_mask(mask_f)
            nc.vector.tensor_copy(mask_b[:, 0:PJ - 1], mask_f[:, 1:PJ])
            link(nc.vector.memset(mask_b[:, PJ - 1:PJ], 0.0))
            link(nc.vector.memset(chain_m[:, :, :], 0.0))
            nc.vector.tensor_tensor(chain_m[:, 0, :], first, last_, ALU.is_equal)
            link(nc.vector.tensor_tensor(chain_m[:, 1, 1:P], first[:, 1:P], last_[:, 0:P - 1], ALU.is_equal))
            nc.vector.tensor_tensor(chain_m[:, 2, 1:P], chain_m[:, 0, 1:P], chain_m[:, 1, 1:P], ALU.mult)
            link(nc.vector.tensor_tensor(chain_m[:, 3, 0:P - 1], chain_m[:, 0, 0:P - 1], chain_m[:, 1, 1:P], ALU.mult))
            to_mask(chain_m[:, 1:4, :])

            def scan_heads(dst, src, mask, back, initial):
                for h in range(HEADS):
                    d, s, m = dst[:, :, h], src[:, :, h], mask
                    if back:
                        d, s, m = d[:, ::-1], s[:, ::-1], m[:, ::-1]
                    last = nc.vector.tensor_tensor_scan(d, m, s, -BIG if initial is None else initial[:, h:h + 1], ALU.add, ALU.max)
                link(last)

            for n, (dst, src, mask) in enumerate(((m_run, s_run, mask_f), (b_run, m_run, mask_b))):
                scan_heads(dst, src, mask, n == 1, None)
                edge = PJ - 1 if n == 0 else 0
                nc.vector.tensor_copy(carry[:, 2 * n, :], dst[:, edge, :]).then_inc(phase, 1)
                dve.wait_ge(pe_small, 2 * n + 2)
                link(nc.vector.tensor_copy(tails[:, 2 * n, :], banks[0:HEADS, 7, 0:P]))
                run, tl, cm = chain_m[:, 2 + n, :], tails[:, 2 * n, :], tails[:, 2 * n + 1, :]
                if n == 0:
                    link(nc.vector.tensor_tensor_scan(cm, run, tl, -BIG, ALU.add, ALU.max))
                    nc.vector.memset(tl[:, 0:1], -BIG)
                    link(nc.vector.tensor_tensor(tl[:, 1:P], cm[:, 0:P - 1], chain_m[:, 1, 1:P], ALU.add))
                else:
                    link(nc.vector.tensor_tensor_scan(cm[:, ::-1], run[:, ::-1], tl[:, ::-1], -BIG, ALU.add, ALU.max))
                    nc.vector.memset(tl[:, P - 1:P], -BIG)
                    link(nc.vector.tensor_tensor(tl[:, 0:P - 1], cm[:, 1:P], chain_m[:, 1, 1:P], ALU.add))
                nc.vector.tensor_copy(cm, tl).then_inc(phase, 1)
                dve.wait_ge(pe_small, 2 * n + 3)
                link(nc.vector.tensor_copy(carry[:, 2 * n + 1, :], banks[:, 7, P:P + HEADS]))
                scan_heads(dst, src, mask, n == 1, carry[:, 2 * n + 1, :])
            nc.vector.tensor_tensor(s_run, s_run, b_run, ALU.subtract).then_inc(phase, 1)
            dve.wait_ge(phase, PHASE["shifted"])

            def prepare(q, g, k, i):
                dve.wait_ge(grp_done, g + (NG * hop_no(q) + 1))
                make_onehot(q, g, k)
                if q == PASS_VALUE:
                    dve.wait_ge(v_back[k], i * 16 + 16)
                    v = v_slot[:, k, :, :].rearrange("p t (h d) -> p t h d", h=HEADS)
                    e = expo[:, bass.ds(g * TG, TG), :]
                    nc.vector.tensor_tensor(v, v, e.unsqueeze(3).to_broadcast([P, TG, HEADS, HD]), ALU.mult)
                    nc.vector.tensor_copy(xcol[:, k, :, HEADS + 1:XW], ew[:, bass.ds(g * TG, TG)].unsqueeze(2))
                    nc.vector.tensor_copy(xcol[:, k, :, 0:HEADS], e).then_inc(msg_ready, 1)
                if q == PASS_GCN1:
                    dve.wait_ge(hist_done, g + 1)
                    nc.vector.tensor_tensor(oh_hi[:, k, :, :], iota_f[:, 0:32].unsqueeze(1).to_broadcast([P, TG, 32]),
                                            src_hi[:, bass.ds(g * TG, TG)].unsqueeze(2).to_broadcast([P, TG, 32]), ALU.is_equal)
                    nc.vector.tensor_tensor(oh_lo[:, k, :, :], iota_f[:, :].unsqueeze(1).to_broadcast([P, TG, P]),
                                            src_lo[:, bass.ds(g * TG, TG)].unsqueeze(2).to_broadcast([P, TG, P]), ALU.is_equal
                                            ).then_inc(hist_oh, 1)

            def add_sums(q, g, k):
                h = hop_no(q)
                first = dve.value_load(base_i[0:1, bass.ds(g, 1)], min_val=0, max_val=NA - P)
                dve.wait_ge(grp_done, g + (NG * h + 3))
                dve.wait_ge(evac_done, g + (NG * h + 2))
                win = acc[:, :, bass.ds(first, P)]
                if q == PASS_VALUE:
                    dw = den[:, bass.ds(first, P)]
                    nc.vector.tensor_tensor(dw, dw, banks[0:XW, 3 * k + 2, 0:P], ALU.add)
                nc.vector.tensor_tensor(win, win, banks[:, 3 * k:3 * k + 2, 0:P], ALU.add).then_inc(evac_done, 1)

            V = nc.vector

            def row(t, b):
                return t[:, bass.ds(b, 1), :].rearrange("p a d -> p (a d)")

            def rows_step(q, b, slot=None):
                def per_node(j):
                    return node[:, j, bass.ds(b, 1)]

                done = blocks_before(q)
                if slot is None:
                    dve.wait_ge(pe_a, b + (done + 2))
                    ps = banks[:, B_ROWS, 0:D]
                else:
                    dve.wait_ge(hop_done, b + (blocks_before(q, COUNTED) + 1))
                    ps = banks[:, slot, 0:D]
                x_b, r_b, h_b = row(x_rows, b), row(r_rows, b), row(h_rows, b)
                if q == PASS_GCN1:
                    dve.wait_ge(tab_ready, b + (done + 1))
                if q == PASS_VALUE:
                    link(V.tensor_copy(blk_sc[:, 0:XW], banks[:, B_ROWS, D:D + XW]))
                    V.tensor_scalar(blk_sc[:, 10:11], blk_sc[:, 9:10], 1.0, None, ALU.add)
                    V.tensor_scalar(blk_sc[:, 8:9], blk_sc[:, 8:9], 1.0, None, ALU.max)
                    link(V.tensor_scalar(blk_sc[:, 0:HEADS], blk_sc[:, 0:HEADS], 1e-30, None, ALU.max))
                    V.tensor_scalar(blk_sc[:, 11:12], blk_sc[:, 10:11], 0.0, None, ALU.is_gt)
                    V.tensor_scalar(blk_sc[:, 16:17], blk_sc[:, 10:11], 1e-12, None, ALU.max).then_inc(deg_done, 1)
                    V.reciprocal(per_node(RDEG), blk_sc[:, 8:9])
                    link(V.reciprocal(blk_sc[:, 0:HEADS], blk_sc[:, 0:HEADS]))
                    V.tensor_tensor(rows[:, :].rearrange("p (h d) -> p h d", h=HEADS), ps.rearrange("p (h d) -> p h d", h=HEADS),
                                    blk_sc[:, 0:HEADS].unsqueeze(2).to_broadcast([P, HEADS, HD]), ALU.mult).then_inc(rows_done, 1)
                    dve.wait_ge(dstd_done, b + 1)
                    link(V.reciprocal(blk_sc[:, 12:13], dstd[:, :]))
                    link(V.tensor_tensor(per_node(DINV), blk_sc[:, 12:13], blk_sc[:, 11:12], ALU.mult))
                    link(V.tensor_scalar(per_node(HDINV), per_node(DINV), 0.5, None, ALU.mult))
                    link(V.tensor_tensor(per_node(HD2), per_node(HDINV), per_node(DINV), ALU.mult))
                    link(V.tensor_scalar(per_node(HD2P), per_node(HD2), 0.5, None, ALU.add))
                elif q == PASS_GCN1:
                    V.scalar_tensor_tensor(rows[:, :], ps, per_node(HDINV), h_b, ALU.mult, ALU.add).then_inc(x_done, 1)
                    dve.wait_ge(x_done, b + (done + 1))
                    V.scalar_tensor_tensor(h_b, rows[:, :], per_node(HD2), r_b, ALU.mult, ALU.add).then_inc(blk_done, 1)
                elif q == PASS_GCN2:
                    link(V.scalar_tensor_tensor(rows[:, :], ps, per_node(HDINV), h_b, ALU.mult, ALU.add))
                    V.tensor_scalar(rows[:, :], rows[:, :], 0.0, None, ALU.max).then_inc(rows_done, 1)
                elif q == PASS_SAGE:
                    V.scalar_tensor_tensor(rows[:, :], ps, per_node(RDEG), x_b, ALU.mult, ALU.add).then_inc(rows_done_sage, 1)
                elif q in (PASS_SG1, PASS_SG2):
                    V.scalar_tensor_tensor(x_b, ps, per_node(NORM), x_b, ALU.mult, ALU.add).then_inc(hop_dve, 1)
                else:
                    V.scalar_tensor_tensor(rows[:, :], ps, per_node(NORM), x_b, ALU.mult, ALU.add).then_inc(rows_done, 1)
                    dve.wait_ge(rows_done, b + (blocks_before(q, TURNED) + 1))
                    dve.sem_inc(hop_dve, 1)

            def bias_step(q, b):
                x_b = row(x_rows, b)
                if q == PASS_VALUE:
                    link(V.tensor_tensor(pre_b[:, :], x_b, bias[:, 0, :], ALU.add))
                elif q == PASS_GCN2:
                    link(V.tensor_tensor(pre_b[:, :], x_b, bias[:, 1, :], ALU.add))
                elif q == PASS_SAGE:
                    dve.wait_ge(rows_done_sage, b + 1)
                    link(V.tensor_tensor(pre_b[:, :], rows[:, :], bias[:, 2, :], ALU.add))

            def norm_step(q, b):
                if q not in DENSE:
                    return

                def per_node(j):
                    return node[:, j, bass.ds(b, 1)]

                done, dense = blocks_before(q, SUMMED), blocks_before(q, DENSE)
                dve.wait_ge(pe_c, b + (dense + 1))
                ps = banks[:, B_ROWS, 0:D]
                x_b, r_b, h_b = row(x_rows, b), row(r_rows, b), row(h_rows, b)
                if q == PASS_SG3:
                    link(V.tensor_tensor(ysum[:, :], ps, bias[:, 3, :], ALU.add))
                    link(V.scalar_tensor_tensor(ysum[:, :], ysum[:, :], 0.0, r_b, ALU.max, ALU.add))
                else:
                    link(V.tensor_tensor(ysum[:, :], ps, pre_b[:, :], ALU.add))
                link(V.bn_stats(stats[:, :], ysum[:, :]))
                dve.sem_inc(dve_step, 1)
                V.bn_aggr(mv[:, :], stats[:, :]).then_inc(var_done, 1)
                dve.wait_ge(std_done, b + (dense + 1))
                link(V.reciprocal(rstd[:, :], std[:, :]))
                V.tensor_scalar(x_b, ysum[:, :], mv[:, 0:1], rstd[:, :], ALU.subtract, ALU.mult).then_inc(x_done, 1)
                dve.wait_ge(x_done, b + (done + 1))
                if q == PASS_VALUE:
                    V.tensor_scalar(h_b, x_b, per_node(HD2P), None, ALU.mult)
                    V.tensor_scalar(r_b, x_b, 0.5, None, ALU.mult).then_inc(blk_done, 1)
                elif q == PASS_SAGE:
                    V.tensor_copy(r_b, x_b).then_inc(blk_done, 1)
                else:
                    dve.sem_inc(blk_done, 1)

            def strip_onehots(q, i, k):
                n = BUILDS.index(q) * NG
                s = i * 2 + (n + k)
                tile0 = dve.value_load(tile0_i[0:1, bass.ds(s, 1)], min_val=0, max_val=NT - ST)
                dve.wait_ge(strip_done, s + 1)
                V.scalar_tensor_tensor(key_tile[:, k, 0:ST], dstrip[:, bass.ds(tile0, ST)], iota_f[:, bass.ds(s, 1)],
                                       key1[:, bass.ds(tile0, ST)], ALU.is_equal, ALU.mult).then_inc(key_done, 1)
                for t in range(ST):
                    V.tensor_scalar(oh_src[:, t, :], iota_f[:, :], src_lo[:, bass.ds(tile0 + t, 1)], None, ALU.is_equal)
                dve.wait_ge(key_done, s + 1)
                for t in range(ST):
                    last = V.tensor_scalar(oh_key[:, t, :], key_iota, key_tile[:, k, t:t + 1], None, ALU.is_equal)
                last.then_inc(oh_strip, 1)

            for q in SUMMED:
                h = hop_no(q)
                if q != PASS_VALUE:
                    dve.wait_ge(staged, blocks_before(q))
                if q == PASS_VALUE:
                    V.memset(den, 0.0)
                link(V.memset(acc[:, :, :], 0.0))
                if q == PASS_VALUE:
                    dve.wait_ge(moved, 80)
                if q == PASS_GCN1:
                    dve.wait_ge(edges_in, 32)
                    lo, hi = edge_t[:, 1, :], edge_t[:, 0, :]
                    V.tensor_scalar(lo, edge_i[:, 1, :], SW - 1, None, ALU.bitwise_and)
                    link(V.tensor_scalar(hi, edge_i[:, 1, :], 5, None, ALU.arith_shift_right))
                    V.tensor_copy(dstrip, hi)
                    link(V.tensor_copy(key1, lo))
                    link(V.scalar_tensor_tensor(key1, src_hi[:, :], float(SW), key1, ALU.mult, ALU.add))
                    link(V.tensor_scalar(key1, key1, 1.0, None, ALU.add))
                    link(V.tensor_scalar(key_iota[:, 0:P], iota_f[:, :], 1.0, None, ALU.add))
                    for c in range(1, -(-SC // P)):
                        w = min(P, SC - c * P)
                        link(V.tensor_scalar(key_iota[:, c * P:c * P + w], iota_f[:, 0:w], float(c * P + 1), None, ALU.add))
                prepare(q, 0, 0, 0)
                with dve.Fori(0, LAG) as i:
                    prepare(q, i * 2 + 1, 1, i)
                    if q in BUILDS:
                        strip_onehots(q, i, 0)
                    add_sums(q, i * 2, 0)
                    prepare(q, i * 2 + 2, 0, i + 1)
                    if q in BUILDS:
                        strip_onehots(q, i, 1)
                    add_sums(q, i * 2 + 1, 1)

                def both(i, last):
                    b = i - LAG
                    prepare(q, i * 2 + 1, 1, i)
                    rows_step(q, b)
                    if q in BUILDS:
                        strip_onehots(q, i, 0)
                    add_sums(q, i * 2, 0)
                    bias_step(q, b)
                    if not last:
                        prepare(q, i * 2 + 2, 0, i + 1)
                    if q in BUILDS:
                        strip_onehots(q, i, 1)
                    add_sums(q, i * 2 + 1, 1)
                    norm_step(q, b)

                start = chain_total(chain)
                size = LINKS[q]
                with dve.Fori(LAG, NG // 2 - 1) as i:
                    if size:
                        chain.enter(i * size + (start - LAG * size))
                    both(i, False)
                    if size:
                        n = chain.leave()
                        assert n == size, (q, n)
                chain.enter(start + (LOOPED - 1) * size)
                both(NG // 2 - 1, True)
                for b in range(LOOPED, NB):
                    rows_step(q, b)
                    bias_step(q, b)
                    norm_step(q, b)
                if q == PASS_GCN1:
                    dve.wait_ge(hist_done, NG + 3)
                    V.tensor_scalar(node[:, OUTDEG, :], banks[:, 2, 0:NB], 1.0, None, ALU.max).then_inc(norm_ready, 1)
                    dve.wait_ge(norm_root, 1)
                    link(V.reciprocal(node[:, NORM, :], node[:, NORM2, :]))
                    link(V.tensor_tensor(node[:, NORM2, :], node[:, NORM, :], node[:, NORM, :], ALU.mult))

            def rest_step(stage_no, b, whole, rest, to):
                dve.wait_ge(hi_done, b + (stage_no * NB + 1))
                V.tensor_tensor(rest, whole, row(parts[to][0], b), ALU.subtract).then_inc(rest1, 1)

            def low_step(stage_no, b, rest, to):
                dve.wait_ge(mid_done, b + (stage_no * NB + 1))
                V.tensor_tensor(row(parts[to][2], b), rest, row(parts[to][1], b), ALU.subtract).then_inc(lo_done, 1)

            dve.wait_ge(u_ready, NB)
            rest_step(0, 0, row(h_rows, 0), row(h_rows, 0), 0)
            with dve.Fori(0, NB - 1) as b:
                rest_step(0, b + 1, row(h_rows, b + 1), row(h_rows, b + 1), 0)
                low_step(0, b, row(h_rows, b), 0)
            low_step(0, NB - 1, row(h_rows, NB - 1), 0)
            for n, q in enumerate(COUNTED):
                if q != PASS_SG3:
                    def hop_rows(b, slot, i):
                        dve.wait_ge(hop_act, b + (NB * n + 3))
                        rows_step(q, b, slot)
                        rest_step(n + 1, b, tab_row[:, :], ysum[:, :], (n + 1) % 2)
                        low_step(n + 1, b, ysum[:, :], (n + 1) % 2)

                    odd_block_pairs(dve, NB * n, hop_rows)
                else:
                    start = chain_total(chain)
                    size = LINKS[q]
                    with dve.Fori(0, NB // 2) as i:
                        for k in range(2):
                            chain.enter(i * (2 * size) + (start + k * size))
                            rows_step(q, i * 2 + k, (NB * n + k) % 2)
                            norm_step(q, i * 2 + k)
                            assert chain.leave() == size
                    chain.enter(start + (NB - 1) * size)
                    rows_step(q, NB - 1, (NB * n) % 2)
                    norm_step(q, NB - 1)


def kernel(**inputs):
    import numpy as np
    import concourse.bacc as bacc
    from concourse.bass_utils import run_bass_kernel_spmd

    nc = bacc.Bacc("TRN2", target_bir_lowering=False, num_devices=1)
    x = np.asarray(inputs["x"])

    def padded(v, fill, rows):
        v = np.asarray(v)
        o = np.full((rows,) + v.shape[1:], fill, v.dtype)
        o[:v.shape[0]] = v
        return o

    def tiles(v):
        return v.reshape(NG, P, TG).transpose(1, 0, 2).reshape(P, NT)

    xp = padded(x, 0, NP)
    src = padded(inputs["src"], N, EP)
    dst = padded(inputs["dst"], N, EP)
    run = dst.reshape(P, PJ)
    ef = padded(inputs["edge_attr_64"], 0, EP)
    arrays = {
        "x": xp, "x_t": xp.T,
        "src_t": tiles(src), "dst_t": tiles(dst), "dst_run": run,
        "src_e": src.reshape(NT, P).T, "dst_e": dst.reshape(NT, P).T, "last": dst[P - 1::P],
        "base": dst[::EG], "ends": np.stack([run[:, 0], run[:, -1]]),
        "ew_t": tiles(padded(inputs["edge_weight"], 0, EP)),
        "ew1_t": tiles(padded(np.asarray(inputs["edge_weight1"])[:, 0], 0, EP)),
        "ef_t": ef.reshape(NG, P, TG, FE).transpose(3, 0, 2, 1).reshape(FE, EP),
        "Wq": inputs["L0_gnn_Wq"], "Wk": inputs["L0_gnn_Wk"], "Wv": inputs["L0_gnn_Wv"], "Wo": inputs["L0_gnn_Wo"],
        "W1": inputs["L0_gnn_W1"], "b1_t": np.asarray(inputs["L0_gnn_b1"]).reshape(FC, P).T,
        "W2": inputs["L0_gnn_W2"], "b2": inputs["L0_gnn_b2"], "bo": inputs["L0_gnn_bo"],
        "L1_Wt": np.asarray(inputs["L1_gnn_W"]).T, "L1_b": inputs["L1_gnn_b"],
        "L2_Wt": np.asarray(inputs["L2_gnn_W"]).T, "L2_b": inputs["L2_gnn_b"],
        "L3_W": inputs["L3_gnn_W"], "L3_b": inputs["L3_gnn_b"],
    }
    arrays = {k: np.ascontiguousarray(v) for k, v in arrays.items()}
    a = {k: nc.dram_tensor("in_" + k, v.shape, mybir.dt.from_np(v.dtype), kind="ExternalInput").ap()
         for k, v in arrays.items()}
    out = nc.dram_tensor("out", [N, D], F32, kind="ExternalOutput").ap()
    gnn_program(nc, a, out)
    r = run_bass_kernel_spmd(nc, [{"in_" + k: v for k, v in arrays.items()}], core_ids=[0])
    return r.results[0]["out"]
```

```python
import concourse.bass as bass
from concourse import mybir
from contextlib import ExitStack

F32 = mybir.dt.float32
I32 = mybir.dt.int32
BF16 = mybir.dt.bfloat16
F16 = mybir.dt.float16
ALU = mybir.AluOpType
ACT = mybir.ActivationFunctionType
AX = mybir.AxisListType

P = 128
N = 3125
D = 256
FC = D // P
E = 53125
HEADS = 8
HD = D // HEADS
FE = 64
TG = 8
EG = TG * P
NG = -(-E // EG)
NG += NG % 2
EP = NG * EG
NT = NG * TG
PJ = EP // P
NB = -(-N // P)
NP = NB * P
NA = NP + P
LAG = 3
LOOPED = NG // 2 - LAG
BIG = 1.0e30
XW = HEADS + 2
EPS = 1e-5
SW = 32
ST = 7
STRIPS = 2 * NG
PER_BLOCK = P // SW
SC = NB * SW
SET_BLOCKS = 5
SETS = NB // SET_BLOCKS
SPLIT_BANK = 512 // SW

PASS_SCORE, PASS_VALUE, PASS_GCN1, PASS_GCN2, PASS_SAGE, PASS_SG1, PASS_SG2, PASS_SG3 = range(8)
HOPS = [PASS_VALUE, PASS_GCN1, PASS_GCN2, PASS_SAGE, PASS_SG1, PASS_SG2, PASS_SG3]
TABLED = [PASS_VALUE, PASS_GCN1, PASS_GCN2, PASS_SG3]
SUMMED = [PASS_VALUE, PASS_GCN1, PASS_GCN2, PASS_SAGE]
BUILDS = [PASS_GCN2, PASS_SAGE]
COUNTED = [PASS_SG1, PASS_SG2, PASS_SG3]
DENSE = {PASS_VALUE: 0, PASS_GCN2: 1, PASS_SAGE: 3, PASS_SG3: 4}
TURNED = [PASS_VALUE, PASS_GCN2, PASS_SG3]


def gnn_program(nc, a, out):
    ctx = ExitStack()
    with ctx:
        def sb(name, shape, dt=F32):
            return ctx.enter_context(nc.sbuf_tensor(name, shape, dt))

        def sem(name):
            return ctx.enter_context(nc.semaphore(name))

        def dram(name, shape):
            return nc.dram_tensor(name, shape, F32).ap()

        q_table = dram("q_table", [NA, D])
        k_table = dram("k_table", [NP, D])
        v_table = dram("v_table", [NP, D])
        table = {q: dram(f"h_table{q}", [NP, D]) for q in (PASS_GCN1, PASS_GCN2, PASS_SAGE)}
        counts = nc.dram_tensor("counts", [STRIPS // PER_BLOCK, P, NB, P], BF16).ap()
        score_dram = dram("score_dram", [EP, HEADS])
        exp_dram = dram("exp_dram", [EP, HEADS])

        x_rows = sb("x_rows", [P, NB, D])
        r_rows = sb("r_rows", [P, NB, D])
        h_rows = sb("h_rows", [P, NB, D])
        acc = sb("acc", [P, FC, NA])
        gath = sb("gath", [P, 2, TG, 2 * D])
        onehot = sb("onehot", [P, 2, TG, P])
        q_win = sb("q_win", [P, 2, D])
        prod = sb("prod", [P, 2, 2, D])
        w_qkv_t = sb("w_qkv", [P, FC * 3 * D])
        w_lin = sb("w_lin", [P, 5, FC, D])
        bias = sb("bias", [P, 4, D])
        w1 = sb("w1", [FE, D])
        b1c = sb("b1c", [P, FC])
        w2 = sb("w2", [P, FC, HEADS])
        b2b = sb("b2b", [P, HEADS])
        src_i = sb("src_i", [P, NT + 2 * TG], I32)
        dst_i = sb("dst_i", [P, NT], I32)
        src_lo = sb("src_lo", [P, NT])
        src_hi = sb("src_hi", [P, NT])
        ew = sb("ew", [P, NT])
        ew1 = sb("ew1", [P, NT])
        rel = sb("rel", [P, NG, TG])
        base_i = sb("base_i", [P, NG], I32)
        win_node = sb("win_node", [P, NG])
        idx_slot = sb("idx_slot", [P, 2, 2 * TG], I32)
        tile0_i = sb("tile0_i", [1, P], I32)
        iota_i = sb("iota_i", [P, P], I32)
        iota_f = sb("iota_f", [P, P])
        part_i = sb("part_i", [P, 1], I32)
        part_f = sb("part_f", [P, 1])
        ident = sb("ident", [P, P])
        zero_b = sb("zero_b", [P, P], BF16)
        eps = sb("eps", [P, 1])
        misc = sb("misc", [P, NA])
        xcol = sb("xcol", [P, 2, TG, XW])
        oh_hi = sb("oh_hi", [P, 2, TG, 32], BF16)
        stage = sb("stage", [P, FC, P])
        den_stage = sb("den_stage", [XW, P])
        x_stage = sb("x_stage", [P, D])
        rows = sb("rows", [P, D])
        turned = sb("turned", [P, FC, P])

        pre_b = sb("pre_b", [P, D])
        tab_row = sb("tab_row", [P, D])
        ysum = sb("ysum", [P, D])
        stats = sb("stats", [P, 6])
        mv = sb("mv", [P, 2])
        std = sb("std", [P, 1])
        rstd = sb("rstd", [P, 1])
        dstd = sb("dstd", [P, 1])
        blk_sc = sb("blk_sc", [P, 20])
        node = sb("node", [P, 8, NB])
        DINV, HDINV, HD2, HD2P, RDEG, NORM, NORM2, OUTDEG = range(8)
        ends = sb("ends", [HEADS, 2, P])
        ends_i = sb("ends_i", [HEADS, 2, P], I32)
        carry = sb("carry", [P, 4, HEADS])
        broken = sb("broken", [P, 2])
        path_f = sb("path_f", [1, 1])
        path_i = sb("path_i", [1, 1], I32)

        accf = acc[:, :, :].rearrange("p c n -> p (c n)")
        oht = accf[:, 0:2 * EG].rearrange("p (k e) -> p k e", k=2)
        ef = accf[0:FE, 2 * EG:4 * EG].rearrange("p (k e) -> p k e", k=2)
        hid = accf[:, 4 * EG:6 * EG].rearrange("p (u e) -> p u e", u=4)
        ohf = onehot[:, :, :, :].rearrange("p k t n -> p (k t n)")
        dst_row = ohf.bitcast(I32).rearrange("p (k e) -> p k e", k=2)
        den = misc[0:XW, :]
        miscb = misc[:, :].bitcast(BF16)
        c_build = miscb[:, 0:NB * P].rearrange("p (c n) -> p c n", n=P)
        c_slot = miscb[:, 0:2 * NB * P].rearrange("p (k c n) -> p k c n", k=2, n=P)
        w_qkv = w_qkv_t[:, :].rearrange("p (c f) -> p c f", c=FC)
        key1 = w_qkv_t[:, 0:NT]
        dstrip = w_qkv_t[:, NT:2 * NT]
        key_iota = w_qkv_t[:, 2 * NT:2 * NT + SC // 2].bitcast(F16)
        key_tile = w_qkv_t[:, 1300:1300 + 2 * TG].rearrange("p (k t) -> p k t", k=2)
        chain_m = ohf[0:HEADS, 0:4 * P].rearrange("h (m p) -> h m p", m=4)
        tails = ohf[0:HEADS, 4 * P:8 * P].rearrange("h (m p) -> h m p", m=4)
        qkv_out = ohf[:, 0:6 * D].rearrange("p (k f) -> p k f", k=2)
        xst = prod[:, :, :, :].rearrange("p a b d -> p (a b d)").rearrange("p (k c n) -> p k c n", k=4, c=FC)[:, 0:2, :, :]
        oh_lo = prod[:, :, :, :].rearrange("p a b d -> p (a b d)").bitcast(BF16).rearrange("p (k t n) -> p k t n", k=2, t=TG)
        hf = h_rows[:, :, :].rearrange("p b d -> p (b d)")
        score = hf[:, 0:NT * HEADS]
        s_run = r_rows[:, :, :].rearrange("p b d -> p (b d)")[:, 0:PJ * HEADS].rearrange("p (j h) -> p j h", h=HEADS)
        m_run = hf[:, 0:PJ * HEADS].rearrange("p (j h) -> p j h", h=HEADS)
        b_run = accf[:, 0:PJ * HEADS].rearrange("p (j h) -> p j h", h=HEADS)
        dst_run_i = accf[:, PJ * HEADS:PJ * HEADS + PJ].bitcast(I32)
        dst_run = accf[:, PJ * HEADS + PJ:PJ * HEADS + 2 * PJ]
        mask_f = accf[:, PJ * HEADS + 2 * PJ:PJ * HEADS + 3 * PJ]
        mask_b = accf[:, PJ * HEADS + 3 * PJ:PJ * HEADS + 4 * PJ]
        gathf = gath[:, :, :, :].rearrange("p k t f -> p (k t f)")
        row_slot = gathf[:, 0:2 * TG * D].rearrange("p (k t f) -> p k t f", k=2, t=TG)
        expo = gathf[:, 2 * TG * D:2 * TG * D + NT * HEADS].rearrange("p (t h) -> p t h", h=HEADS)

        s_part = gathf[0:HEADS, 2 * TG * D:2 * TG * D + 3 * EG // 2].bitcast(BF16).rearrange("h (j e) -> h j e", j=3)
        s_rest = gathf[0:HEADS, 2 * TG * D + 3 * EG // 2:2 * TG * D + 5 * EG // 2]
        ident_b = gathf[0:HEADS, 7 * EG:7 * EG + HEADS // 2].bitcast(BF16)
        upper = gathf[:, 2 * TG * D:4 * TG * D]
        oh_key = upper[:, 0:ST * SC // 2].bitcast(BF16).rearrange("p (t n) -> p t n", t=ST)
        oh_src = upper[:, ST * SC // 2:ST * SC // 2 + ST * P // 2].bitcast(BF16).rearrange("p (t n) -> p t n", t=ST)
        edge_i = upper[:, 0:2 * NT].bitcast(I32).rearrange("p (k t) -> p k t", k=2)
        edge_t = upper[:, 2 * NT:4 * NT].bitcast(I32).rearrange("p (k t) -> p k t", k=2)
        last_i = gathf[:, 2 * NT:3 * NT].bitcast(I32)
        last_lt = gathf[:, 3 * NT:4 * NT]
        first_i = gathf[:, 5760:5760 + NT].bitcast(I32)
        run_i = gathf[:, 6176:6176 + NT].bitcast(I32)
        check = gathf[:, 6592:6592 + NT]
        gathb = gathf.bitcast(BF16)
        hfb = hf.bitcast(BF16)
        accb = accf.bitcast(BF16)

        def parts_of(hi_mid, lo):
            v = [hi_mid[:, 0:NB * D], hi_mid[:, NB * D:2 * NB * D], lo]
            return [t.rearrange("p (b f) -> p b f", b=NB) for t in v]

        parts = [parts_of(accb, gathb[:, 0:NB * D]), parts_of(hfb, gathb[:, NB * D:2 * NB * D])]

        banks = ctx.enter_context(nc.psum_tensor("banks", [P, 8, 512], F32))
        B_ROWS, B_TURN = 6, 7
        Q_BANKS = [4, 5, 7, 4]
        Q_READ = [8, 6, 7, 9]

        def part(first, width):
            return gathf[:, first:first + width]

        g_kv, g_q, g_tmp = part(0, 2 * D), part(2 * D, D), part(3 * D, D)
        g_hidden = part(4 * D, D).rearrange("p (c e) -> p c e", c=FC)
        g_rows_w = part(5 * D, D)
        g_ef = gathf[0:FE, 6 * D:6 * D + P]
        g_dst, g_mask = part(7 * D, P).bitcast(I32), part(7 * D + P, P)
        g_s = part(8 * D, P * HEADS)
        g_masked = part(12 * D, P * HEADS).rearrange("p (e h) -> p e h", h=HEADS)
        g_iota = part(16 * D, SET_BLOCKS * P)
        g_max = part(20 * D, NB * HEADS).rearrange("p (b h) -> p b h", h=HEADS)
        g_extra = part(21 * D, NB * (XW + 1)).rearrange("p (b x) -> p b x", x=XW + 1)
        g_zero = part(23 * D, D).bitcast(BF16)
        g_node, g_first = part(24 * D, NB), part(24 * D + 32, SETS)
        g_m, g_e, g_rel = part(25 * D, HEADS), part(25 * D + 16, HEADS), part(25 * D + 32, 2)
        g_onehot = ohf[:, 0:2 * SET_BLOCKS * P].rearrange("p (k j n) -> p k j n", k=2, j=SET_BLOCKS)
        g_acc = accf[:, 0:NB * D].rearrange("p (b d) -> p b d", d=D)
        m_table = dram("m_table", [NP, HEADS])
        g_table = {q: dram(f"any_table{q}", [NP, D]) for q in HOPS[1:]}

        loaded = sem("loaded")
        b2_loaded = sem("b2_loaded")
        gath_done = [[sem(f"gath_done{k}{half}") for half in range(2)] for k in range(2)]
        idx_ready = sem("idx_ready")
        pool_step = sem("pool_step")
        consts_done = sem("consts_done")
        link_sem = sem("link_sem")
        w_in = sem("w_in")
        setup_done = sem("setup_done")
        path_known = sem("path_known")
        phase = sem("phase")
        exps_done = sem("exps_done")
        xt_in = [sem(f"xt_in{k}") for k in range(2)]
        qkv_done = sem("qkv_done")
        qkv_act = sem("qkv_act")
        qkv_stored = [sem(f"qkv_stored{k}") for k in range(2)]
        qkv_free = sem("qkv_free")
        moved = sem("moved")
        oh_ready = sem("oh_ready")
        msg_ready = sem("msg_ready")
        half_read = sem("half_read")
        grp_done = sem("grp_done")
        evac_done = sem("evac_done")
        hist_oh = sem("hist_oh")
        hist_done = sem("hist_done")
        qwin_done = [sem(f"qwin_done{k}") for k in range(2)]
        dst_in = [sem(f"dst_in{k}") for k in range(2)]
        ef_done = [sem(f"ef_done{k}") for k in range(2)]
        hid_done = sem("hid_done")
        hid_evac = sem("hid_evac")
        s_done = sem("s_done")
        s_hi = sem("s_hi")
        s_left = sem("s_left")
        s_mid = sem("s_mid")
        s_low = sem("s_low")
        s_back = sem("s_back")
        s_read = sem("s_read")
        qk_done = sem("qk_done")
        qk_read = sem("qk_read")
        red_done = sem("red_done")
        pe_small = sem("pe_small")
        dve_step = sem("dve_step")
        pe_step = sem("pe_step")
        staged = sem("staged")
        pe_a = sem("pe_a")
        rows_done = sem("rows_done")
        rows_done_sage = sem("rows_done_sage")
        pe_b = sem("pe_b")
        turn_done = sem("turn_done")
        pe_c = sem("pe_c")
        var_done = sem("var_done")
        std_done = sem("std_done")
        deg_done = sem("deg_done")
        dstd_done = sem("dstd_done")
        x_done = sem("x_done")
        blk_done = sem("blk_done")
        tab_ready = sem("tab_ready")
        tab_stored = sem("tab_stored")
        tab_free = sem("tab_free")
        edges_in = sem("edges_in")
        oh_strip = sem("oh_strip")
        key_done = sem("key_done")
        strip_done = sem("strip_done")
        strip_out = sem("strip_out")
        c_stored = sem("c_stored")
        c_free = sem("c_free")
        c_in = [sem(f"c_in{k}") for k in range(2)]
        u_ready = sem("u_ready")
        hi_done = sem("hi_done")
        mid_done = sem("mid_done")
        rest1 = sem("rest1")
        lo_done = sem("lo_done")
        hop_done = sem("hop_done")
        hop_dve = sem("hop_dve")
        hop_act = sem("hop_act")
        norm_ready = sem("norm_ready")
        norm_root = sem("norm_root")
        stored = sem("stored")

        g_hid = sem("g_hid")
        g_ef_in = sem("g_ef_in")
        g_relu = sem("g_relu")
        g_mlp = sem("g_mlp")
        g_idx = sem("g_idx")
        g_gath = sem("g_gath")
        g_scored = sem("g_scored")
        g_stage = sem("g_stage")
        g_moved = sem("g_moved")
        g_tabled = sem("g_tabled")
        g_spread = sem("g_spread")
        g_mask_ok = sem("g_mask_ok")
        g_masked_ok = sem("g_masked_ok")
        g_red_ok = sem("g_red_ok")
        g_max_ok = sem("g_max_ok")
        g_maxed = sem("g_maxed")
        g_m_in = [sem(f"g_m_in{k}") for k in range(2)]
        g_in = {q: [sem(f"g_in{q}_{k}") for k in range(2)] for q in HOPS}
        g_rel_ok = sem("g_rel_ok")
        g_shift = sem("g_shift")
        g_exp = sem("g_exp")
        g_msg = sem("g_msg")
        g_used = sem("g_used")
        g_closed = sem("g_closed")
        g_evac = sem("g_evac")
        g_zeroed = sem("g_zeroed")
        g_deg = sem("g_deg")
        g_root = sem("g_root")
        g_rows = sem("g_rows")
        g_turned = sem("g_turned")
        g_feat = sem("g_feat")
        g_prod = sem("g_prod")
        g_var = sem("g_var")
        g_std = sem("g_std")
        g_link = sem("g_link")

        N_LOADS = 23
        STAGES = ["scores", "tails_f", "chain_f", "tails_b", "chain_b", "shifted"]
        PHASE = {name: v + 1 for v, name in enumerate(STAGES)}

        block = ctx.enter_context(nc.Block())

        def hop_no(q):
            return HOPS.index(q)

        def blocks_before(q, only=HOPS):
            return NB * sum(1 for p in only if p < q)

        def choose_path(eng, windows_path, any_order_path):
            eng.wait_ge(path_known, 1)
            fits = eng.value_load(path_i[0:1, 0:1], min_val=0, max_val=1)
            with eng.If(fits == 1):
                windows_path()
            with eng.Else():
                any_order_path()

        def gathered(eng, k, half, i, n):
            eng.wait_ge(gath_done[k][half], i * (8 * TG) + 8 * TG * (NG // 2 * n + 1))

        def each_group(eng, body):
            with eng.Fori(0, NG // 2) as i:
                for k in range(2):
                    body(i * 2 + k, k, i)

        def each_block_pair(eng, body):
            with eng.Fori(0, NB // 2) as i:
                for k in range(2):
                    body(i * 2 + k, k, i)
            for b in range(NB // 2 * 2, NB):
                body(b, b % 2, b // 2)

        def store_block(eng, q, b, n):
            done = blocks_before(q, TABLED)
            eng.wait_ge(tab_ready, b + (done + 2))
            dst = out if q == PASS_SG3 else table[q + 1]
            eng.dma_start(dst[bass.ds(b * P, n), :], tab_row[0:n, :]).then_inc(tab_stored, 16)
            eng.wait_ge(tab_stored, b * 16 + (16 * done + 16))
            eng.sem_inc(tab_free, 1)

        def odd_block_pairs(eng, t0, body):
            with eng.Fori(0, NB // 2) as i:
                for k in range(2):
                    body(i * 2 + k, (t0 + k) % 2, i)
            for b in range(NB // 2 * 2, NB):
                body(b, (t0 + b) % 2, b // 2)

        @block.sync
        def _(sp):
            sp.sem_inc(qkv_free, 2)
            sp.sem_inc(tab_free, 1)
            sp.sem_inc(c_free, 1)

            def w_view(t):
                return t.rearrange("(c p) f -> p c f", p=P)

            def load_xt(b, k):
                sp.wait_ge(qkv_done, b + 1)
                sp.dma_start(xst[:, k, :, :], a["x_t"].rearrange("(c p) n -> p c n", p=P)[:, :, bass.ds(b * P, P)]
                             ).then_inc(xt_in[k], 16)

            for n, w in enumerate(("Wq", "Wk", "Wv")):
                sp.dma_start(w_qkv[:, :, n * D:(n + 1) * D], w_view(a[w])).then_inc(w_in, 16)
            load_xt(0, 0)
            load_xt(1, 1)
            loads = [
                (src_i[:, 0:NT], a["src_t"]), (edge_t[:, 0, :], a["src_e"]), (edge_t[:, 1, :], a["dst_e"]),
                (last_i, a["last"].partition_broadcast(P)), (first_i, a["first"].partition_broadcast(P)), (run_i, a["dst_run"]),
                (dst_i[:, :], a["dst_t"]), (base_i[:, :], a["base"].partition_broadcast(P)),
                (w1[:, :], a["W1"]), (b1c[:, :], a["b1_t"]), (w2[:, :, :], w_view(a["W2"])),
                (ends_i[:, :, :], a["ends"].partition_broadcast(HEADS)),
                (ew[:, :], a["ew_t"]), (ew1[:, :], a["ew1_t"]),
                (w_lin[:, 0, :, :], w_view(a["Wo"])), (w_lin[:, 1, :, :], w_view(a["L1_Wt"])),
                (w_lin[:, 2, :, :], w_view(a["L2_Wt"][0:D, :])), (w_lin[:, 3, :, :], w_view(a["L2_Wt"][D:2 * D, :])),
                (w_lin[:, 4, :, :], w_view(a["L3_W"])),
                (bias[:, 0, :], a["bo"].partition_broadcast(P)), (bias[:, 1, :], a["L1_b"].partition_broadcast(P)),
                (bias[:, 2, :], a["L2_b"].partition_broadcast(P)), (bias[:, 3, :], a["L3_b"].partition_broadcast(P)),
            ]
            assert len(loads) == N_LOADS
            for dst, src in loads:
                sp.dma_start(dst, src).then_inc(loaded, 16)
            sp.dma_start(b2b[:, :], a["b2"].partition_broadcast(P)).then_inc(b2_loaded, 16)

            def store_qkv(b, k):
                sp.wait_ge(qkv_act, b + 3)
                for n, to in enumerate((q_table, k_table, v_table)):
                    sp.dma_start(to[bass.ds(b * P, P), :], qkv_out[:, k, n * D:(n + 1) * D]).then_inc(qkv_stored[k], 16)

            def free_qkv(k, i):
                sp.wait_ge(qkv_stored[k], i * 48 + 48)
                sp.sem_inc(qkv_free, 1)

            load_xt(2, 0)
            store_qkv(0, 0)
            with sp.Fori(0, NB // 2 - 1) as i:
                load_xt(i * 2 + 3, 1)
                store_qkv(i * 2 + 1, 1)
                free_qkv(0, i)
                load_xt(i * 2 + 4, 0)
                store_qkv(i * 2 + 2, 0)
                free_qkv(1, i)
            for b in range(NB // 2 * 2 - 1, NB):
                store_qkv(b, b % 2)
                free_qkv((b - 1) % 2, (b - 1) // 2)
            free_qkv((NB - 1) % 2, (NB - 1) // 2)
            sp.dma_start(q_table[NP:NA, :], qkv_out[:, (NB - 1) % 2, 0:D]).then_inc(qkv_stored[(NB - 1) % 2], 16)
            sp.wait_ge(qkv_stored[(NB - 1) % 2], 48 * ((NB + 1) // 2) + 16)
            sp.sem_inc(qkv_free, 1)
            sp.dma_start(x_rows[:, :, :], a["x"].rearrange("(b p) f -> p b f", p=P)).then_inc(b2_loaded, 16)

            def any_order_path():
                sp.sem_inc(g_hid, 1)
                sp.sem_inc(g_maxed, 1)
                with sp.Fori(0, NT) as t:
                    sp.wait_ge(g_hid, t + 1)
                    sp.dma_start(g_ef, a["ef_t"][:, bass.ds(t * P, P)]).then_inc(g_ef_in, 16)
                sp.wait_ge(g_stage, 1)
                sp.dma_start(score_dram.rearrange("(g p i) h -> p g (i h)", g=NG, p=P),
                             score.rearrange("p (g x) -> p g x", g=NG)).then_inc(g_moved, 16)
                sp.wait_ge(g_moved, 16)
                with sp.Fori(0, NT) as t:
                    sp.wait_ge(g_maxed, t + 1)
                    sp.dma_start(g_s, score_dram.rearrange("(t e) h -> t (e h)", e=P)[bass.ds(t, 1), :].partition_broadcast(P)
                                 ).then_inc(g_spread, 16)
                    sp.dma_start(g_dst, a["dst_nat"][bass.ds(t, 1), :].partition_broadcast(P)).then_inc(g_spread, 16)
                sp.wait_ge(g_stage, 2)
                sp.dma_start(m_table.rearrange("(b p) h -> p b h", p=P), g_max).then_inc(g_moved, 16)
                sp.wait_ge(g_moved, 32)
                sp.sem_inc(g_tabled, 1)
                for n, q in enumerate(HOPS):
                    sp.wait_ge(g_stage, n + 3)
                    rows_now = x_rows[:, :, :] if q in (PASS_GCN2, PASS_SG3) else g_acc
                    if q == PASS_SG3:
                        full = N // P
                        sp.dma_start(out[0:full * P, :].rearrange("(b p) d -> p b d", p=P), rows_now[:, 0:full, :]).then_inc(g_moved, 16)
                        sp.dma_start(out[full * P:N, :], rows_now[0:N - full * P, full, :]).then_inc(g_moved, 16)
                        sp.wait_ge(g_moved, 64 + 16 * n)
                    else:
                        sp.dma_start(g_table[q + 1].rearrange("(b p) d -> p b d", p=P), rows_now).then_inc(g_moved, 16)
                        sp.wait_ge(g_moved, 48 + 16 * n)
                        sp.sem_inc(g_tabled, 1)

            def windows_path():
                def score_io(g, k, i):
                    first = sp.value_load(base_i[0:1, bass.ds(g, 1)], min_val=0, max_val=NA - P)
                    sp.wait_ge(hid_done, g * 4 + 4)
                    sp.dma_start(ef[:, k, :], a["ef_t"][:, bass.ds(g * EG, EG)]).then_inc(ef_done[k], 16)
                    sp.wait_ge(qk_done, g * 4 + 4)
                    sp.dma_start(dst_row[:, k, :], a["dst_rows"][bass.ds(g, 1), :].partition_broadcast(P)).then_inc(dst_in[k], 16)
                    sp.dma_start(q_win[:, k, :], q_table[bass.ds(first, P), :]).then_inc(qwin_done[k], 16)

                each_group(sp, score_io)

                sp.wait_ge(phase, PHASE["scores"])
                sp.dma_start(score_dram.rearrange("(g p i) h -> p g (i h)", g=NG, p=P),
                             score.rearrange("p (g x) -> p g x", g=NG)).then_inc(moved, 16)
                sp.dma_start(dst_run_i, a["dst_run"]).then_inc(moved, 16)
                sp.wait_ge(moved, 32)
                sp.dma_start(s_run, score_dram.rearrange("(p j) h -> p j h", p=P)).then_inc(moved, 16)
                sp.wait_ge(exps_done, 1)
                sp.dma_start(exp_dram.rearrange("(p j) h -> p j h", p=P), s_run).then_inc(moved, 16)
                sp.wait_ge(moved, 64)
                sp.dma_start(expo.rearrange("p (g t) h -> p g (t h)", g=NG),
                             exp_dram.rearrange("(g p i) h -> p g (i h)", g=NG, p=P)).then_inc(moved, 16)

                def store_table(q, b):
                    store_block(sp, q, b, P)

                with sp.Fori(0, NB) as b:
                    store_table(PASS_VALUE, b)
                sp.wait_ge(grp_done, NG + 2)
                sp.dma_start(edge_i[:, 0, :], a["src_e"]).then_inc(edges_in, 16)
                sp.dma_start(edge_i[:, 1, :], a["dst_e"]).then_inc(edges_in, 16)

                with sp.Fori(0, NB) as b:
                    store_table(PASS_GCN1, b)

                def store_counts(q, m):
                    n = BUILDS.index(q) * (NG // 4)
                    sp.wait_ge(strip_out, m * PER_BLOCK + (PER_BLOCK * (n + 1) + 1))
                    sp.dma_start(counts[bass.ds(m + n, 1), :, :, :].rearrange("a p c n -> p (a c) n"), c_build).then_inc(c_stored, 16)
                    sp.wait_ge(c_stored, m * 16 + (16 * n + 16))
                    sp.sem_inc(c_free, 1)

                for q in BUILDS:
                    tabled = q in TABLED
                    store_counts(q, 0)
                    store_counts(q, 1)
                    if tabled:
                        store_table(q, 0)
                    with sp.Fori(2, NG // 4) as m:
                        if tabled:
                            store_table(q, m * 2 - 3)
                        store_counts(q, m)
                        if tabled:
                            store_table(q, m * 2 - 2)
                    if tabled:
                        for b in range(NG // 2 - 3, NB):
                            store_table(q, b)

                def load_nth(t, k, b):
                    if not isinstance(t, int) or t >= 2:
                        sp.wait_ge(hop_done, t - 1)
                    sp.dma_start(c_slot[:, k, :, :], counts[bass.ds(b, 1), :, :, :].rearrange("a p c n -> p (a c) n")
                                 ).then_inc(c_in[k], 16)

                for n in range(len(COUNTED)):
                    t0 = NB * n
                    if n < 2:
                        first_pair = 0
                        if n == 0:
                            load_nth(0, 0, 0)
                            load_nth(1, 1, 1)
                            first_pair = 1
                        with sp.Fori(first_pair, NB // 2) as i:
                            for k in range(2):
                                load_nth(i * 2 + (k + t0), (t0 + k) % 2, i * 2 + k)
                        load_nth(t0 + NB - 1, (t0 + NB - 1) % 2, NB - 1)
                    else:
                        load_nth(t0, t0 % 2, 0)
                        load_nth(t0 + 1, (t0 + 1) % 2, 1)
                        with sp.Fori(0, NB // 2 - 1) as i:
                            for k in range(2):
                                load_nth(i * 2 + (k + t0 + 2), (t0 + k) % 2, i * 2 + (k + 2))
                                store_block(sp, PASS_SG3, i * 2 + k, P)
                        store_block(sp, PASS_SG3, NB - 3, P)
                        load_nth(t0 + NB - 1, (t0 + NB - 1) % 2, NB - 1)
                        store_block(sp, PASS_SG3, NB - 2, P)
                        store_block(sp, PASS_SG3, NB - 1, N - (NB - 1) * P)

            choose_path(sp, windows_path, any_order_path)

        @block.gpsimd
        def _(pool):
            pool.iota(iota_i[:, :], pattern=[[1, P]], base=0, channel_multiplier=0).then_inc(consts_done, 1)
            pool.iota(part_i[:, :], pattern=[[1, 1]], base=0, channel_multiplier=1).then_inc(consts_done, 1)
            pool.wait_ge(loaded, 16 * N_LOADS)

            pool.memset(src_i[:, NT:NT + 2 * TG], 0).then_inc(consts_done, 1)
            pool.wait_ge(consts_done, 3)

            def any_order_path():
                pool.sem_inc(g_scored, 1)
                pool.sem_inc(g_used, 1)
                pool.wait_ge(qkv_free, NB + 3)
                with pool.Fori(0, NT) as t:
                    pool.wait_ge(g_scored, t + 1)
                    pool.sem_inc(pool_step, 1)
                    pool.tensor_copy(idx_slot[:, 0, 0:1], src_i[:, bass.ds(t, 1)]).then_inc(g_idx, 1)
                    pool.tensor_copy(idx_slot[:, 0, 1:2], dst_i[:, bass.ds(t, 1)]).then_inc(g_idx, 1)
                    pool.wait_ge(g_idx, t * 2 + 2)
                    pool.sem_inc(pool_step, 1)
                    pool.indirect_dma_start(g_kv[:, 0:D], None, k_table, bass.IndirectOffsetOnAxis(idx_slot[:, 0, 0:1], 0)).then_inc(g_gath, 16)
                    pool.indirect_dma_start(g_q, None, q_table, bass.IndirectOffsetOnAxis(idx_slot[:, 0, 1:2], 0)).then_inc(g_gath, 16)
                for n, q in enumerate(HOPS):
                    pool.wait_ge(g_tabled, n + 1)
                    with pool.Fori(0, SETS) as s:
                        with pool.Fori(0, NT // 2) as j:
                            for k in range(2):
                                pool.wait_ge(g_used, s * NT + j * 2 + (k + SETS * NT * n + 1))
                                pool.sem_inc(pool_step, 1)
                                pool.tensor_copy(idx_slot[:, 0, 0:1], src_i[:, bass.ds(j * 2 + k, 1)]).then_inc(g_idx, 1)
                                pool.tensor_copy(idx_slot[:, 0, 1:2], dst_i[:, bass.ds(j * 2 + k, 1)]).then_inc(g_idx, 1)
                                pool.wait_ge(g_idx, s * (2 * NT) + j * 4 + (2 * k + 2 * SETS * NT * n + 2 * NT + 2))
                                pool.sem_inc(pool_step, 1)
                                if q == PASS_VALUE:
                                    pool.indirect_dma_start(g_m, None, m_table, bass.IndirectOffsetOnAxis(idx_slot[:, 0, 1:2], 0)
                                                            ).then_inc(g_m_in[k], 16)
                                pool.indirect_dma_start(g_kv[:, D:2 * D] if q == PASS_VALUE else g_q, None, v_table if q == PASS_VALUE else g_table[q],
                                                        bass.IndirectOffsetOnAxis(idx_slot[:, 0, 0:1], 0)).then_inc(g_in[q][k], 16)

            def windows_path():
                for n, q in enumerate([PASS_SCORE] + SUMMED):
                    if q == PASS_SCORE:
                        pool.wait_ge(qkv_free, NB + 3)
                        source = k_table
                    elif q == PASS_VALUE:
                        pool.wait_ge(qk_read, NG * 4 + 8)
                        source = v_table
                    else:
                        pool.wait_ge(tab_free, blocks_before(q, TABLED) + 1)
                        source = table[q]
                    copies = 1 + NG // 2

                    def gather(g, j, m):
                        k = m % 2
                        if k == 0:
                            pool.wait_ge(idx_ready, j * 2 + (m // 2 + 1 + copies * n))
                            pool.sem_inc(pool_step, 1)
                        for t in range(TG):
                            if q != PASS_SCORE and t % (TG // 2) == 0:
                                pool.wait_ge(half_read if t == 0 else grp_done, g + (NG * SUMMED.index(q) + 1))
                                pool.sem_inc(pool_step, 1)
                            if q == PASS_SCORE and t % 2 == 0:
                                pool.wait_ge(qk_read, g * 4 + (t // 2 + 1))
                                pool.sem_inc(pool_step, 1)
                            pool.indirect_dma_start(row_slot[:, k, t, :], None, source,
                                                    bass.IndirectOffsetOnAxis(idx_slot[:, m // 2, k * TG + t:k * TG + t + 1], 0)
                                                    ).then_inc(gath_done[k][t // (TG // 2)], 16)
                        if k == 1:
                            pool.tensor_copy(idx_slot[:, (m + 1) // 2 % 2, :], src_i[:, bass.ds((g + 1) * TG, 2 * TG)]
                                             ).then_inc(idx_ready, 1)

                    if n:
                        pool.wait_ge(idx_ready, copies * n)
                        for k in range(2):
                            for half in range(2):
                                pool.wait_ge(gath_done[k][half], 8 * TG * (NG // 2) * n)
                    pool.tensor_copy(idx_slot[:, 0, :], src_i[:, 0:2 * TG]).then_inc(idx_ready, 1)
                    with pool.Fori(0, NG // 4) as j:
                        for m in range(4):
                            gather(j * 4 + m, j, m)

            choose_path(pool, windows_path, any_order_path)

        @block.scalar
        def _(act):
            act.sem_inc(hid_evac, 8)
            act.sem_inc(tab_ready, 1)
            act.sem_inc(strip_out, 1)
            act.sem_inc(hop_act, 2)
            act.sem_inc(qkv_act, 2)

            def copy_qkv(b, k, i):
                act.wait_ge(qkv_done, b + 3)
                act.wait_ge(qkv_free, b + 1)
                nc.scalar.activation(qkv_out[:, k, :].rearrange("p (n f) -> p n f", n=3), banks[:, 3 * k:3 * k + 3, 0:D], ACT.Copy
                                     ).then_inc(qkv_act, 1)

            each_block_pair(act, copy_qkv)

            def any_order_path():
                act.sem_inc(g_relu, 1)
                with act.Fori(0, NT) as t:
                    act.wait_ge(g_hid, t + 2)
                    act.wait_ge(g_mlp, t + 1)
                    for c in range(FC):
                        last = nc.scalar.activation(g_hidden[:, c, :], banks[:, 0, c * P:(c + 1) * P], ACT.Relu, bias=b1c[:, c:c + 1])
                    last.then_inc(g_relu, 1)
                with act.Fori(0, SETS) as s:
                    with act.Fori(0, NT) as t:
                        act.wait_ge(g_shift, s * NT + t + 1)
                        nc.scalar.activation(xcol[:, 0, 0, 0:HEADS], g_e, ACT.Exp).then_inc(g_exp, 1)
                act.wait_ge(g_deg, 1)
                nc.scalar.activation(node[:, DINV, :], node[:, HD2, :], ACT.Sqrt)
                nc.scalar.activation(node[:, NORM2, :], node[:, OUTDEG, :], ACT.Sqrt).then_inc(g_root, 1)
                for n, q in enumerate(DENSE):
                    with act.Fori(0, NB) as b:
                        act.wait_ge(g_turned, b + (NB * n + 1))
                        nc.scalar.activation(turned[:, :, :], banks[:, 5, 0:D].rearrange("p (c n) -> p c n", c=FC), ACT.Copy)
                        nc.scalar.activation(stage[:, :, :], banks[:, 5, D:2 * D].rearrange("p (c n) -> p c n", c=FC), ACT.Copy
                                             ).then_inc(g_feat, 1)
                        act.wait_ge(g_var, b + (NB * n + 1))
                        nc.scalar.activation(std[:, :], mv[:, 1:2], ACT.Sqrt, bias=eps[:, :]).then_inc(g_std, 1)

            def windows_path():
                def score_copies(g, k, i):
                    for u in range(4):
                        half, c = u // 2, u % 2
                        act.wait_ge(hid_done, g * 4 + (u + 9))
                        act.wait_ge(s_done, g * 2 + (half + 1))
                        nc.scalar.activation(hid[:, u, :], banks[:, 2 + u % 2, :], ACT.Relu, bias=b1c[:, c:c + 1]
                                             ).then_inc(hid_evac, 1)
                    act.wait_ge(s_back, g + 1)
                    for half in range(2):
                        act.wait_ge(s_done, g * 2 + (half + 3))
                        nc.scalar.activation(s_part[:, 0, half * 512:half * 512 + 512], banks[0:HEADS, half, :], ACT.Copy).then_inc(s_hi, 1)
                    act.wait_ge(s_left, g + 1)
                    nc.scalar.activation(s_part[:, 1, :], s_rest, ACT.Copy).then_inc(s_mid, 1)

                each_group(act, score_copies)
                act.wait_ge(phase, PHASE["shifted"])
                nc.scalar.activation(s_run, s_run, ACT.Exp).then_inc(exps_done, 1)

                def root(dst, src, done, biased=False):
                    if biased:
                        nc.scalar.activation(dst, src, ACT.Sqrt, bias=eps[:, :]).then_inc(done, 1)
                    else:
                        nc.scalar.activation(dst, src, ACT.Sqrt).then_inc(done, 1)

                def scale(j, b):
                    return node[:, j, bass.ds(b, 1)]

                def x_block(b):
                    return x_rows[:, bass.ds(b, 1), :].rearrange("p a d -> p (a d)")

                def stage_block(q, b):
                    done = blocks_before(q)
                    groups = min(2 * (b + LAG), NG) if isinstance(b, int) else b * 2 + 2 * LAG
                    act.wait_ge(evac_done, groups + (NG * hop_no(q) + 2))
                    act.wait_ge(pe_a, b + (done + 1))
                    if q == PASS_VALUE:
                        nc.scalar.activation(den_stage[:, :], den[:, bass.ds(b * P, P)], ACT.Copy)
                    if q == PASS_SAGE:
                        nc.scalar.activation(x_stage[:, :].unsqueeze(1), x_rows[:, bass.ds(b, 1), :], ACT.Copy)
                    nc.scalar.activation(stage[:, :, :], acc[:, :, bass.ds(b * P, P)], ACT.Copy).then_inc(staged, 1)
                    if q == PASS_VALUE:
                        act.wait_ge(deg_done, b + 1)
                        root(dstd[:, :], blk_sc[:, 16:17], dstd_done)

                def turn_block(q, b):
                    if q in DENSE:
                        bank_sem = pe_a if q == PASS_SAGE else pe_b
                        before = blocks_before(q) + 1 if q == PASS_SAGE else blocks_before(q, TURNED)
                        act.wait_ge(bank_sem, b + (before + 1))
                        nc.scalar.activation(turned[:, :, :], banks[:, B_TURN, 0:D].rearrange("p (c n) -> p c n", c=FC), ACT.Copy
                                             ).then_inc(turn_done, 1)

                def finish_block(q, b):
                    if q in DENSE:
                        act.wait_ge(var_done, b + (blocks_before(q, DENSE) + 1))
                        root(std[:, :], mv[:, 1:2], std_done, biased=True)
                    if q == PASS_SAGE:
                        act.wait_ge(x_done, b + (blocks_before(q, SUMMED) + 1))
                        nc.scalar.activation(h_rows[:, bass.ds(b, 1), :].rearrange("p a d -> p (a d)"), x_block(b), ACT.Copy,
                                             scale=scale(NORM, b)).then_inc(u_ready, 1)
                        return
                    act.wait_ge(tab_free, b + (blocks_before(q, TABLED) + 1))
                    act.wait_ge(x_done, b + (blocks_before(q, SUMMED) + 1))
                    if q == PASS_VALUE:
                        nc.scalar.activation(tab_row[:, :], x_block(b), ACT.Copy, scale=scale(DINV, b)).then_inc(tab_ready, 1)
                    elif q == PASS_GCN1:
                        nc.scalar.activation(tab_row[:, :], rows[:, :], ACT.Copy, scale=scale(DINV, b)).then_inc(tab_ready, 1)
                    else:
                        nc.scalar.activation(tab_row[:, :], x_block(b), ACT.Copy).then_inc(tab_ready, 1)

                def strip_copy(q, i, k):
                    n = BUILDS.index(q) * NG
                    act.wait_ge(strip_done, i * 2 + (n + k + 2))
                    act.wait_ge(c_free, i // 2 + (BUILDS.index(q) * (NG // 4) + 1))
                    at = i % 2 * (2 * SW) + k * SW
                    nc.scalar.activation(c_build[:, 0:SPLIT_BANK, bass.ds(at, SW)],
                                         banks[:, 2, :].rearrange("p (c n) -> p c n", n=SW), ACT.Copy)
                    nc.scalar.activation(c_build[:, SPLIT_BANK:NB, bass.ds(at, SW)],
                                         banks[:, 5, 0:SC - 512].rearrange("p (c n) -> p c n", n=SW), ACT.Copy).then_inc(strip_out, 1)

                for q in SUMMED:
                    if q in BUILDS:
                        with act.Fori(0, LAG) as i:
                            for k in range(2):
                                strip_copy(q, i, k)
                    with act.Fori(LAG, NG // 2) as i:
                        stage_block(q, i - LAG)
                        if q in BUILDS:
                            strip_copy(q, i, 0)
                        turn_block(q, i - LAG)
                        if q in BUILDS:
                            strip_copy(q, i, 1)
                        finish_block(q, i - LAG)
                    for b in range(LOOPED, NB):
                        stage_block(q, b)
                        turn_block(q, b)
                        finish_block(q, b)
                    if q == PASS_GCN1:
                        act.wait_ge(norm_ready, 1)
                        root(node[:, NORM2, :], node[:, OUTDEG, :], norm_root)

                def split(stage_no, b, src, to, factor=None):
                    hi, mid, _ = parts[to]
                    n = stage_no * NB
                    kw = {} if factor is None else {"scale": factor}
                    if factor is not None:
                        act.wait_ge(lo_done, b + n)
                        nc.scalar.activation(tab_row[:, :], src, ACT.Copy, **kw)
                    nc.scalar.activation(hi[:, bass.ds(b, 1), :].rearrange("p a d -> p (a d)"), src, ACT.Copy, **kw).then_inc(hi_done, 1)

                def middle(stage_no, b, to, rest):
                    act.wait_ge(rest1, b + (stage_no * NB + 1))
                    nc.scalar.activation(parts[to][1][:, bass.ds(b, 1), :].rearrange("p a d -> p (a d)"), rest, ACT.Copy
                                         ).then_inc(mid_done, 1)

                act.wait_ge(evac_done, NG * len(SUMMED) + 2)
                act.wait_ge(u_ready, NB)
                act.wait_ge(staged, NB * len(SUMMED))
                act.wait_ge(pe_a, NB * len(SUMMED) + 1)

                def h_block(b):
                    return h_rows[:, bass.ds(b, 1), :].rearrange("p a d -> p (a d)")

                split(0, 0, h_block(0), 0)
                with act.Fori(0, NB - 1) as b:
                    split(0, b + 1, h_block(b + 1), 0)
                    middle(0, b, 0, h_block(b))
                middle(0, NB - 1, 0, h_block(NB - 1))
                for n, q in enumerate(COUNTED):
                    if q != PASS_SG3:
                        def hop_split(b, slot, i):
                            act.wait_ge(hop_done, b + (NB * n + 1))
                            split(n + 1, b, banks[:, slot, 0:D], (n + 1) % 2, scale(NORM2, b))
                            act.wait_ge(hi_done, b + (NB * (n + 1) + 1))
                            act.sem_inc(hop_act, 1)
                            middle(n + 1, b, (n + 1) % 2, ysum[:, :])

                        odd_block_pairs(act, NB * n, hop_split)
                    else:
                        with act.Fori(0, NB) as b:
                            turn_block(q, b)
                            finish_block(q, b)

            choose_path(act, windows_path, any_order_path)

        @block.tensor
        def _(pe):
            for s, n in ((qkv_done, 2), (grp_done, 2), (half_read, 2), (hist_done, 2), (qk_done, 8), (hid_done, 8), (s_done, 2), (s_back, 1),
                         (pe_a, 1), (strip_done, 1)):
                pe.sem_inc(s, n)
            pe.wait_ge(w_in, 48)

            def qkv(b, k, i):
                pe.wait_ge(xt_in[k], i * 16 + 16)
                pe.wait_ge(qkv_act, b + 1)
                for n in range(3):
                    for c in range(FC):
                        last = nc.tensor.matmul(banks[:, 3 * k + n, 0:D], xst[:, k, c, :], w_qkv[:, c, n * D:(n + 1) * D],
                                                start=(c == 0), stop=(c == FC - 1))
                last.then_inc(qkv_done, 1)

            each_block_pair(pe, qkv)
            pe.wait_ge(qkv_act, NB + 2)
            pe.wait_ge(setup_done, 1)
            nc.tensor.transpose(banks[0:1, 7, 0:P], part_f[:, :], ident[:, :])
            nc.tensor.transpose(banks[0:1, 7, P:2 * P], broken[:, 0:1], ident[:, :]).then_inc(pe_small, 1)

            def any_order_path():
                pe.sem_inc(g_mlp, 1)
                with pe.Fori(0, NT) as t:
                    pe.wait_ge(g_ef_in, t * 16 + 16)
                    pe.wait_ge(g_relu, t + 1)
                    for c in range(FC):
                        last = nc.tensor.matmul(banks[:, 0, c * P:(c + 1) * P], w1[:, c * P:(c + 1) * P], g_ef, start=True, stop=True)
                    last.then_inc(g_hid, 1)
                    pe.wait_ge(g_relu, t + 2)
                    pe.wait_ge(g_scored, t + 1)
                    for c in range(FC):
                        last = nc.tensor.matmul(banks[:, 1, 0:HEADS], g_hidden[:, c, :], w2[:, c, :], start=(c == 0), stop=(c == FC - 1))
                    last.then_inc(g_mlp, 1)

                def g_product(n, q):
                    with pe.Fori(0, NB) as b:
                        pe.wait_ge(g_rows, b + (NB * n + 1))
                        for c in range(FC):
                            nc.tensor.transpose(banks[:, 5, c * P:(c + 1) * P], rows[:, c * P:(c + 1) * P], ident[:, :])
                        for c in range(FC):
                            last = nc.tensor.transpose(banks[:, 5, D + c * P:D + (c + 1) * P], x_stage[:, c * P:(c + 1) * P], ident[:, :])
                        last.then_inc(g_turned, 1)
                        pe.wait_ge(g_feat, b + (NB * n + 1))
                        if q == PASS_SAGE:
                            for c in range(FC):
                                nc.tensor.matmul(banks[:, 6, 0:D], turned[:, c, :], w_lin[:, 2, c, :], start=(c == 0), stop=False)
                            for c in range(FC):
                                last = nc.tensor.matmul(banks[:, 6, 0:D], stage[:, c, :], w_lin[:, 3, c, :], start=False, stop=(c == FC - 1))
                        else:
                            for c in range(FC):
                                last = nc.tensor.matmul(banks[:, 6, 0:D], turned[:, c, :], w_lin[:, DENSE[q], c, :],
                                                        start=(c == 0), stop=(c == FC - 1))
                        last.then_inc(g_prod, 1)

                pe.wait_ge(g_zeroed, 1)
                for n, q in enumerate(HOPS):
                    wide = D + XW + 1 if q == PASS_VALUE else D
                    with pe.Fori(0, SETS) as s:
                        pe.wait_ge(g_evac, s + (SETS * n + 1))
                        for j in range(SET_BLOCKS):
                            nc.tensor.matmul(banks[:, j, 0:wide], zero_b[:, :], g_zero[:, 0:wide], start=True, stop=False)
                        with pe.Fori(0, NT) as t:
                            pe.wait_ge(g_msg, s * NT + t + (SETS * NT * n + 1))
                            for j in range(SET_BLOCKS):
                                last = nc.tensor.matmul(banks[:, j, 0:D], g_onehot[:, 0, j, :], g_rows_w, start=False, stop=False,
                                                        skip_group_check=True)
                                if q == PASS_VALUE:
                                    nc.tensor.matmul(banks[:, j, D:D + XW], g_onehot[:, 0, j, :], xcol[:, 0, 0, :], start=False, stop=False,
                                                     skip_group_check=True)
                                    last = nc.tensor.matmul(banks[:, j, D + XW:D + XW + 1], g_onehot[:, 1, j, :], xcol[:, 0, 0, HEADS:HEADS + 1],
                                                            start=False, stop=False, skip_group_check=True)
                            last.then_inc(g_used, 1)
                        for j in range(SET_BLOCKS):
                            last = nc.tensor.matmul(banks[:, j, 0:wide], zero_b[:, :], g_zero[:, 0:wide], start=False, stop=True)
                        last.then_inc(g_closed, 1)
                    if q in DENSE:
                        g_product(list(DENSE).index(q), q)

            def windows_path():
                def scores_back(g):
                    pe.wait_ge(s_low, g + 1)
                    pe.wait_ge(s_read, g + 1)
                    for t in range(TG):
                        for j in range(3):
                            last = nc.tensor.matmul(banks[:, 6, t * HEADS:(t + 1) * HEADS], s_part[:, j, t * P:(t + 1) * P], ident_b,
                                                    start=(j == 0), stop=(j == 2))
                    last.then_inc(s_back, 1)

                def scores(g, k, i, first=False):
                    def hidden(half):
                        for c in range(2):
                            u = half * 2 + c
                            pe.wait_ge(hid_evac, g * 4 + (u + 7))
                            nc.tensor.matmul(banks[:, 2 + u % 2, :], w1[:, c * P:(c + 1) * P],
                                             ef[:, k, half * 512:half * 512 + 512], start=True, stop=True).then_inc(hid_done, 1)

                    def mlp_scores(half):
                        if not first:
                            pe.wait_ge(s_left, g)
                        pe.wait_ge(hid_evac, g * 4 + (half * 2 + 10))
                        for c in range(2):
                            last = nc.tensor.matmul(banks[0:HEADS, half, :], w2[:, c, :], hid[:, half * 2 + c, :], start=(c == 0), stop=(c == 1))
                        last.then_inc(s_done, 1)

                    def q_rows(pair):
                        pe.wait_ge(qk_read, g * 4 + Q_READ[pair])
                        for t in range(2):
                            tile = pair * 2 + t
                            last = nc.tensor.matmul(banks[:, Q_BANKS[pair], t * D:(t + 1) * D], oht[:, k, tile * P:(tile + 1) * P],
                                                    q_win[:, k, :], start=True, stop=True)
                        last.then_inc(qk_done, 1)

                    pe.wait_ge(ef_done[k], i * 16 + 16)
                    hidden(0)
                    hidden(1)
                    pe.wait_ge(oh_ready, g + 1)
                    pe.wait_ge(qwin_done[k], i * 16 + 16)
                    q_rows(0)
                    q_rows(1)
                    if not first:
                        scores_back(g - 1)
                    mlp_scores(0)
                    mlp_scores(1)
                    q_rows(2)
                    q_rows(3)

                scores(0, 0, 0, first=True)
                scores(1, 1, 0)
                with pe.Fori(1, NG // 2) as i:
                    for k in range(2):
                        scores(i * 2 + k, k, i)
                scores_back(NG - 1)

                for n in range(2):
                    pe.wait_ge(phase, PHASE["tails_f" if n == 0 else "tails_b"])
                    nc.tensor.transpose(banks[0:HEADS, 7, 0:P], carry[:, 2 * n, :], ident[:, :]).then_inc(pe_small, 1)
                    pe.wait_ge(phase, PHASE["chain_f" if n == 0 else "chain_b"])
                    nc.tensor.transpose(banks[:, 7, P:P + HEADS], tails[:, 2 * n + 1, :], ident[0:HEADS, 0:HEADS]).then_inc(pe_small, 1)

                def group_sums(q, g, k, i):
                    h = hop_no(q)
                    pe.wait_ge(oh_ready, g + (NG * q + 1))
                    pe.wait_ge(evac_done, g + (NG * h + 1))
                    for t in range(TG):
                        half, t_half = t // (TG // 2), t % (TG // 2)
                        if t_half == 0 and q == PASS_VALUE:
                            pe.wait_ge(msg_ready, g * 2 + (half + 1))
                        elif t_half == 0:
                            gathered(pe, k, half, i, SUMMED.index(q) + 1)
                        for c in range(FC):
                            last = nc.tensor.matmul(banks[:, 3 * k + c, 0:P], row_slot[:, k, t, c * P:(c + 1) * P], onehot[:, k, t, :],
                                                    start=(t == 0), stop=(t == TG - 1))
                        if q == PASS_VALUE:
                            last = nc.tensor.matmul(banks[0:XW, 3 * k + 2, 0:P], xcol[:, k, t, :], onehot[:, k, t, :],
                                                    start=(t == 0), stop=(t == TG - 1))
                        if t == TG // 2 - 1:
                            last.then_inc(half_read, 1)
                    last.then_inc(grp_done, 1)
                    if q == PASS_GCN1:
                        pe.wait_ge(hist_oh, g + 1)
                        for t in range(TG):
                            last = nc.tensor.matmul(banks[:, 2, 0:32], oh_lo[:, k, t, :], oh_hi[:, k, t, :], start=False, stop=False,
                                                    skip_group_check=True)
                        last.then_inc(hist_done, 1)

                def turn_rows(q, b):
                    done = blocks_before(q)
                    pe.wait_ge(staged, b + (done + 1))
                    pe.wait_ge(blk_done, b + (done + 1))
                    if q == PASS_VALUE:
                        pe.sem_inc(pe_step, 1)
                        nc.tensor.transpose(banks[:, B_ROWS, D:D + XW], den_stage[:, :], ident[0:XW, 0:XW])
                    for c in range(FC):
                        if q == PASS_SAGE:
                            nc.tensor.transpose(banks[:, B_TURN, c * P:(c + 1) * P], x_stage[:, c * P:(c + 1) * P], ident[:, :])
                    for c in range(FC):
                        if q == PASS_SAGE:
                            last = nc.tensor.matmul(banks[:, B_ROWS, 0:D], stage[:, c, :], w_lin[:, 2, c, :],
                                                    start=(c == 0), stop=(c == FC - 1))
                        else:
                            last = nc.tensor.transpose(banks[:, B_ROWS, c * P:(c + 1) * P], stage[:, c, :], ident[:, :])
                    last.then_inc(pe_a, 1)

                def turn_back(q, b):
                    if q in TURNED:
                        pe.wait_ge(rows_done, b + (blocks_before(q, TURNED) + 1))
                        for c in range(FC):
                            last = nc.tensor.transpose(banks[:, B_TURN, c * P:(c + 1) * P], rows[:, c * P:(c + 1) * P], ident[:, :])
                        last.then_inc(pe_b, 1)

                def product(q, b):
                    if q in DENSE:
                        pe.wait_ge(turn_done, b + (blocks_before(q, DENSE) + 1))
                        if q == PASS_SAGE:
                            pe.wait_ge(rows_done_sage, b + 1)
                        for c in range(FC):
                            last = nc.tensor.matmul(banks[:, B_ROWS, 0:D], turned[:, c, :], w_lin[:, DENSE[q], c, :],
                                                    start=(c == 0), stop=(c == FC - 1))
                        last.then_inc(pe_c, 1)

                def strip(q, i, k):
                    n = BUILDS.index(q) * NG
                    pe.wait_ge(oh_strip, i * 2 + (n + k + 1))
                    pe.wait_ge(strip_out, i * 2 + (n + k + 1))
                    for t in range(ST):
                        nc.tensor.matmul(banks[:, 2, :], oh_src[:, t, :], oh_key[:, t, 0:512], start=(t == 0), stop=(t == ST - 1))
                        last = nc.tensor.matmul(banks[:, 5, 0:SC - 512], oh_src[:, t, :], oh_key[:, t, 512:SC],
                                                start=(t == 0), stop=(t == ST - 1))
                    last.then_inc(strip_done, 1)

                for q in SUMMED:
                    if q == PASS_GCN1:
                        nc.tensor.matmul(banks[:, 2, 0:32], zero_b[:, :], zero_b[:, 0:32], start=True, stop=False)
                    with pe.Fori(0, LAG) as i:
                        for k in range(2):
                            group_sums(q, i * 2 + k, k, i)
                            if q in BUILDS:
                                strip(q, i, k)
                    with pe.Fori(LAG, NG // 2) as i:
                        group_sums(q, i * 2, 0, i)
                        turn_rows(q, i - LAG)
                        if q in BUILDS:
                            strip(q, i, 0)
                        group_sums(q, i * 2 + 1, 1, i)
                        turn_back(q, i - LAG)
                        product(q, i - LAG)
                        if q in BUILDS:
                            strip(q, i, 1)
                    if q == PASS_GCN1:
                        nc.tensor.matmul(banks[:, 2, 0:32], zero_b[:, :], zero_b[:, 0:32], start=False, stop=True
                                         ).then_inc(hist_done, 1)
                    for b in range(LOOPED, NB):
                        turn_rows(q, b)
                        turn_back(q, b)
                        product(q, b)

                for n, q in enumerate(COUNTED):
                    def counted(b, k, i, first):
                        t = NB * n
                        slot = (t + k) % 2
                        pe.wait_ge(c_in[slot], i * 16 + (16 * ((t + k) // 2) + 16))
                        pe.wait_ge(hop_dve, b + (t + 1))
                        if q != PASS_SG3:
                            pe.wait_ge(hop_act, b + (t + 1))
                        else:
                            pe.wait_ge(hop_act, 2 * NB + 2)

                        for c in range(NB):
                            if first:
                                pe.wait_ge(lo_done, NB * n + c + 1)
                            for j in range(3):
                                last = nc.tensor.matmul(banks[:, slot, 0:D], c_slot[:, slot, c, :], parts[n % 2][j][:, c, :],
                                                        start=(c == 0 and j == 0), stop=(c == NB - 1 and j == 2))
                        last.then_inc(hop_done, 1)

                    counted(0, 0, 0, True)
                    counted(1, 1, 0, False)
                    if q == PASS_SG3:
                        turn_back(q, 0)
                        product(q, 0)
                    with pe.Fori(1, NB // 2) as i:
                        for k in range(2):
                            counted(i * 2 + k, k, i, False)
                            if q == PASS_SG3:
                                turn_back(q, i * 2 + (k - 1))
                                product(q, i * 2 + (k - 1))
                    counted(NB - 1, 0, NB // 2, False)
                    if q == PASS_SG3:
                        for b in (NB - 2, NB - 1):
                            turn_back(q, b)
                            product(q, b)

            choose_path(pe, windows_path, any_order_path)

        @block.vector
        def _(dve):
            class Chain:
                def __init__(self, counted):
                    self.counted, self.at, self.n = counted, 0, 0

                def link(self, ins):
                    self.n += 1
                    ins.then_inc(self.counted, 1)
                    dve.wait_ge(self.counted, self.at + self.n)

                def enter(self, at):
                    self.at, self.n = at, 0

                def leave(self):
                    n, self.n = self.n, 0
                    return n

            def chain_total(c):
                c.enter(c.at + c.n)
                return c.at

            LINKS = {PASS_VALUE: 12, PASS_GCN1: 0, PASS_GCN2: 5, PASS_SAGE: 4, PASS_SG1: 0, PASS_SG2: 0, PASS_SG3: 4}
            chain = Chain(link_sem)
            link = chain.link

            def advance(name):
                dve.wait_ge(phase, PHASE[name])

            for s, n in ((evac_done, 2), (qk_read, 8), (s_read, 1), (red_done, 8), (blk_done, 1), (hop_dve, 2)):
                dve.sem_inc(s, n)
            dve.wait_ge(consts_done, 2)
            dve.wait_ge(loaded, 16 * N_LOADS)
            nc.vector.memset(zero_b[:, :], 0.0)
            nc.vector.memset(eps[:, :], EPS)
            nc.vector.memset(xcol[:, :, :, HEADS:HEADS + 1], 1.0)
            nc.vector.tensor_copy(part_f[:, :], part_i[:, :])
            link(nc.vector.tensor_copy(iota_f[:, :], iota_i[:, :]))
            nc.vector.tensor_scalar(ident[:, :], iota_f[:, :], part_f[:, :], None, ALU.is_equal)
            nc.vector.tensor_scalar(ident_b, iota_f[0:HEADS, 0:HEADS], part_f[0:HEADS, :], None, ALU.is_equal)
            nc.vector.tensor_tensor(rel[:, :, :], dst_i[:, :].rearrange("p (g t) -> p g t", g=NG),
                                    base_i[:, :].unsqueeze(2).to_broadcast([P, NG, TG]), ALU.subtract)
            nc.vector.tensor_scalar(win_node[:, :], base_i[:, :], part_f[:, :], None, ALU.add)
            lo_i = gathf[:, 0:NT].bitcast(I32)
            hi_i = gathf[:, NT:2 * NT].bitcast(I32)
            nc.vector.tensor_scalar(lo_i, edge_t[:, 0, :], P - 1, None, ALU.bitwise_and)
            link(nc.vector.tensor_scalar(hi_i, edge_t[:, 0, :], 7, None, ALU.arith_shift_right))
            nc.vector.tensor_copy(src_lo[:, :], lo_i)
            link(nc.vector.tensor_copy(src_hi[:, :], hi_i))
            link(nc.vector.tensor_scalar(part_f[:, :], part_f[:, :], float(SW), None, ALU.mult))
            link(nc.vector.tensor_scalar(last_lt, last_i, part_f[:, :], None, ALU.is_lt))
            link(nc.vector.tensor_reduce(part_f[:, :], last_lt, AX.X, ALU.add))
            link(nc.vector.tensor_scalar(part_f[:, :], part_f[:, :], float(NT - ST), None, ALU.min))
            V = nc.vector
            def count_broken(width, *steps):
                for step in steps:
                    link(step(check[:, 0:width]))
                link(V.tensor_reduce(broken[:, 1:2], check[:, 0:width], AX.X, ALU.add))
                link(V.tensor_tensor(broken[:, 0:1], broken[:, 0:1], broken[:, 1:2], ALU.add))

            link(V.tensor_copy(broken[:, 0:1], part_i[:, :]))
            link(V.tensor_scalar(broken[:, 0:1], broken[:, 0:1], float(SW), float(SW), ALU.mult, ALU.add))
            link(V.tensor_scalar(check, first_i, broken[:, 0:1], None, ALU.is_lt))
            link(V.tensor_reduce(broken[:, 0:1], check, AX.X, ALU.add))
            link(V.tensor_tensor(broken[:, 0:1], broken[:, 0:1], part_f[:, :], ALU.subtract))
            link(V.tensor_scalar(broken[:, 0:1], broken[:, 0:1], float(ST), None, ALU.is_gt))
            count_broken(PJ - 1, lambda c: V.tensor_tensor(c, run_i[:, 1:PJ], run_i[:, 0:PJ - 1], ALU.is_lt))
            count_broken(P - 1, lambda c: V.memset(c, 0.0),
                         lambda c: V.tensor_tensor(c[0:HEADS, :], ends_i[:, 0, 1:P], ends_i[:, 1, 0:P - 1], ALU.is_lt))
            count_broken(NT, lambda c: V.tensor_tensor(c, first_i, last_i, ALU.is_equal))
            count_broken(NG, lambda c: V.tensor_tensor(c, last_i.rearrange("p (g t) -> p g t", t=TG)[:, :, TG - 1], base_i[:, :], ALU.subtract),
                         lambda c: V.tensor_scalar(c, c, float(P), None, ALU.is_ge))
            count_broken(LOOPED, lambda c: V.tensor_scalar(c, iota_f[:, 1:LOOPED + 1], float(P), None, ALU.mult),
                         lambda c: V.tensor_tensor(c, base_i[:, :].rearrange("p (h k) -> p h k", k=2)[:, LAG:LAG + LOOPED, 0], c, ALU.is_lt))
            link(nc.vector.tensor_tensor(bias[:, 3, :], bias[:, 3, :], bias[:, 3, :], ALU.add))
            nc.vector.tensor_tensor(bias[:, 3, :], bias[:, 3, :], bias[:, 3, :], ALU.add).then_inc(setup_done, 1)

            dve.wait_ge(pe_small, 1)
            link(nc.vector.tensor_copy(tile0_i[:, :], banks[0:1, 7, 0:P]))
            link(nc.vector.tensor_reduce(path_f[:, :], banks[0:1, 7, P:2 * P], AX.X, ALU.add))
            nc.vector.tensor_scalar(path_i[:, :], path_f[:, :], 0.5, None, ALU.is_lt).then_inc(path_known, 1)

            weights = {PASS_GCN1: ew, PASS_GCN2: ew, PASS_SAGE: ew1}

            def row(t, b):
                return t[:, bass.ds(b, 1), :].rearrange("p a d -> p (a d)")

            def any_order_path():
                g_chain = Chain(g_link)
                g_l = g_chain.link
                dve.sem_inc(g_evac, 1)
                dve.wait_ge(b2_loaded, 32)
                dve.wait_ge(qkv_free, NB + 3)
                with dve.Fori(0, NT) as t:
                    g_chain.enter(t * 3)
                    dve.wait_ge(g_gath, t * 32 + 32)
                    g_l(V.tensor_tensor(g_tmp, g_q, g_kv[:, 0:D], ALU.mult))
                    g_l(V.tensor_reduce(g_e, g_tmp.rearrange("p (h d) -> p h d", h=HEADS), AX.X, ALU.add))
                    dve.wait_ge(g_mlp, t + 2)
                    g_l(V.scalar_tensor_tensor(g_e, g_e, float(HD) ** -0.5, banks[:, 1, 0:HEADS], ALU.mult, ALU.add))
                    V.tensor_tensor(score[:, bass.ds(t * HEADS, HEADS)], g_e, b2b[:, :], ALU.add).then_inc(g_scored, 1)
                g_chain.enter(NT * 3)
                dve.wait_ge(g_scored, NT + 1)
                dve.sem_inc(g_stage, 1)

                g_l(V.memset(g_max, -BIG))
                g_l(V.tensor_scalar(broken[:, 0:1], part_i[:, :], 1.0, None, ALU.mult))
                g_l(V.tensor_scalar(g_node, iota_f[:, 0:NB], float(P), broken[:, 0:1], ALU.mult, ALU.add))
                with dve.Fori(0, NT) as t:
                    dve.wait_ge(g_spread, t * 32 + 32)
                    dve.sem_inc(dve_step, 1)
                    with dve.Fori(0, NB) as b:
                        at = t * NB + b + 1
                        V.tensor_scalar(g_mask, g_dst, g_node[:, bass.ds(b, 1)], 1.0, ALU.is_equal, ALU.subtract).then_inc(g_mask_ok, 1)
                        dve.wait_ge(g_mask_ok, at)
                        V.scalar_tensor_tensor(g_masked, g_mask.unsqueeze(2).to_broadcast([P, P, HEADS]), BIG,
                                               g_s.rearrange("p (e h) -> p e h", h=HEADS), ALU.mult, ALU.add).then_inc(g_masked_ok, 1)
                        dve.wait_ge(g_masked_ok, at)
                        V.tensor_reduce(g_e, g_masked.rearrange("p e h -> p h e"), AX.X, ALU.max).then_inc(g_red_ok, 1)
                        dve.wait_ge(g_red_ok, at)
                        m_b = g_max[:, bass.ds(b, 1), :].rearrange("p a h -> p (a h)")
                        V.tensor_tensor(m_b, m_b, g_e, ALU.max).then_inc(g_max_ok, 1)
                        dve.wait_ge(g_max_ok, at)
                    dve.sem_inc(g_maxed, 1)
                dve.sem_inc(g_stage, 1)

                for j in range(SET_BLOCKS):
                    g_l(V.tensor_scalar(g_iota[:, j * P:(j + 1) * P], iota_f[:, :], float(j * P), None, ALU.add))
                g_l(V.tensor_scalar(g_first, iota_f[:, 0:SETS], float(SET_BLOCKS * P), None, ALU.mult))
                g_l(V.memset(g_zero, 0.0))
                dve.sem_inc(g_zeroed, 1)

                def all_blocks(j):
                    return node[:, j, :].unsqueeze(2).to_broadcast([P, NB, D])

                def hop_sums(n, q):
                    with dve.Fori(0, SETS) as s:
                        with dve.Fori(0, NT // 2) as j:
                            for k in range(2):
                                t = j * 2 + k
                                col = bass.ds(t, 1)
                                dve.wait_ge(g_used, s * NT + j * 2 + (k + SETS * NT * n + 1))
                                V.tensor_tensor(g_rel[:, 0:1], dst_i[:, col], g_first[:, bass.ds(s, 1)], ALU.subtract)
                                V.tensor_tensor(g_rel[:, 1:2], src_i[:, col], g_first[:, bass.ds(s, 1)], ALU.subtract).then_inc(g_rel_ok, 1)
                                dve.wait_ge(g_rel_ok, s * NT + j * 2 + (k + SETS * NT * n + 1))
                                V.tensor_scalar(g_onehot[:, 0, :, :].rearrange("p j n -> p (j n)"), g_iota, g_rel[:, 0:1], None, ALU.is_equal)
                                dve.wait_ge(g_in[q][k], s * (8 * NT) + j * 16 + 16)
                                if q == PASS_VALUE:
                                    V.tensor_scalar(g_onehot[:, 1, :, :].rearrange("p j n -> p (j n)"), g_iota, g_rel[:, 1:2], None, ALU.is_equal)
                                    dve.wait_ge(g_m_in[k], s * (8 * NT) + j * 16 + 16)
                                    V.tensor_tensor(g_e, score[:, bass.ds(t * HEADS, HEADS)], g_m, ALU.subtract).then_inc(g_shift, 1)
                                    V.tensor_copy(xcol[:, 0, 0, HEADS + 1:XW], ew[:, col])
                                    dve.wait_ge(g_exp, s * NT + j * 2 + (k + 1))
                                    V.tensor_tensor(g_rows_w.rearrange("p (h d) -> p h d", h=HEADS),
                                                    g_kv[:, D:2 * D].rearrange("p (h d) -> p h d", h=HEADS),
                                                    xcol[:, 0, 0, 0:HEADS].unsqueeze(2).to_broadcast([P, HEADS, HD]), ALU.mult).then_inc(g_msg, 1)
                                elif q in weights:
                                    V.tensor_scalar(g_rows_w, g_q, weights[q][:, col], None, ALU.mult).then_inc(g_msg, 1)
                                else:
                                    V.tensor_copy(g_rows_w, g_q).then_inc(g_msg, 1)
                        dve.wait_ge(g_closed, s + (SETS * n + 1))
                        dve.sem_inc(dve_step, 1)
                        if q == PASS_VALUE:
                            V.tensor_copy(g_extra[:, bass.ds(s * SET_BLOCKS, SET_BLOCKS), :], banks[:, 0:SET_BLOCKS, D:D + XW + 1])
                        V.tensor_copy(g_acc[:, bass.ds(s * SET_BLOCKS, SET_BLOCKS), :], banks[:, 0:SET_BLOCKS, 0:D]).then_inc(g_evac, 1)
                    dve.wait_ge(g_evac, SETS * (n + 1) + 1)

                def product_and_norm(n, q):
                    start = chain_total(g_chain)
                    size = 7 if q == PASS_SG3 else 6
                    with dve.Fori(0, NB) as b:
                        g_chain.enter(b * size + start)
                        x_b = row(x_rows, b)
                        sums = x_b if q == PASS_SG3 else row(g_acc, b)
                        dve.sem_inc(dve_step, 1)
                        V.tensor_copy(rows[:, :], sums)
                        g_l(V.tensor_copy(x_stage[:, :], x_b))
                        dve.sem_inc(g_rows, 1)
                        dve.wait_ge(g_prod, b + (NB * n + 1))
                        g_l(V.tensor_tensor(ysum[:, :], banks[:, 6, 0:D], bias[:, n, :], ALU.add))
                        if q == PASS_SG3:
                            g_l(V.tensor_scalar(ysum[:, :], ysum[:, :], 0.0, None, ALU.max))
                            g_l(V.tensor_tensor(ysum[:, :], ysum[:, :], row(r_rows, b), ALU.add))
                        else:
                            g_l(V.tensor_tensor(ysum[:, :], ysum[:, :], x_b, ALU.add))
                        g_l(V.bn_stats(stats[:, :], ysum[:, :]))
                        dve.sem_inc(dve_step, 1)
                        V.bn_aggr(mv[:, :], stats[:, :]).then_inc(g_var, 1)
                        dve.wait_ge(g_std, b + (NB * n + 1))
                        g_l(V.reciprocal(rstd[:, :], std[:, :]))
                        g_l(V.tensor_scalar(x_b, ysum[:, :], mv[:, 0:1], rstd[:, :], ALU.subtract, ALU.mult))
                        assert g_chain.leave() == size
                    g_chain.enter(start + NB * size)

                for n, q in enumerate(HOPS):
                    hop_sums(n, q)
                    if q == PASS_VALUE:
                        weight_sum = g_extra[:, :, XW - 1]
                        g_l(V.tensor_scalar(g_extra[:, :, 0:HEADS], g_extra[:, :, 0:HEADS], 1e-30, None, ALU.max))
                        g_l(V.reciprocal(g_extra[:, :, 0:HEADS], g_extra[:, :, 0:HEADS]))
                        acc4 = g_acc.rearrange("p b (h d) -> p b h d", h=HEADS)
                        g_l(V.tensor_tensor(acc4, acc4, g_extra[:, :, 0:HEADS].unsqueeze(3).to_broadcast([P, NB, HEADS, HD]), ALU.mult))
                        g_l(V.tensor_scalar(node[:, RDEG, :], g_extra[:, :, HEADS], 1.0, None, ALU.max))
                        g_l(V.reciprocal(node[:, RDEG, :], node[:, RDEG, :]))
                        g_l(V.tensor_scalar(weight_sum, weight_sum, 1.0, None, ALU.add))
                        g_l(V.tensor_scalar(node[:, HD2, :], weight_sum, 1e-12, None, ALU.max))
                        g_l(V.tensor_scalar(weight_sum, weight_sum, 0.0, None, ALU.is_gt))
                        g_l(V.tensor_scalar(node[:, OUTDEG, :], g_extra[:, :, XW], 1.0, None, ALU.max))
                        dve.sem_inc(g_deg, 1)
                        dve.wait_ge(g_root, 1)
                        g_l(V.reciprocal(node[:, DINV, :], node[:, DINV, :]))
                        g_l(V.tensor_tensor(node[:, DINV, :], node[:, DINV, :], weight_sum, ALU.mult))
                        g_l(V.tensor_scalar(node[:, HDINV, :], node[:, DINV, :], 0.5, None, ALU.mult))
                        g_l(V.tensor_tensor(node[:, HD2, :], node[:, HDINV, :], node[:, DINV, :], ALU.mult))
                        g_l(V.tensor_scalar(node[:, HD2P, :], node[:, HD2, :], 0.5, None, ALU.add))
                        g_l(V.reciprocal(node[:, NORM, :], node[:, NORM2, :]))
                        g_l(V.tensor_tensor(node[:, NORM2, :], node[:, NORM, :], node[:, NORM, :], ALU.mult))
                        product_and_norm(0, q)
                        g_l(V.tensor_tensor(h_rows[:, :, :], x_rows[:, :, :], all_blocks(HD2P), ALU.mult))
                        g_l(V.tensor_scalar(r_rows[:, :, :], x_rows[:, :, :], 0.5, None, ALU.mult))
                        g_l(V.tensor_tensor(g_acc, x_rows[:, :, :], all_blocks(DINV), ALU.mult))
                    elif q == PASS_GCN1:
                        g_l(V.tensor_tensor(g_acc, g_acc, all_blocks(HDINV), ALU.mult))
                        g_l(V.tensor_tensor(g_acc, g_acc, h_rows[:, :, :], ALU.add))
                        g_l(V.tensor_tensor(h_rows[:, :, :], g_acc, all_blocks(HD2), ALU.mult))
                        g_l(V.tensor_tensor(h_rows[:, :, :], h_rows[:, :, :], r_rows[:, :, :], ALU.add))
                        g_l(V.tensor_tensor(g_acc, g_acc, all_blocks(DINV), ALU.mult))
                    elif q == PASS_GCN2:
                        g_l(V.tensor_tensor(g_acc, g_acc, all_blocks(HDINV), ALU.mult))
                        g_l(V.tensor_tensor(g_acc, g_acc, h_rows[:, :, :], ALU.add))
                        g_l(V.tensor_scalar(g_acc, g_acc, 0.0, None, ALU.max))
                        product_and_norm(1, q)
                    elif q == PASS_SAGE:
                        g_l(V.tensor_tensor(g_acc, g_acc, all_blocks(RDEG), ALU.mult))
                        product_and_norm(2, q)
                        g_l(V.tensor_copy(r_rows[:, :, :], x_rows[:, :, :]))
                        g_l(V.tensor_tensor(g_acc, x_rows[:, :, :], all_blocks(NORM), ALU.mult))
                    else:
                        g_l(V.tensor_tensor(h_rows[:, :, :], g_acc, all_blocks(NORM), ALU.mult))
                        g_l(V.tensor_tensor(x_rows[:, :, :], x_rows[:, :, :], h_rows[:, :, :], ALU.add))
                        if q == PASS_SG3:
                            product_and_norm(3, q)
                        else:
                            g_l(V.tensor_tensor(g_acc, h_rows[:, :, :], all_blocks(NORM), ALU.mult))
                    dve.sem_inc(g_stage, 1)

            def windows_path():
                def make_onehot(q, g, k):
                    w = weights.get(q)
                    for t in range(TG):
                        r = rel[:, bass.ds(g, 1), t:t + 1].rearrange("p a b -> p (a b)")
                        if w is None:
                            last = nc.vector.tensor_scalar(onehot[:, k, t, :], iota_f[:, :], r, None, ALU.is_equal)
                        else:
                            last = nc.vector.tensor_scalar(onehot[:, k, t, :], iota_f[:, :], r,
                                                           w[:, bass.ds(g * TG + t, 1)], ALU.is_equal, ALU.mult)
                    last.then_inc(oh_ready, 1)

                def score_prepare(g, k, i):
                    dve.wait_ge(qk_done, g * 4 + 4)
                    dve.wait_ge(dst_in[k], i * 16 + 16)
                    nc.vector.tensor_scalar(oht[:, k, :], dst_row[:, k, :], win_node[:, bass.ds(g, 1)], None, ALU.is_equal
                                            ).then_inc(oh_ready, 1)

                def pair_scores(g, k, i, pair):
                    if pair % 2 == 0:
                        gathered(dve, k, pair // 2, i, 0)
                    dve.wait_ge(qk_done, g * 4 + (pair + 9))
                    dve.wait_ge(red_done, g * 4 + (pair + 7))
                    nc.vector.tensor_tensor(prod[:, pair % 2, :, :], banks[:, Q_BANKS[pair], :].rearrange("p (t d) -> p t d", t=2),
                                            row_slot[:, k, 2 * pair:2 * pair + 2, :], ALU.mult).then_inc(qk_read, 1)
                    dve.wait_ge(qk_read, g * 4 + (pair + 9))
                    nc.vector.tensor_reduce(score[:, bass.ds(g * (TG * HEADS) + pair * 2 * HEADS, 2 * HEADS)],
                                            prod[:, pair % 2, :, :].rearrange("p t (h d) -> p (t h) d", h=HEADS),
                                            AX.X, ALU.add).then_inc(red_done, 1)

                def add_mlp(g):
                    dve.wait_ge(red_done, g * 4 + 12)
                    dve.wait_ge(s_back, g + 2)
                    part = score[:, bass.ds(g * (TG * HEADS), TG * HEADS)]
                    nc.vector.scalar_tensor_tensor(part, part, float(HD) ** -0.5, banks[:, 6, 0:TG * HEADS], ALU.mult, ALU.add
                                                   ).then_inc(s_read, 1)

                def score_finish(g, k, i, first=False, last=False):
                    pair_scores(g, k, i, 0)
                    pair_scores(g, k, i, 1)
                    if not last:
                        score_prepare(g + 1, 1 - k, i + k)
                    if not first:
                        add_mlp(g - 1)
                    dve.wait_ge(s_hi, g * 2 + 2)
                    nc.vector.tensor_tensor(s_rest.rearrange("h (a e) -> h a e", a=2), banks[0:HEADS, 0:2, :],
                                            s_part[:, 0, :].rearrange("h (a e) -> h a e", a=2), ALU.subtract).then_inc(s_left, 1)
                    pair_scores(g, k, i, 2)
                    pair_scores(g, k, i, 3)
                    dve.wait_ge(s_mid, g + 1)
                    nc.vector.tensor_tensor(s_part[:, 2, :], s_rest, s_part[:, 1, :], ALU.subtract).then_inc(s_low, 1)

                dve.wait_ge(qkv_free, NB + 3)
                score_prepare(0, 0, 0)
                score_finish(0, 0, 0, first=True)
                score_finish(1, 1, 0)
                with dve.Fori(1, NG // 2 - 1) as i:
                    for k in range(2):
                        score_finish(i * 2 + k, k, i)
                score_finish(NG - 2, 0, NG // 2 - 1)
                score_finish(NG - 1, 1, NG // 2 - 1, last=True)
                add_mlp(NG - 1)
                dve.wait_ge(s_read, NG + 1)
                dve.wait_ge(b2_loaded, 32)
                s3 = score.rearrange("p (t h) -> p t h", h=HEADS)
                nc.vector.tensor_tensor(s3, s3, b2b[:, :].unsqueeze(1).to_broadcast([P, NT, HEADS]), ALU.add).then_inc(phase, 1)

                dve.wait_ge(moved, 48)
                first, last_ = ends[:, 0, :], ends[:, 1, :]
                link(nc.vector.tensor_copy(ends[:, :, :], ends_i[:, :, :]))
                link(nc.vector.tensor_copy(dst_run, dst_run_i))

                def to_mask(m):
                    link(nc.vector.tensor_scalar(m, m, BIG, -BIG, ALU.mult, ALU.add))

                nc.vector.memset(mask_f[:, 0:1], 1.0)
                link(nc.vector.tensor_tensor(mask_f[:, 1:PJ], dst_run[:, 1:PJ], dst_run[:, 0:PJ - 1], ALU.is_equal))
                to_mask(mask_f)
                nc.vector.tensor_copy(mask_b[:, 0:PJ - 1], mask_f[:, 1:PJ])
                link(nc.vector.memset(mask_b[:, PJ - 1:PJ], 0.0))
                link(nc.vector.memset(chain_m[:, :, :], 0.0))
                nc.vector.tensor_tensor(chain_m[:, 0, :], first, last_, ALU.is_equal)
                link(nc.vector.tensor_tensor(chain_m[:, 1, 1:P], first[:, 1:P], last_[:, 0:P - 1], ALU.is_equal))
                nc.vector.tensor_tensor(chain_m[:, 2, 1:P], chain_m[:, 0, 1:P], chain_m[:, 1, 1:P], ALU.mult)
                link(nc.vector.tensor_tensor(chain_m[:, 3, 0:P - 1], chain_m[:, 0, 0:P - 1], chain_m[:, 1, 1:P], ALU.mult))
                to_mask(chain_m[:, 1:4, :])

                def scan_heads(dst, src, mask, back, initial):
                    for h in range(HEADS):
                        d, s, m = dst[:, :, h], src[:, :, h], mask
                        if back:
                            d, s, m = d[:, ::-1], s[:, ::-1], m[:, ::-1]
                        last = nc.vector.tensor_tensor_scan(d, m, s, -BIG if initial is None else initial[:, h:h + 1], ALU.add, ALU.max)
                    link(last)

                for n, (dst, src, mask) in enumerate(((m_run, s_run, mask_f), (b_run, m_run, mask_b))):
                    scan_heads(dst, src, mask, n == 1, None)
                    edge = PJ - 1 if n == 0 else 0
                    nc.vector.tensor_copy(carry[:, 2 * n, :], dst[:, edge, :]).then_inc(phase, 1)
                    dve.wait_ge(pe_small, 2 * n + 2)
                    link(nc.vector.tensor_copy(tails[:, 2 * n, :], banks[0:HEADS, 7, 0:P]))
                    run, tl, cm = chain_m[:, 2 + n, :], tails[:, 2 * n, :], tails[:, 2 * n + 1, :]
                    if n == 0:
                        link(nc.vector.tensor_tensor_scan(cm, run, tl, -BIG, ALU.add, ALU.max))
                        nc.vector.memset(tl[:, 0:1], -BIG)
                        link(nc.vector.tensor_tensor(tl[:, 1:P], cm[:, 0:P - 1], chain_m[:, 1, 1:P], ALU.add))
                    else:
                        link(nc.vector.tensor_tensor_scan(cm[:, ::-1], run[:, ::-1], tl[:, ::-1], -BIG, ALU.add, ALU.max))
                        nc.vector.memset(tl[:, P - 1:P], -BIG)
                        link(nc.vector.tensor_tensor(tl[:, 0:P - 1], cm[:, 1:P], chain_m[:, 1, 1:P], ALU.add))
                    nc.vector.tensor_copy(cm, tl).then_inc(phase, 1)
                    dve.wait_ge(pe_small, 2 * n + 3)
                    link(nc.vector.tensor_copy(carry[:, 2 * n + 1, :], banks[:, 7, P:P + HEADS]))
                    scan_heads(dst, src, mask, n == 1, carry[:, 2 * n + 1, :])
                nc.vector.tensor_tensor(s_run, s_run, b_run, ALU.subtract).then_inc(phase, 1)
                dve.wait_ge(phase, PHASE["shifted"])

                def prepare(q, g, k, i):
                    dve.wait_ge(grp_done, g + (NG * hop_no(q) + 1))
                    make_onehot(q, g, k)
                    if q == PASS_VALUE:
                        nc.vector.tensor_copy(xcol[:, k, :, HEADS + 1:XW], ew[:, bass.ds(g * TG, TG)].unsqueeze(2))
                        nc.vector.tensor_copy(xcol[:, k, :, 0:HEADS], expo[:, bass.ds(g * TG, TG), :])
                        for half in range(2):
                            gathered(dve, k, half, i, 1)
                            v = row_slot[:, k, half * 4:half * 4 + 4, :].rearrange("p t (h d) -> p t h d", h=HEADS)
                            e = expo[:, bass.ds(g * TG + half * 4, 4), :]
                            nc.vector.tensor_tensor(v, v, e.unsqueeze(3).to_broadcast([P, 4, HEADS, HD]), ALU.mult).then_inc(msg_ready, 1)
                    if q == PASS_GCN1:
                        dve.wait_ge(hist_done, g + 1)
                        nc.vector.tensor_tensor(oh_hi[:, k, :, :], iota_f[:, 0:32].unsqueeze(1).to_broadcast([P, TG, 32]),
                                                src_hi[:, bass.ds(g * TG, TG)].unsqueeze(2).to_broadcast([P, TG, 32]), ALU.is_equal)
                        nc.vector.tensor_tensor(oh_lo[:, k, :, :], iota_f[:, :].unsqueeze(1).to_broadcast([P, TG, P]),
                                                src_lo[:, bass.ds(g * TG, TG)].unsqueeze(2).to_broadcast([P, TG, P]), ALU.is_equal
                                                ).then_inc(hist_oh, 1)

                def add_sums(q, g, k):
                    h = hop_no(q)
                    first = dve.value_load(base_i[0:1, bass.ds(g, 1)], min_val=0, max_val=NA - P)
                    dve.wait_ge(grp_done, g + (NG * h + 3))
                    dve.wait_ge(evac_done, g + (NG * h + 2))
                    win = acc[:, :, bass.ds(first, P)]
                    if q == PASS_VALUE:
                        dw = den[:, bass.ds(first, P)]
                        nc.vector.tensor_tensor(dw, dw, banks[0:XW, 3 * k + 2, 0:P], ALU.add)
                    nc.vector.tensor_tensor(win, win, banks[:, 3 * k:3 * k + 2, 0:P], ALU.add).then_inc(evac_done, 1)

                def rows_step(q, b, slot=None):
                    def per_node(j):
                        return node[:, j, bass.ds(b, 1)]

                    done = blocks_before(q)
                    if slot is None:
                        dve.wait_ge(pe_a, b + (done + 2))
                        ps = banks[:, B_ROWS, 0:D]
                    else:
                        dve.wait_ge(hop_done, b + (blocks_before(q, COUNTED) + 1))
                        ps = banks[:, slot, 0:D]
                    x_b, r_b, h_b = row(x_rows, b), row(r_rows, b), row(h_rows, b)
                    if q == PASS_GCN1:
                        dve.wait_ge(tab_ready, b + (done + 1))
                    if q == PASS_VALUE:
                        link(V.tensor_copy(blk_sc[:, 0:XW], banks[:, B_ROWS, D:D + XW]))
                        V.tensor_scalar(blk_sc[:, 10:11], blk_sc[:, 9:10], 1.0, None, ALU.add)
                        V.tensor_scalar(blk_sc[:, 8:9], blk_sc[:, 8:9], 1.0, None, ALU.max)
                        link(V.tensor_scalar(blk_sc[:, 0:HEADS], blk_sc[:, 0:HEADS], 1e-30, None, ALU.max))
                        V.tensor_scalar(blk_sc[:, 11:12], blk_sc[:, 10:11], 0.0, None, ALU.is_gt)
                        V.tensor_scalar(blk_sc[:, 16:17], blk_sc[:, 10:11], 1e-12, None, ALU.max).then_inc(deg_done, 1)
                        V.reciprocal(per_node(RDEG), blk_sc[:, 8:9])
                        link(V.reciprocal(blk_sc[:, 0:HEADS], blk_sc[:, 0:HEADS]))
                        V.tensor_tensor(rows[:, :].rearrange("p (h d) -> p h d", h=HEADS), ps.rearrange("p (h d) -> p h d", h=HEADS),
                                        blk_sc[:, 0:HEADS].unsqueeze(2).to_broadcast([P, HEADS, HD]), ALU.mult).then_inc(rows_done, 1)
                        dve.wait_ge(dstd_done, b + 1)
                        link(V.reciprocal(blk_sc[:, 12:13], dstd[:, :]))
                        link(V.tensor_tensor(per_node(DINV), blk_sc[:, 12:13], blk_sc[:, 11:12], ALU.mult))
                        link(V.tensor_scalar(per_node(HDINV), per_node(DINV), 0.5, None, ALU.mult))
                        link(V.tensor_tensor(per_node(HD2), per_node(HDINV), per_node(DINV), ALU.mult))
                        link(V.tensor_scalar(per_node(HD2P), per_node(HD2), 0.5, None, ALU.add))
                    elif q == PASS_GCN1:
                        V.scalar_tensor_tensor(rows[:, :], ps, per_node(HDINV), h_b, ALU.mult, ALU.add).then_inc(x_done, 1)
                        dve.wait_ge(x_done, b + (done + 1))
                        V.scalar_tensor_tensor(h_b, rows[:, :], per_node(HD2), r_b, ALU.mult, ALU.add).then_inc(blk_done, 1)
                    elif q == PASS_GCN2:
                        link(V.scalar_tensor_tensor(rows[:, :], ps, per_node(HDINV), h_b, ALU.mult, ALU.add))
                        V.tensor_scalar(rows[:, :], rows[:, :], 0.0, None, ALU.max).then_inc(rows_done, 1)
                    elif q == PASS_SAGE:
                        V.scalar_tensor_tensor(rows[:, :], ps, per_node(RDEG), x_b, ALU.mult, ALU.add).then_inc(rows_done_sage, 1)
                    elif q in (PASS_SG1, PASS_SG2):
                        V.scalar_tensor_tensor(x_b, ps, per_node(NORM), x_b, ALU.mult, ALU.add).then_inc(hop_dve, 1)
                    else:
                        V.scalar_tensor_tensor(rows[:, :], ps, per_node(NORM), x_b, ALU.mult, ALU.add).then_inc(rows_done, 1)
                        dve.wait_ge(rows_done, b + (blocks_before(q, TURNED) + 1))
                        dve.sem_inc(hop_dve, 1)

                def bias_step(q, b):
                    x_b = row(x_rows, b)
                    if q == PASS_VALUE:
                        link(V.tensor_tensor(pre_b[:, :], x_b, bias[:, 0, :], ALU.add))
                    elif q == PASS_GCN2:
                        link(V.tensor_tensor(pre_b[:, :], x_b, bias[:, 1, :], ALU.add))
                    elif q == PASS_SAGE:
                        dve.wait_ge(rows_done_sage, b + 1)
                        link(V.tensor_tensor(pre_b[:, :], rows[:, :], bias[:, 2, :], ALU.add))

                def norm_step(q, b):
                    if q not in DENSE:
                        return

                    def per_node(j):
                        return node[:, j, bass.ds(b, 1)]

                    done, dense = blocks_before(q, SUMMED), blocks_before(q, DENSE)
                    dve.wait_ge(pe_c, b + (dense + 1))
                    ps = banks[:, B_ROWS, 0:D]
                    x_b, r_b, h_b = row(x_rows, b), row(r_rows, b), row(h_rows, b)
                    if q == PASS_SG3:
                        link(V.tensor_tensor(ysum[:, :], ps, bias[:, 3, :], ALU.add))
                        link(V.scalar_tensor_tensor(ysum[:, :], ysum[:, :], 0.0, r_b, ALU.max, ALU.add))
                    else:
                        link(V.tensor_tensor(ysum[:, :], ps, pre_b[:, :], ALU.add))
                    link(V.bn_stats(stats[:, :], ysum[:, :]))
                    dve.sem_inc(dve_step, 1)
                    V.bn_aggr(mv[:, :], stats[:, :]).then_inc(var_done, 1)
                    dve.wait_ge(std_done, b + (dense + 1))
                    link(V.reciprocal(rstd[:, :], std[:, :]))
                    V.tensor_scalar(x_b, ysum[:, :], mv[:, 0:1], rstd[:, :], ALU.subtract, ALU.mult).then_inc(x_done, 1)
                    dve.wait_ge(x_done, b + (done + 1))
                    if q == PASS_VALUE:
                        V.tensor_scalar(h_b, x_b, per_node(HD2P), None, ALU.mult)
                        V.tensor_scalar(r_b, x_b, 0.5, None, ALU.mult).then_inc(blk_done, 1)
                    elif q == PASS_SAGE:
                        V.tensor_copy(r_b, x_b).then_inc(blk_done, 1)
                    else:
                        dve.sem_inc(blk_done, 1)

                def strip_onehots(q, i, k):
                    n = BUILDS.index(q) * NG
                    s = i * 2 + (n + k)
                    tile0 = dve.value_load(tile0_i[0:1, bass.ds(s, 1)], min_val=0, max_val=NT - ST)
                    dve.wait_ge(strip_done, s + 1)
                    V.scalar_tensor_tensor(key_tile[:, k, 0:ST], dstrip[:, bass.ds(tile0, ST)], iota_f[:, bass.ds(s, 1)],
                                           key1[:, bass.ds(tile0, ST)], ALU.is_equal, ALU.mult).then_inc(key_done, 1)
                    for t in range(ST):
                        V.tensor_scalar(oh_src[:, t, :], iota_f[:, :], src_lo[:, bass.ds(tile0 + t, 1)], None, ALU.is_equal)
                    dve.wait_ge(key_done, s + 1)
                    for t in range(ST):
                        last = V.tensor_scalar(oh_key[:, t, :], key_iota, key_tile[:, k, t:t + 1], None, ALU.is_equal)
                    last.then_inc(oh_strip, 1)

                for q in SUMMED:
                    h = hop_no(q)
                    if q != PASS_VALUE:
                        dve.wait_ge(staged, blocks_before(q))
                    if q == PASS_VALUE:
                        V.memset(den, 0.0)
                    link(V.memset(acc[:, :, :], 0.0))
                    if q == PASS_VALUE:
                        dve.wait_ge(moved, 80)
                    if q == PASS_GCN1:
                        dve.wait_ge(edges_in, 32)
                        lo, hi = edge_t[:, 1, :], edge_t[:, 0, :]
                        V.tensor_scalar(lo, edge_i[:, 1, :], SW - 1, None, ALU.bitwise_and)
                        link(V.tensor_scalar(hi, edge_i[:, 1, :], 5, None, ALU.arith_shift_right))
                        V.tensor_copy(dstrip, hi)
                        link(V.tensor_copy(key1, lo))
                        link(V.scalar_tensor_tensor(key1, src_hi[:, :], float(SW), key1, ALU.mult, ALU.add))
                        link(V.tensor_scalar(key1, key1, 1.0, None, ALU.add))
                        link(V.tensor_scalar(key_iota[:, 0:P], iota_f[:, :], 1.0, None, ALU.add))
                        for c in range(1, -(-SC // P)):
                            w = min(P, SC - c * P)
                            link(V.tensor_scalar(key_iota[:, c * P:c * P + w], iota_f[:, 0:w], float(c * P + 1), None, ALU.add))
                    prepare(q, 0, 0, 0)
                    with dve.Fori(0, LAG) as i:
                        prepare(q, i * 2 + 1, 1, i)
                        if q in BUILDS:
                            strip_onehots(q, i, 0)
                        add_sums(q, i * 2, 0)
                        prepare(q, i * 2 + 2, 0, i + 1)
                        if q in BUILDS:
                            strip_onehots(q, i, 1)
                        add_sums(q, i * 2 + 1, 1)

                    def both(i, last):
                        b = i - LAG
                        prepare(q, i * 2 + 1, 1, i)
                        if q in BUILDS:
                            strip_onehots(q, i, 0)
                        add_sums(q, i * 2, 0)
                        rows_step(q, b)
                        bias_step(q, b)
                        if not last:
                            prepare(q, i * 2 + 2, 0, i + 1)
                        if q in BUILDS:
                            strip_onehots(q, i, 1)
                        add_sums(q, i * 2 + 1, 1)
                        norm_step(q, b)

                    start = chain_total(chain)
                    size = LINKS[q]
                    with dve.Fori(LAG, NG // 2 - 1) as i:
                        if size:
                            chain.enter(i * size + (start - LAG * size))
                        both(i, False)
                        if size:
                            n = chain.leave()
                            assert n == size, (q, n)
                    chain.enter(start + (LOOPED - 1) * size)
                    both(NG // 2 - 1, True)
                    for b in range(LOOPED, NB):
                        rows_step(q, b)
                        bias_step(q, b)
                        norm_step(q, b)
                    if q == PASS_GCN1:
                        dve.wait_ge(hist_done, NG + 3)
                        V.tensor_scalar(node[:, OUTDEG, :], banks[:, 2, 0:NB], 1.0, None, ALU.max).then_inc(norm_ready, 1)
                        dve.wait_ge(norm_root, 1)
                        link(V.reciprocal(node[:, NORM, :], node[:, NORM2, :]))
                        link(V.tensor_tensor(node[:, NORM2, :], node[:, NORM, :], node[:, NORM, :], ALU.mult))

                def rest_step(stage_no, b, whole, rest, to):
                    dve.wait_ge(hi_done, b + (stage_no * NB + 1))
                    V.tensor_tensor(rest, whole, row(parts[to][0], b), ALU.subtract).then_inc(rest1, 1)

                def low_step(stage_no, b, rest, to):
                    dve.wait_ge(mid_done, b + (stage_no * NB + 1))
                    V.tensor_tensor(row(parts[to][2], b), rest, row(parts[to][1], b), ALU.subtract).then_inc(lo_done, 1)

                dve.wait_ge(u_ready, NB)
                rest_step(0, 0, row(h_rows, 0), row(h_rows, 0), 0)
                with dve.Fori(0, NB - 1) as b:
                    rest_step(0, b + 1, row(h_rows, b + 1), row(h_rows, b + 1), 0)
                    low_step(0, b, row(h_rows, b), 0)
                low_step(0, NB - 1, row(h_rows, NB - 1), 0)
                for n, q in enumerate(COUNTED):
                    if q != PASS_SG3:
                        def hop_rows(b, slot, i):
                            dve.wait_ge(hop_act, b + (NB * n + 3))
                            rows_step(q, b, slot)
                            rest_step(n + 1, b, tab_row[:, :], ysum[:, :], (n + 1) % 2)
                            low_step(n + 1, b, ysum[:, :], (n + 1) % 2)

                        odd_block_pairs(dve, NB * n, hop_rows)
                    else:
                        start = chain_total(chain)
                        size = LINKS[q]
                        with dve.Fori(0, NB // 2) as i:
                            for k in range(2):
                                chain.enter(i * (2 * size) + (start + k * size))
                                rows_step(q, i * 2 + k, (NB * n + k) % 2)
                                norm_step(q, i * 2 + k)
                                assert chain.leave() == size
                        chain.enter(start + (NB - 1) * size)
                        rows_step(q, NB - 1, (NB * n) % 2)
                        norm_step(q, NB - 1)

            choose_path(dve, windows_path, any_order_path)


def kernel(**inputs):
    import numpy as np
    import concourse.bacc as bacc
    from concourse.bass_utils import run_bass_kernel_spmd

    nc = bacc.Bacc("TRN2", target_bir_lowering=False, num_devices=1)
    x = np.asarray(inputs["x"])

    def padded(v, fill, rows):
        v = np.asarray(v)
        o = np.full((rows,) + v.shape[1:], fill, v.dtype)
        o[:v.shape[0]] = v
        return o

    def tiles(v):
        return v.reshape(NG, P, TG).transpose(1, 0, 2).reshape(P, NT)

    xp = padded(x, 0, NP)
    src = padded(inputs["src"], N, EP)
    dst = padded(inputs["dst"], N, EP)
    run = dst.reshape(P, PJ)
    ef = padded(inputs["edge_attr_64"], 0, EP)
    arrays = {
        "x": xp, "x_t": xp.T,
        "src_t": tiles(src), "dst_t": tiles(dst), "dst_run": run,
        "dst_rows": np.ascontiguousarray(tiles(dst).T).reshape(NG, EG), "dst_nat": dst.reshape(NT, P), "src_e": src.reshape(NT, P).T, "dst_e": dst.reshape(NT, P).T, "first": dst[::P], "last": dst[P - 1::P],
        "base": dst[::EG], "ends": np.stack([run[:, 0], run[:, -1]]),
        "ew_t": tiles(padded(inputs["edge_weight"], 0, EP)),
        "ew1_t": tiles(padded(np.asarray(inputs["edge_weight1"])[:, 0], 0, EP)),
        "ef_t": ef.reshape(NG, P, TG, FE).transpose(3, 0, 2, 1).reshape(FE, EP),
        "Wq": inputs["L0_gnn_Wq"], "Wk": inputs["L0_gnn_Wk"], "Wv": inputs["L0_gnn_Wv"], "Wo": inputs["L0_gnn_Wo"],
        "W1": inputs["L0_gnn_W1"], "b1_t": np.asarray(inputs["L0_gnn_b1"]).reshape(FC, P).T,
        "W2": inputs["L0_gnn_W2"], "b2": inputs["L0_gnn_b2"], "bo": inputs["L0_gnn_bo"],
        "L1_Wt": np.asarray(inputs["L1_gnn_W"]).T, "L1_b": inputs["L1_gnn_b"],
        "L2_Wt": np.asarray(inputs["L2_gnn_W"]).T, "L2_b": inputs["L2_gnn_b"],
        "L3_W": inputs["L3_gnn_W"], "L3_b": inputs["L3_gnn_b"],
    }
    arrays = {k: np.ascontiguousarray(v) for k, v in arrays.items()}
    a = {k: nc.dram_tensor("in_" + k, v.shape, mybir.dt.from_np(v.dtype), kind="ExternalInput").ap()
         for k, v in arrays.items()}
    out = nc.dram_tensor("out", [N, D], F32, kind="ExternalOutput").ap()
    gnn_program(nc, a, out)
    r = run_bass_kernel_spmd(nc, [{"in_" + k: v for k, v in arrays.items()}], core_ids=[0])
    return r.results[0]["out"]
```
